# Optimizing a Trainium2 kernel written in Bass

```python
import numpy as np
import jax
import jax.numpy as jnp

def _softmax(x, axis=-1):
    return jax.nn.softmax(x, axis=axis)

def _gelu(x):
    return jax.nn.gelu(x, approximate=True)

def _silu(x):
    return jax.nn.silu(x)

def _sigmoid(x):
    return jax.nn.sigmoid(x)

def _layernorm(x, axis=-1, eps=1e-05):
    m = jnp.mean(x, axis=axis, keepdims=True)
    v = jnp.var(x, axis=axis, keepdims=True)
    return (x - m) / jnp.sqrt(v + eps)

def _scatter_add(tgt, idx, src, axis=0):
    return tgt.at[idx].add(src)

def _segment_sum(src, seg, n):
    return jax.ops.segment_sum(src, seg, n)
kernel_name = 'mk_adj_ffn_d4_adj_r2_797187'

def setup_inputs(seed: int=0):
    np.random.seed(seed)
    _w = jnp.asarray

    def _rec_inputs():
        import jax
        import jax.numpy as jnp
        _gk = jax.random.key(seed)
        x = 7.22e-05 + 1 * jax.random.normal(jax.random.fold_in(_gk, 1), (32, 256, 128), jnp.float32)
        _w = (1.0 + jnp.arange(256, dtype=jnp.float32)) ** (-0.5)
        _w = _w / _w.mean()
        _pij = jnp.clip(0.03125 * _w[:, None] * _w[None, :], 0.0, 1.0)
        _a = jax.random.uniform(jax.random.fold_in(_gk, 2), (32, 256, 256)) < _pij
        _a = jnp.logical_or(_a, jnp.swapaxes(_a, -1, -2))
        _a = jnp.logical_or(_a, jnp.eye(256, dtype=bool))
        _af = _a.astype(jnp.float32)
        adj = _af
        return (x, adj)
    x, adj = _rec_inputs()

    def _L0_gnn_setup():
        import jax, jax.numpy as jnp
        import numpy as np
        from jax import lax
        DIM = 128
        EPS = 1e-05

        def _bn(h, g, b, m, v):
            scale = g / jnp.sqrt(v + EPS)
            return h * scale[None, :, None] + (b - m * scale)[None, :, None]

        def _conv1d(h, w, pad):
            return lax.conv_general_dilated(h, w, window_strides=(1,), padding=[(pad, pad)], dimension_numbers=('NCH', 'OIH', 'NCH'))
        key = jax.random.key(seed)
        ks = jax.random.split(key, 16)
        bs, n, d = (16, 1024, DIM)
        s = 0.05
        return {'x': jax.random.normal(ks[0], (bs, n, d), jnp.float32), 'mask': jnp.ones((bs, n, n), jnp.float32), 'w_se': jax.random.normal(ks[1], (3, d), jnp.float32) * s, 'b_se': jnp.zeros((3,), jnp.float32), 'conv1_w': jax.random.normal(ks[2], (d, d, 1), jnp.float32) * s, 'bn1_g': jnp.ones((d,), jnp.float32), 'bn1_b': jnp.zeros((d,), jnp.float32), 'bn1_m': jnp.zeros((d,), jnp.float32), 'bn1_v': jnp.ones((d,), jnp.float32), 'conv2_w': jax.random.normal(ks[3], (d, d, 17), jnp.float32) * s, 'bn2_g': jnp.ones((d,), jnp.float32), 'bn2_b': jnp.zeros((d,), jnp.float32), 'bn2_m': jnp.zeros((d,), jnp.float32), 'bn2_v': jnp.ones((d,), jnp.float32), 'w_msg': jax.random.normal(ks[4], (d, d), jnp.float32) * s, 'b_msg': jnp.zeros((d,), jnp.float32), 'w_ih': jax.random.normal(ks[5], (3 * d, 2 * d), jnp.float32) * s, 'b_ih': jnp.zeros((3 * d,), jnp.float32), 'w_hh': jax.random.normal(ks[6], (3 * d, d), jnp.float32) * s, 'b_hh': jnp.zeros((3 * d,), jnp.float32)}
    _L0_gnn_all = _L0_gnn_setup()
    _L0_gnn_in = {k: v for k, v in _L0_gnn_all.items() if k in ('w_se', 'b_se', 'conv1_w', 'bn1_g', 'bn1_b', 'bn1_m', 'bn1_v', 'conv2_w', 'bn2_g', 'bn2_b', 'bn2_m', 'bn2_v', 'w_msg', 'b_msg', 'w_ih', 'b_ih', 'w_hh', 'b_hh')}
    del _L0_gnn_all

    def _L0_ffn_setup():
        import jax, jax.numpy as jnp
        import numpy as np
        D_MODEL = 128
        N_EXPERTS = 16
        HIDDEN = 256
        SCALE = 0.02
        key = jax.random.key(seed)
        ks = jax.random.split(key, 5)
        x = jax.random.normal(ks[0], (4, 4096, D_MODEL), dtype=jnp.float32)
        gate_w = jax.random.normal(ks[1], (D_MODEL, N_EXPERTS), dtype=jnp.float32) * SCALE
        gate_b = jnp.zeros((N_EXPERTS,), dtype=jnp.float32)
        w1 = jax.random.normal(ks[2], (N_EXPERTS, D_MODEL, HIDDEN), dtype=jnp.float32) * SCALE
        w2 = jax.random.normal(ks[3], (N_EXPERTS, D_MODEL, HIDDEN), dtype=jnp.float32) * SCALE
        w3 = jax.random.normal(ks[4], (N_EXPERTS, HIDDEN, D_MODEL), dtype=jnp.float32) * SCALE
        return {'x': x, 'gate_w': gate_w, 'gate_b': gate_b, 'w1': w1, 'w2': w2, 'w3': w3}
    _L0_ffn_all = _L0_ffn_setup()
    _L0_ffn_in = {k: v for k, v in _L0_ffn_all.items() if k in ('gate_w', 'gate_b', 'w1', 'w2', 'w3')}
    del _L0_ffn_all

    def _L1_gnn_setup():
        import jax, jax.numpy as jnp
        import numpy as np
        B, N, D = (4, 2048, 128)
        DENSITY = 0.02
        key = jax.random.key(seed)
        kx, ka1, ka2, kwt, kbt, kwh, kth = jax.random.split(key, 7)
        x = jax.random.normal(kx, (B, N, D), dtype=jnp.float32)
        mask = jax.random.uniform(ka1, (B, N, N)) < DENSITY
        vals = jax.random.uniform(ka2, (B, N, N), dtype=jnp.float32)
        adj = jnp.where(mask, vals, 0.0).astype(jnp.float32)
        s = 0.02
        W_t = s * jax.random.normal(kwt, (D, D), dtype=jnp.float32)
        b_t = s * jax.random.normal(kbt, (D,), dtype=jnp.float32)
        W_h = s * jax.random.normal(kwh, (D, D), dtype=jnp.float32)
        theta = s * jax.random.normal(kth, (D, D), dtype=jnp.float32)
        return {'x': x, 'adj': adj, 'W_t': W_t, 'b_t': b_t, 'W_h': W_h, 'theta': theta}
    _L1_gnn_all = _L1_gnn_setup()
    _L1_gnn_in = {k: v for k, v in _L1_gnn_all.items() if k in ('W_t', 'b_t', 'W_h', 'theta')}
    del _L1_gnn_all

    def _L1_ffn_setup():
        import math
        import jax, jax.numpy as jnp
        import numpy as np
        CAPACITY_FACTOR = 1.25
        key = jax.random.key(seed)
        ks = jax.random.split(key, 5)
        B, L, D, F, E = (8, 4096, 128, 512, 8)
        h = jax.random.normal(ks[0], (B, L, D), dtype=jnp.float32)
        gate_w = jax.random.normal(ks[1], (D, E), dtype=jnp.float32) * 0.02
        gate_b = jnp.zeros((E,), dtype=jnp.float32)
        w1 = jax.random.normal(ks[2], (E, D, F), dtype=jnp.float32) * (1.0 / math.sqrt(D))
        b1 = jnp.zeros((E, F), dtype=jnp.float32)
        w2 = jax.random.normal(ks[3], (E, F, D), dtype=jnp.float32) * (1.0 / math.sqrt(F))
        b2 = jnp.zeros((E, D), dtype=jnp.float32)
        return {'h': h, 'gate_w': gate_w, 'gate_b': gate_b, 'w1': w1, 'b1': b1, 'w2': w2, 'b2': b2}
    _L1_ffn_all = _L1_ffn_setup()
    _L1_ffn_in = {k: v for k, v in _L1_ffn_all.items() if k in ('gate_w', 'gate_b', 'w1', 'b1', 'w2', 'b2')}
    del _L1_ffn_all

    def _L2_gnn_setup():
        import jax, jax.numpy as jnp
        import numpy as np
        B, K, H = (32, 512, 128)
        LN_EPS = 1e-05

        def layer_norm(x, gamma, beta):
            mu = jnp.mean(x, axis=-1, keepdims=True)
            var = jnp.mean(jnp.square(x - mu), axis=-1, keepdims=True)
            return (x - mu) * jax.lax.rsqrt(var + LN_EPS) * gamma + beta
        key = jax.random.key(seed)
        k1, k2, k3, k4 = jax.random.split(key, 4)
        x = jax.random.normal(k1, (B, K, H), dtype=jnp.float32)
        adj = jax.random.uniform(k2, (B, K, K), dtype=jnp.float32)
        s = 1.0 / np.sqrt(H)
        W_rel = jax.random.normal(k3, (H, H), dtype=jnp.float32) * s
        b_rel = jnp.zeros((H,), dtype=jnp.float32)
        W_root = jax.random.normal(k4, (H, H), dtype=jnp.float32) * s
        ln_gamma = jnp.ones((H,), dtype=jnp.float32)
        ln_beta = jnp.zeros((H,), dtype=jnp.float32)
        return {'x': x, 'adj': adj, 'W_rel': W_rel, 'b_rel': b_rel, 'W_root': W_root, 'ln_gamma': ln_gamma, 'ln_beta': ln_beta}
    _L2_gnn_all = _L2_gnn_setup()
    _L2_gnn_in = {k: v for k, v in _L2_gnn_all.items() if k in ('W_rel', 'b_rel', 'W_root', 'ln_gamma', 'ln_beta')}
    del _L2_gnn_all

    def _L2_ffn_setup():
        import jax, jax.numpy as jnp
        import numpy as np
        H, P, G, NS, K = (8, 64, 64, 64, 3)
        D_INNER = H * P
        CONV_DIM = D_INNER + 2 * NS
        D_IN_PROJ = 2 * D_INNER + 2 * NS + 2 * H

        def _hydra(u, in_w, conv_w, conv_b, dt_bias, A_log, Dp, fcD_w, norm_w, out_w):
            Bt, L, _ = u.shape
            zxbcdt = u @ in_w.T
            z = zxbcdt[..., :D_INNER]
            xBC = zxbcdt[..., D_INNER:D_INNER + CONV_DIM]
            dt = zxbcdt[..., -2 * H:]
            dt = jnp.concatenate([dt[..., :H], jnp.flip(dt[..., H:], axis=1)], axis=0)
            dt = jax.nn.softplus(dt + dt_bias)
            xp = jnp.pad(xBC, ((0, 0), (K - 1, 0), (0, 0)))
            xBC = sum((xp[:, k:k + L, :] * conv_w[:, k] for k in range(K))) + conv_b
            xBC = jax.nn.silu(xBC)
            x = xBC[..., :D_INNER]
            Bm = xBC[..., D_INNER:D_INNER + NS]
            Cm = xBC[..., D_INNER + NS:]
            x_og = x
            x2 = jnp.concatenate([x, jnp.flip(x, 1)], 0).reshape(2 * Bt, L, H, P)
            B2 = jnp.concatenate([Bm, jnp.flip(Bm, 1)], 0)
            C2 = jnp.concatenate([Cm, jnp.flip(Cm, 1)], 0)
            dA = jnp.exp(dt * -jnp.exp(A_log))
            dBx = jnp.einsum('blh,bln,blhp->blhpn', dt, B2, x2)

            def step(h, inp):
                dA_t, dBx_t, C_t = inp
                h = h * dA_t[:, :, None, None] + dBx_t
                return (h, jnp.einsum('bhpn,bn->bhp', h, C_t))
            h0 = jnp.zeros((2 * Bt, H, P, NS), u.dtype)
            _, ys = jax.lax.scan(step, h0, (dA.transpose(1, 0, 2), dBx.transpose(1, 0, 2, 3, 4), C2.transpose(1, 0, 2)))
            y = ys.transpose(1, 0, 2, 3).reshape(2 * Bt, L, D_INNER)
            y_fw, y_bw = (y[:Bt], jnp.flip(y[Bt:], 1))
            y = jnp.pad(y_fw[:, :-1], ((0, 0), (1, 0), (0, 0))) + jnp.pad(y_bw[:, 1:], ((0, 0), (0, 1), (0, 0)))
            y = y + x_og * jnp.repeat(x_og @ fcD_w.T + Dp, P, axis=-1)
            yg = y * jax.nn.silu(z)
            yg = yg * jax.lax.rsqrt(jnp.mean(jnp.square(yg), -1, keepdims=True) + 1e-05) * norm_w
            return yg @ out_w.T
        key = jax.random.key(seed)
        ks = jax.random.split(key, 10)
        dim, Bsz, N = (128, 4, 4096)
        s = 0.02
        return {'x': jax.random.normal(ks[0], (Bsz, N, dim), jnp.float32), 'W_fx': jax.random.normal(ks[1], (D_INNER, dim), jnp.float32) * s, 'b_fx': jnp.zeros((D_INNER,), jnp.float32), 'W_x': jax.random.normal(ks[2], (D_INNER, dim), jnp.float32) * s, 'b_x': jnp.zeros((D_INNER,), jnp.float32), 'W_slice': jax.random.normal(ks[3], (G, P), jnp.float32) * s, 'b_slice': jnp.zeros((G,), jnp.float32), 'temperature': jnp.full((1, H, 1, 1), 0.5, jnp.float32), 'hy_in_w': jax.random.normal(ks[4], (D_IN_PROJ, D_INNER), jnp.float32) * s, 'hy_conv_w': jax.random.normal(ks[5], (CONV_DIM, K), jnp.float32) * s, 'hy_conv_b': jnp.zeros((CONV_DIM,), jnp.float32), 'hy_dt_bias': jnp.log(jnp.expm1(jnp.full((H,), 0.01, jnp.float32))), 'hy_A_log': jnp.log(jnp.linspace(1.0, 16.0, H)).astype(jnp.float32), 'hy_D': jnp.ones((H,), jnp.float32), 'hy_fcD_w': jax.random.normal(ks[6], (H, D_INNER), jnp.float32) * s, 'hy_norm_w': jnp.ones((D_INNER,), jnp.float32), 'hy_out_w': jax.random.normal(ks[7], (D_INNER, D_INNER), jnp.float32) * s, 'out_w': jax.random.normal(ks[8], (dim, D_INNER), jnp.float32) * s, 'out_b': jnp.zeros((dim,), jnp.float32)}
    _L2_ffn_all = _L2_ffn_setup()
    _L2_ffn_in = {k: v for k, v in _L2_ffn_all.items() if k in ('W_fx', 'b_fx', 'W_x', 'b_x', 'W_slice', 'b_slice', 'temperature', 'hy_in_w', 'hy_conv_w', 'hy_conv_b', 'hy_dt_bias', 'hy_A_log', 'hy_D', 'hy_fcD_w', 'hy_norm_w', 'hy_out_w', 'out_w', 'out_b')}
    del _L2_ffn_all

    def _L3_gnn_setup():
        import math
        import jax, jax.numpy as jnp
        import numpy as np
        HIDDEN = 128
        HEADS = 8
        HEAD_DIM = HIDDEN // HEADS
        key = jax.random.key(seed)
        ks = jax.random.split(key, 8)
        b, n = (2, 2048)
        node_state = jax.random.normal(ks[0], (b, n, HIDDEN), dtype=jnp.float32)
        adjacency = jax.random.uniform(ks[1], (b, n, n), dtype=jnp.float32)
        s = 1.0 / math.sqrt(HIDDEN)
        Wq = jax.random.uniform(ks[2], (HIDDEN, HIDDEN), jnp.float32, -s, s)
        Wk = jax.random.uniform(ks[3], (HIDDEN, HIDDEN), jnp.float32, -s, s)
        Wv = jax.random.uniform(ks[4], (HIDDEN, HIDDEN), jnp.float32, -s, s)
        Wo = jax.random.uniform(ks[5], (HIDDEN, HIDDEN), jnp.float32, -s, s)
        bo = jax.random.uniform(ks[6], (HIDDEN,), jnp.float32, -s, s)
        return {'node_state': node_state, 'adjacency': adjacency, 'Wq': Wq, 'Wk': Wk, 'Wv': Wv, 'Wo': Wo, 'bo': bo}
    _L3_gnn_all = _L3_gnn_setup()
    _L3_gnn_in = {k: v for k, v in _L3_gnn_all.items() if k in ('Wq', 'Wk', 'Wv', 'Wo', 'bo')}
    del _L3_gnn_all

    def _L3_ffn_setup():
        import jax, jax.numpy as jnp
        import numpy as np
        B, T, C = (64, 192, 128)
        NH, NKV = (4, 2)
        HD = C // NH
        NREP = NH // NKV
        NE, TOPK = (8, 2)
        HID = int(8 / 3 * C)
        EPS_RMS = 1e-06

        def _rope_tables(t_len):
            inv_freq = 1.0 / 10000.0 ** (np.arange(0, HD, 2, dtype=np.float32) / HD)
            t = np.arange(t_len, dtype=np.float32)
            freqs = np.outer(t, inv_freq)
            emb = np.concatenate([freqs, freqs], axis=-1)
            return (jnp.asarray(np.cos(emb)), jnp.asarray(np.sin(emb)))

        def _rotate_half(x):
            h = x.shape[-1] // 2
            return jnp.concatenate([-x[..., h:], x[..., :h]], axis=-1)

        def _rmsnorm(v, w):
            return v * jax.lax.rsqrt(jnp.mean(v * v, axis=-1, keepdims=True) + EPS_RMS) * w
        key = jax.random.key(seed)
        ks = jax.random.split(key, 10)
        s = lambda k, shape: jax.random.normal(k, shape, jnp.float32) * 0.02
        return {'x': jax.random.normal(ks[0], (B, T, C), jnp.float32), 'ln1_w': jnp.ones((C,), jnp.float32), 'ln2_w': jnp.ones((C,), jnp.float32), 'wq': s(ks[1], (NH * HD, C)), 'wk': s(ks[2], (NKV * HD, C)), 'wv': s(ks[3], (NKV * HD, C)), 'wo': s(ks[4], (C, C)), 'router_w': s(ks[5], (NE, C)), 'w1': s(ks[6], (NE, HID, C)), 'w2': s(ks[7], (NE, C, HID)), 'w3': s(ks[8], (NE, HID, C))}
    _L3_ffn_all = _L3_ffn_setup()
    _L3_ffn_in = {k: v for k, v in _L3_ffn_all.items() if k in ('ln1_w', 'ln2_w', 'wq', 'wk', 'wv', 'wo', 'router_w', 'w1', 'w2', 'w3')}
    del _L3_ffn_all
    return {'x': x, 'adj': adj, 'L0_gnn_w_se': _L0_gnn_in['w_se'], 'L0_gnn_b_se': _L0_gnn_in['b_se'], 'L0_gnn_conv1_w': _L0_gnn_in['conv1_w'], 'L0_gnn_bn1_g': _L0_gnn_in['bn1_g'], 'L0_gnn_bn1_b': _L0_gnn_in['bn1_b'], 'L0_gnn_bn1_m': _L0_gnn_in['bn1_m'], 'L0_gnn_bn1_v': _L0_gnn_in['bn1_v'], 'L0_gnn_conv2_w': _L0_gnn_in['conv2_w'], 'L0_gnn_bn2_g': _L0_gnn_in['bn2_g'], 'L0_gnn_bn2_b': _L0_gnn_in['bn2_b'], 'L0_gnn_bn2_m': _L0_gnn_in['bn2_m'], 'L0_gnn_bn2_v': _L0_gnn_in['bn2_v'], 'L0_gnn_w_msg': _L0_gnn_in['w_msg'], 'L0_gnn_b_msg': _L0_gnn_in['b_msg'], 'L0_gnn_w_ih': _L0_gnn_in['w_ih'], 'L0_gnn_b_ih': _L0_gnn_in['b_ih'], 'L0_gnn_w_hh': _L0_gnn_in['w_hh'], 'L0_gnn_b_hh': _L0_gnn_in['b_hh'], 'L0_ffn_gate_w': _L0_ffn_in['gate_w'], 'L0_ffn_gate_b': _L0_ffn_in['gate_b'], 'L0_ffn_w1': _L0_ffn_in['w1'], 'L0_ffn_w2': _L0_ffn_in['w2'], 'L0_ffn_w3': _L0_ffn_in['w3'], 'L1_gnn_W_t': _L1_gnn_in['W_t'], 'L1_gnn_b_t': _L1_gnn_in['b_t'], 'L1_gnn_W_h': _L1_gnn_in['W_h'], 'L1_gnn_theta': _L1_gnn_in['theta'], 'L1_ffn_gate_w': _L1_ffn_in['gate_w'], 'L1_ffn_gate_b': _L1_ffn_in['gate_b'], 'L1_ffn_w1': _L1_ffn_in['w1'], 'L1_ffn_b1': _L1_ffn_in['b1'], 'L1_ffn_w2': _L1_ffn_in['w2'], 'L1_ffn_b2': _L1_ffn_in['b2'], 'L2_gnn_W_rel': _L2_gnn_in['W_rel'], 'L2_gnn_b_rel': _L2_gnn_in['b_rel'], 'L2_gnn_W_root': _L2_gnn_in['W_root'], 'L2_gnn_ln_gamma': _L2_gnn_in['ln_gamma'], 'L2_gnn_ln_beta': _L2_gnn_in['ln_beta'], 'L2_ffn_W_fx': _L2_ffn_in['W_fx'], 'L2_ffn_b_fx': _L2_ffn_in['b_fx'], 'L2_ffn_W_x': _L2_ffn_in['W_x'], 'L2_ffn_b_x': _L2_ffn_in['b_x'], 'L2_ffn_W_slice': _L2_ffn_in['W_slice'], 'L2_ffn_b_slice': _L2_ffn_in['b_slice'], 'L2_ffn_temperature': _L2_ffn_in['temperature'], 'L2_ffn_hy_in_w': _L2_ffn_in['hy_in_w'], 'L2_ffn_hy_conv_w': _L2_ffn_in['hy_conv_w'], 'L2_ffn_hy_conv_b': _L2_ffn_in['hy_conv_b'], 'L2_ffn_hy_dt_bias': _L2_ffn_in['hy_dt_bias'], 'L2_ffn_hy_A_log': _L2_ffn_in['hy_A_log'], 'L2_ffn_hy_D': _L2_ffn_in['hy_D'], 'L2_ffn_hy_fcD_w': _L2_ffn_in['hy_fcD_w'], 'L2_ffn_hy_norm_w': _L2_ffn_in['hy_norm_w'], 'L2_ffn_hy_out_w': _L2_ffn_in['hy_out_w'], 'L2_ffn_out_w': _L2_ffn_in['out_w'], 'L2_ffn_out_b': _L2_ffn_in['out_b'], 'L3_gnn_Wq': _L3_gnn_in['Wq'], 'L3_gnn_Wk': _L3_gnn_in['Wk'], 'L3_gnn_Wv': _L3_gnn_in['Wv'], 'L3_gnn_Wo': _L3_gnn_in['Wo'], 'L3_gnn_bo': _L3_gnn_in['bo'], 'L3_ffn_ln1_w': _L3_ffn_in['ln1_w'], 'L3_ffn_ln2_w': _L3_ffn_in['ln2_w'], 'L3_ffn_wq': _L3_ffn_in['wq'], 'L3_ffn_wk': _L3_ffn_in['wk'], 'L3_ffn_wv': _L3_ffn_in['wv'], 'L3_ffn_wo': _L3_ffn_in['wo'], 'L3_ffn_router_w': _L3_ffn_in['router_w'], 'L3_ffn_w1': _L3_ffn_in['w1'], 'L3_ffn_w2': _L3_ffn_in['w2'], 'L3_ffn_w3': _L3_ffn_in['w3']}

def reference(x, adj, L0_gnn_w_se, L0_gnn_b_se, L0_gnn_conv1_w, L0_gnn_bn1_g, L0_gnn_bn1_b, L0_gnn_bn1_m, L0_gnn_bn1_v, L0_gnn_conv2_w, L0_gnn_bn2_g, L0_gnn_bn2_b, L0_gnn_bn2_m, L0_gnn_bn2_v, L0_gnn_w_msg, L0_gnn_b_msg, L0_gnn_w_ih, L0_gnn_b_ih, L0_gnn_w_hh, L0_gnn_b_hh, L0_ffn_gate_w, L0_ffn_gate_b, L0_ffn_w1, L0_ffn_w2, L0_ffn_w3, L1_gnn_W_t, L1_gnn_b_t, L1_gnn_W_h, L1_gnn_theta, L1_ffn_gate_w, L1_ffn_gate_b, L1_ffn_w1, L1_ffn_b1, L1_ffn_w2, L1_ffn_b2, L2_gnn_W_rel, L2_gnn_b_rel, L2_gnn_W_root, L2_gnn_ln_gamma, L2_gnn_ln_beta, L2_ffn_W_fx, L2_ffn_b_fx, L2_ffn_W_x, L2_ffn_b_x, L2_ffn_W_slice, L2_ffn_b_slice, L2_ffn_temperature, L2_ffn_hy_in_w, L2_ffn_hy_conv_w, L2_ffn_hy_conv_b, L2_ffn_hy_dt_bias, L2_ffn_hy_A_log, L2_ffn_hy_D, L2_ffn_hy_fcD_w, L2_ffn_hy_norm_w, L2_ffn_hy_out_w, L2_ffn_out_w, L2_ffn_out_b, L3_gnn_Wq, L3_gnn_Wk, L3_gnn_Wv, L3_gnn_Wo, L3_gnn_bo, L3_ffn_ln1_w, L3_ffn_ln2_w, L3_ffn_wq, L3_ffn_wk, L3_ffn_wv, L3_ffn_wo, L3_ffn_router_w, L3_ffn_w1, L3_ffn_w2, L3_ffn_w3):
    import jax
    import jax.numpy as jnp

    def _L0_gnn_ref(x, mask, w_se, b_se, conv1_w, bn1_g, bn1_b, bn1_m, bn1_v, conv2_w, bn2_g, bn2_b, bn2_m, bn2_v, w_msg, b_msg, w_ih, b_ih, w_hh, b_hh):
        import jax, jax.numpy as jnp
        import numpy as np
        from jax import lax
        DIM = 128
        EPS = 1e-05

        def _bn(h, g, b, m, v):
            scale = g / jnp.sqrt(v + EPS)
            return h * scale[None, :, None] + (b - m * scale)[None, :, None]

        def _conv1d(h, w, pad):
            return lax.conv_general_dilated(h, w, window_strides=(1,), padding=[(pad, pad)], dimension_numbers=('NCH', 'OIH', 'NCH'))
        d = x.shape[-1]
        xc = jnp.transpose(x, (0, 2, 1))
        h = _bn(_conv1d(xc, conv1_w, 0), bn1_g, bn1_b, bn1_m, bn1_v)
        h = jax.nn.relu(h)
        h = _bn(_conv1d(h, conv2_w, 8), bn2_g, bn2_b, bn2_m, bn2_v)
        x_conv = jnp.transpose(jax.nn.relu(h + xc), (0, 2, 1))
        s = x @ w_se.T + b_se
        sq = jnp.sum(s * s, axis=-1)
        dist = sq[:, :, None] + sq[:, None, :] - 2.0 * jnp.einsum('bnd,bmd->bnm', s, s)
        A = jnp.exp(-dist) * mask
        msg = jax.nn.relu(x @ w_msg.T + b_msg)
        x_nmp = jnp.einsum('bnm,bmd->bnd', A, msg)
        x_in = jnp.concatenate([x_conv, x_nmp], axis=-1)
        gi = x_in @ w_ih.T + b_ih
        gh = x @ w_hh.T + b_hh
        gi_r, gi_z, gi_n = (gi[..., :d], gi[..., d:2 * d], gi[..., 2 * d:])
        gh_r, gh_z, gh_n = (gh[..., :d], gh[..., d:2 * d], gh[..., 2 * d:])
        r = jax.nn.sigmoid(gi_r + gh_r)
        z = jax.nn.sigmoid(gi_z + gh_z)
        nn_ = jnp.tanh(gi_n + r * gh_n)
        return (1.0 - z) * nn_ + z * x

    def _L0_ffn_ref(x, gate_w, gate_b, w1, w2, w3):
        import jax, jax.numpy as jnp
        import numpy as np
        D_MODEL = 128
        N_EXPERTS = 16
        HIDDEN = 256
        SCALE = 0.02
        n_experts = w1.shape[0]
        logits = jnp.einsum('bsd,de->bse', x, gate_w) + gate_b
        probs = jax.nn.softmax(logits, axis=-1)
        top_probs, top_idx = jax.lax.top_k(probs, 2)
        top_probs = top_probs / jnp.sum(top_probs, axis=-1, keepdims=True)
        dispatch = jnp.sum(jax.nn.one_hot(top_idx, n_experts, dtype=x.dtype) * top_probs[..., None], axis=-2)
        h1 = jnp.einsum('bsd,edh->bseh', x, w1)
        h2 = jnp.einsum('bsd,edh->bseh', x, w2)
        hidden = jax.nn.silu(h1) * h2
        expert_out = jnp.einsum('bseh,eho->bseo', hidden, w3)
        return jnp.einsum('bseo,bse->bso', expert_out, dispatch)

    def _L1_gnn_ref(x, adj, W_t, b_t, W_h, theta):
        import jax, jax.numpy as jnp
        import numpy as np
        B, N, D = (4, 2048, 128)
        DENSITY = 0.02
        in_degrees = jnp.sum(adj, axis=-1)
        norm = jnp.power(in_degrees + 1e-06, -0.5)[..., None]
        f_hom = jnp.einsum('bnd,de->bne', x, theta) * norm
        f_hom = jnp.einsum('bnm,bmd->bnd', adj, f_hom) * norm
        f_het = jnp.einsum('bnd,de->bne', x, W_h)
        gate = jax.nn.sigmoid(jnp.einsum('bnd,de->bne', x, W_t) + b_t)
        out = gate * f_hom + (1.0 - gate) * f_het
        return jax.nn.elu(out)

    def _L1_ffn_ref(h, gate_w, gate_b, w1, b1, w2, b2):
        import math
        import jax, jax.numpy as jnp
        import numpy as np
        CAPACITY_FACTOR = 1.25
        B, L, D = h.shape
        E = gate_w.shape[1]
        T = B * L
        C = max(1, math.ceil(CAPACITY_FACTOR * T / E))
        x = h.reshape(T, D)
        logits = x @ gate_w + gate_b
        probs = jax.nn.softmax(logits, axis=-1)
        idx = jnp.argmax(probs, axis=-1)
        prb = jnp.take_along_axis(probs, idx[:, None], axis=1)[:, 0]
        one_hot = jax.nn.one_hot(idx, E, dtype=jnp.float32)
        pos = (jnp.cumsum(one_hot, axis=0) * one_hot).sum(-1).astype(jnp.int32) - 1
        kept = pos < C
        pos_safe = jnp.where(kept, pos, C)
        buf = jnp.zeros((E, C, D), dtype=h.dtype).at[idx, pos_safe].set(x, mode='drop')
        hmid = jax.nn.relu(jnp.einsum('ecd,edf->ecf', buf, w1) + b1[:, None, :])
        ybuf = jnp.einsum('ecf,efd->ecd', hmid, w2) + b2[:, None, :]
        pos_g = jnp.minimum(pos, C - 1)
        y_tok = ybuf[idx, pos_g] * (prb * kept)[:, None]
        y = y_tok.reshape(B, L, D)
        y = jnp.nan_to_num(y, nan=0.0, posinf=10000.0, neginf=-10000.0)
        return y

    def _L2_gnn_ref(x, adj, W_rel, b_rel, W_root, ln_gamma, ln_beta):
        import jax, jax.numpy as jnp
        import numpy as np
        B, K, H = (32, 512, 128)
        LN_EPS = 1e-05

        def layer_norm(x, gamma, beta):
            mu = jnp.mean(x, axis=-1, keepdims=True)
            var = jnp.mean(jnp.square(x - mu), axis=-1, keepdims=True)
            return (x - mu) * jax.lax.rsqrt(var + LN_EPS) * gamma + beta
        h = layer_norm(x, ln_gamma, ln_beta)
        agg = jnp.einsum('bij,bjh->bih', adj, h)
        conv = jnp.einsum('bkh,ho->bko', agg, W_rel) + b_rel + jnp.einsum('bkh,ho->bko', h, W_root)
        return x + jax.nn.relu(conv)

    def _L2_ffn_ref(x, W_fx, b_fx, W_x, b_x, W_slice, b_slice, temperature, hy_in_w, hy_conv_w, hy_conv_b, hy_dt_bias, hy_A_log, hy_D, hy_fcD_w, hy_norm_w, hy_out_w, out_w, out_b):
        import jax, jax.numpy as jnp
        import numpy as np
        H, P, G, NS, K = (8, 64, 64, 64, 3)
        D_INNER = H * P
        CONV_DIM = D_INNER + 2 * NS
        D_IN_PROJ = 2 * D_INNER + 2 * NS + 2 * H

        def _hydra(u, in_w, conv_w, conv_b, dt_bias, A_log, Dp, fcD_w, norm_w, out_w):
            Bt, L, _ = u.shape
            zxbcdt = u @ in_w.T
            z = zxbcdt[..., :D_INNER]
            xBC = zxbcdt[..., D_INNER:D_INNER + CONV_DIM]
            dt = zxbcdt[..., -2 * H:]
            dt = jnp.concatenate([dt[..., :H], jnp.flip(dt[..., H:], axis=1)], axis=0)
            dt = jax.nn.softplus(dt + dt_bias)
            xp = jnp.pad(xBC, ((0, 0), (K - 1, 0), (0, 0)))
            xBC = sum((xp[:, k:k + L, :] * conv_w[:, k] for k in range(K))) + conv_b
            xBC = jax.nn.silu(xBC)
            x = xBC[..., :D_INNER]
            Bm = xBC[..., D_INNER:D_INNER + NS]
            Cm = xBC[..., D_INNER + NS:]
            x_og = x
            x2 = jnp.concatenate([x, jnp.flip(x, 1)], 0).reshape(2 * Bt, L, H, P)
            B2 = jnp.concatenate([Bm, jnp.flip(Bm, 1)], 0)
            C2 = jnp.concatenate([Cm, jnp.flip(Cm, 1)], 0)
            dA = jnp.exp(dt * -jnp.exp(A_log))
            dBx = jnp.einsum('blh,bln,blhp->blhpn', dt, B2, x2)

            def step(h, inp):
                dA_t, dBx_t, C_t = inp
                h = h * dA_t[:, :, None, None] + dBx_t
                return (h, jnp.einsum('bhpn,bn->bhp', h, C_t))
            h0 = jnp.zeros((2 * Bt, H, P, NS), u.dtype)
            _, ys = jax.lax.scan(step, h0, (dA.transpose(1, 0, 2), dBx.transpose(1, 0, 2, 3, 4), C2.transpose(1, 0, 2)))
            y = ys.transpose(1, 0, 2, 3).reshape(2 * Bt, L, D_INNER)
            y_fw, y_bw = (y[:Bt], jnp.flip(y[Bt:], 1))
            y = jnp.pad(y_fw[:, :-1], ((0, 0), (1, 0), (0, 0))) + jnp.pad(y_bw[:, 1:], ((0, 0), (0, 1), (0, 0)))
            y = y + x_og * jnp.repeat(x_og @ fcD_w.T + Dp, P, axis=-1)
            yg = y * jax.nn.silu(z)
            yg = yg * jax.lax.rsqrt(jnp.mean(jnp.square(yg), -1, keepdims=True) + 1e-05) * norm_w
            return yg @ out_w.T
        B, N, _ = x.shape
        fx = (x @ W_fx.T + b_fx).reshape(B, N, H, P).transpose(0, 2, 1, 3)
        xm = (x @ W_x.T + b_x).reshape(B, N, H, P).transpose(0, 2, 1, 3)
        temp = jnp.maximum(temperature, 1e-06)
        sw = jax.nn.softmax((xm @ W_slice.T + b_slice) / temp, axis=-1)
        snorm = sw.sum(2)
        st = jnp.einsum('bhnc,bhng->bhgc', fx, sw) / (snorm + 1e-05)[..., None]
        st = st.transpose(0, 2, 1, 3).reshape(B, G, D_INNER)
        ot = _hydra(st, hy_in_w, hy_conv_w, hy_conv_b, hy_dt_bias, hy_A_log, hy_D, hy_fcD_w, hy_norm_w, hy_out_w)
        ot = ot.reshape(B, G, H, P).transpose(0, 2, 1, 3)
        out = jnp.einsum('bhgc,bhng->bhnc', ot, sw).transpose(0, 2, 1, 3).reshape(B, N, D_INNER)
        return out @ out_w.T + out_b

    def _L3_gnn_ref(node_state, adjacency, Wq, Wk, Wv, Wo, bo):
        import math
        import jax, jax.numpy as jnp
        import numpy as np
        HIDDEN = 128
        HEADS = 8
        HEAD_DIM = HIDDEN // HEADS
        b, n, _ = node_state.shape

        def split_heads(x):
            return x.reshape(b, n, HEADS, HEAD_DIM).transpose(0, 2, 1, 3)
        q = split_heads(node_state @ Wq.T)
        k = split_heads(node_state @ Wk.T)
        v = split_heads(node_state @ Wv.T)
        scores = jnp.einsum('bhqd,bhkd->bhqk', q, k) / math.sqrt(HEAD_DIM)
        log_adj = jnp.log(adjacency + 1e-06)
        scores = scores + log_adj[:, None, :, :]
        attn = jax.nn.softmax(scores, axis=-1)
        out = jnp.einsum('bhqk,bhkd->bhqd', attn, v)
        out = out.transpose(0, 2, 1, 3).reshape(b, n, HIDDEN)
        return out @ Wo.T + bo

    def _L3_ffn_ref(x, ln1_w, ln2_w, wq, wk, wv, wo, router_w, w1, w2, w3):
        import jax, jax.numpy as jnp
        import numpy as np
        B, T, C = (64, 192, 128)
        NH, NKV = (4, 2)
        HD = C // NH
        NREP = NH // NKV
        NE, TOPK = (8, 2)
        HID = int(8 / 3 * C)
        EPS_RMS = 1e-06

        def _rope_tables(t_len):
            inv_freq = 1.0 / 10000.0 ** (np.arange(0, HD, 2, dtype=np.float32) / HD)
            t = np.arange(t_len, dtype=np.float32)
            freqs = np.outer(t, inv_freq)
            emb = np.concatenate([freqs, freqs], axis=-1)
            return (jnp.asarray(np.cos(emb)), jnp.asarray(np.sin(emb)))

        def _rotate_half(x):
            h = x.shape[-1] // 2
            return jnp.concatenate([-x[..., h:], x[..., :h]], axis=-1)

        def _rmsnorm(v, w):
            return v * jax.lax.rsqrt(jnp.mean(v * v, axis=-1, keepdims=True) + EPS_RMS) * w
        Bx, Tx, Cx = x.shape
        h = _rmsnorm(x, ln1_w)
        q = (h @ wq.T).reshape(Bx, Tx, NH, HD).transpose(0, 2, 1, 3)
        k = (h @ wk.T).reshape(Bx, Tx, NKV, HD).transpose(0, 2, 1, 3)
        v = (h @ wv.T).reshape(Bx, Tx, NKV, HD).transpose(0, 2, 1, 3)
        cos, sin = _rope_tables(Tx)
        cos, sin = (cos[None, None], sin[None, None])
        q = q * cos + _rotate_half(q) * sin
        k = k * cos + _rotate_half(k) * sin
        k = jnp.repeat(k, NREP, axis=1)
        v = jnp.repeat(v, NREP, axis=1)
        scores = jnp.einsum('bhtd,bhsd->bhts', q, k) / jnp.sqrt(jnp.float32(HD))
        causal = jnp.tril(jnp.ones((Tx, Tx), dtype=bool))
        scores = jnp.where(causal[None, None], scores, jnp.float32(-1e+30))
        att = jax.nn.softmax(scores, axis=-1)
        y = jnp.einsum('bhts,bhsd->bhtd', att, v).transpose(0, 2, 1, 3).reshape(Bx, Tx, Cx)
        x = x + y @ wo.T
        flat = _rmsnorm(x, ln2_w).reshape(-1, Cx)
        probs = jax.nn.softmax(flat @ router_w.T, axis=-1)
        tp, ti = jax.lax.top_k(probs, TOPK)
        tp = tp / (jnp.sum(tp, axis=-1, keepdims=True) + 1e-09)
        weights = jnp.sum(tp[..., None] * jax.nn.one_hot(ti, NE, dtype=flat.dtype), axis=1)
        out = jnp.zeros_like(flat)
        for e in range(NE):
            hh = jax.nn.silu(flat @ w1[e].T) * (flat @ w3[e].T)
            out = out + weights[:, e:e + 1] * (hh @ w2[e].T)
        return x + out.reshape(Bx, Tx, Cx)
    x = x + _L0_gnn_ref(_layernorm(x, axis=-1), adj, L0_gnn_w_se, L0_gnn_b_se, L0_gnn_conv1_w, L0_gnn_bn1_g, L0_gnn_bn1_b, L0_gnn_bn1_m, L0_gnn_bn1_v, L0_gnn_conv2_w, L0_gnn_bn2_g, L0_gnn_bn2_b, L0_gnn_bn2_m, L0_gnn_bn2_v, L0_gnn_w_msg, L0_gnn_b_msg, L0_gnn_w_ih, L0_gnn_b_ih, L0_gnn_w_hh, L0_gnn_b_hh)
    x = x + _L0_ffn_ref(_layernorm(x, axis=-1), L0_ffn_gate_w, L0_ffn_gate_b, L0_ffn_w1, L0_ffn_w2, L0_ffn_w3)
    x = x + _L1_gnn_ref(_layernorm(x, axis=-1), adj, L1_gnn_W_t, L1_gnn_b_t, L1_gnn_W_h, L1_gnn_theta)
    x = x + _L1_ffn_ref(_layernorm(x, axis=-1), L1_ffn_gate_w, L1_ffn_gate_b, L1_ffn_w1, L1_ffn_b1, L1_ffn_w2, L1_ffn_b2)
    x = x + _L2_gnn_ref(_layernorm(x, axis=-1), adj, L2_gnn_W_rel, L2_gnn_b_rel, L2_gnn_W_root, L2_gnn_ln_gamma, L2_gnn_ln_beta)
    x = x + _L2_ffn_ref(_layernorm(x, axis=-1), L2_ffn_W_fx, L2_ffn_b_fx, L2_ffn_W_x, L2_ffn_b_x, L2_ffn_W_slice, L2_ffn_b_slice, L2_ffn_temperature, L2_ffn_hy_in_w, L2_ffn_hy_conv_w, L2_ffn_hy_conv_b, L2_ffn_hy_dt_bias, L2_ffn_hy_A_log, L2_ffn_hy_D, L2_ffn_hy_fcD_w, L2_ffn_hy_norm_w, L2_ffn_hy_out_w, L2_ffn_out_w, L2_ffn_out_b)
    x = x + _L3_gnn_ref(_layernorm(x, axis=-1), adj, L3_gnn_Wq, L3_gnn_Wk, L3_gnn_Wv, L3_gnn_Wo, L3_gnn_bo)
    x = x + _L3_ffn_ref(_layernorm(x, axis=-1), L3_ffn_ln1_w, L3_ffn_ln2_w, L3_ffn_wq, L3_ffn_wk, L3_ffn_wv, L3_ffn_wo, L3_ffn_router_w, L3_ffn_w1, L3_ffn_w2, L3_ffn_w3)
    return x

_drawn_inputs = setup_inputs


def setup_inputs(seed=0):
    import zlib

    import numpy as np

    out = dict(_drawn_inputs(seed))
    spreads = {'L0_gnn_b_se': (0.0, 0.8),
     'L0_gnn_bn1_g': (1.0, 0.558),
     'L0_gnn_bn1_b': (0.0, 0.3),
     'L0_gnn_bn1_m': (0.0, 0.297),
     'L0_gnn_bn1_v': (1.0, 0.6),
     'L0_gnn_bn2_g': (1.0, 0.2),
     'L0_gnn_bn2_b': (0.0, 0.402),
     'L0_gnn_bn2_m': (0.0, 0.324),
     'L0_gnn_bn2_v': (1.0, 0.6),
     'L0_gnn_b_msg': (0.0, 0.1),
     'L0_gnn_b_ih': (0.0, 0.1),
     'L0_gnn_b_hh': (0.0, 0.1),
     'L0_ffn_gate_b': (0.0, 0.8),
     'L1_ffn_gate_b': (0.0, 0.1),
     'L1_ffn_b1': (0.0, 0.8),
     'L1_ffn_b2': (0.0, 0.53),
     'L2_gnn_b_rel': (0.0, 0.545),
     'L2_gnn_ln_gamma': (1.0, 0.2),
     'L2_gnn_ln_beta': (0.0, 0.1),
     'L2_ffn_b_fx': (0.0, 0.57),
     'L2_ffn_b_x': (0.0, 0.8),
     'L2_ffn_b_slice': (0.0, 0.8),
     'L2_ffn_temperature': (0.5, 0.6),
     'L2_ffn_hy_conv_b': (0.0, 0.429),
     'L2_ffn_hy_dt_bias': (-4.600166320800781, 0.6),
     'L2_ffn_hy_D': (1.0, 0.6),
     'L2_ffn_hy_norm_w': (1.0, 0.6),
     'L2_ffn_out_b': (0.0, 0.362),
     'L3_ffn_ln1_w': (1.0, 0.6),
     'L3_ffn_ln2_w': (1.0, 0.6)}
    factors = {'L0_ffn_gate_w': 8.0,
     'L0_ffn_w1': 8.0,
     'L0_ffn_w2': 8.0,
     'L0_ffn_w3': 8.0,
     'L1_gnn_W_t': 6.457,
     'L1_gnn_b_t': 8.0,
     'L2_ffn_W_fx': 5.143,
     'L2_ffn_W_x': 8.0,
     'L2_ffn_W_slice': 8.0,
     'L2_ffn_hy_in_w': 3.167,
     'L2_ffn_hy_conv_w': 8.0,
     'L2_ffn_hy_A_log': 8.0,
     'L2_ffn_hy_fcD_w': 8.0,
     'L2_ffn_hy_out_w': 3.015,
     'L2_ffn_out_w': 3.078,
     'L3_gnn_Wq': 8.0,
     'L3_gnn_Wk': 8.0,
     'L3_gnn_bo': 4.933,
     'L3_ffn_wq': 8.0,
     'L3_ffn_wk': 8.0,
     'L3_ffn_wv': 8.0,
     'L3_ffn_wo': 8.0,
     'L3_ffn_router_w': 8.0,
     'L3_ffn_w1': 8.0,
     'L3_ffn_w2': 8.0,
     'L3_ffn_w3': 8.0}
    for name, (base, spread) in spreads.items():
        noise = np.random.default_rng([zlib.crc32(name.encode()), seed]).standard_normal(out[name].shape)
        drawn = base * np.exp(spread * noise) if base else spread * noise
        out[name] = jnp.asarray(drawn.astype(out[name].dtype))
    for name, factor in factors.items():
        out[name] = (out[name] * factor).astype(out[name].dtype)
    return out
```

```python
from contextlib import ExitStack

import numpy as np

import concourse.bass as bass
from concourse import mybir

F32 = mybir.dt.float32
I32 = mybir.dt.int32
ALU = mybir.AluOpType
ACT = mybir.ActivationFunctionType
AX = mybir.AxisListType
ds = bass.ds

P = 128
D = 128
GRAPHS, NODES = 32, 256
TILES = GRAPHS * NODES // P
TURN = 512
TT = TURN // P
TURNS = GRAPHS * NODES // TURN
EPS = 1e-5
RMS_EPS = 1e-6


def every_turn(eng, body):
    body(0, 0, True, False)
    body(1, 1, False, False)
    with eng.Fori(2, TURNS - 2, 2) as t:
        body(t, 0, False, False)
        body(t + 1, 1, False, False)
    body(TURNS - 2, 0, False, False)
    body(TURNS - 1, 1, False, True)


def then(eng, ins, sem, value):
    ins.then_inc(sem, 1)
    eng.wait_ge(sem, value)


CONV_TAPS, CONV_PAD = 17, 8


class Layout:

    def __init__(self, **fields):
        self.at, self.cols = {}, 0
        for name, (rows, cols) in fields.items():
            self.at[name] = (self.cols, rows, cols)
            self.cols += cols

    def view(self, region, name):
        c, rows, cols = self.at[name]
        return region[0:rows, c:c + cols]

    def pack(self, arrays):
        out = np.zeros((P, self.cols), np.float32)
        for name, (c, rows, cols) in self.at.items():
            out[0:rows, c:c + cols] = np.reshape(arrays[name], (rows, cols))
        return out


LAYOUT = {}
LAYOUT["gnn0"] = Layout(
    conv1=(P, D), conv2=(P, CONV_TAPS * D), w_se=(P, 3), b_se=(3, 1), bn=(P, 8),
    w_msg=(P, D), b_msg=(P, D), w_ih=(P, 6 * D), w_hh=(P, 3 * D), b_ih=(P, 3), b_hh=(P, 3))


SPARE = {"ffn2": 16 * P}


class Core:
    pass


def begin_phase(nc, c, name, nxt):
    s = {k: c.sem(f"{name}_{k}") for k in ("var_eps", "rstd", "squared")}
    k = c.order.index(name)
    with nc.Block() as block:
        @block.sync
        def _(sp):
            if k == 0:
                sp.dma_start(c.block[name], c.dram[name]).then_inc(c.w_ready[name], 16)
            if nxt:
                sp.dma_start(c.block[nxt], c.dram[nxt]).then_inc(c.w_ready[nxt], 16)
            sp.wait_ge(c.w_ready[name], 16)

        @block.vector
        def _(v):
            if name == "ffn3":
                mean_square(v, c.var_eps, c.MV, s["squared"], 0, s["var_eps"])
                v.memset(c.shift[:], 0.0)
            else:
                v.tensor_scalar(c.var_eps[:], c.MV[:, :, 1], EPS, None, ALU.add).then_inc(s["var_eps"], 1)
                v.wait_ge(s["rstd"], 1)
                v.scalar_tensor_tensor(c.shift[:], c.MV[:, :, 0], -1.0, c.rstd[:], ALU.mult, ALU.mult)

        @block.gpsimd
        def _(g):
            g.wait_ge(s["var_eps"], 1)
            g.tensor_tensor(c.rstd[:], c.var_eps[:], c.minus_half[:], ALU.pow).then_inc(s["rstd"], 1)


def normalise(v, c, turn, h):
    for k in range(TT):
        t = turn * TT + k
        ins = v.tensor_scalar(h[:, k, :], c.src[:, t, :], c.rstd[:, ds(t, 1)], c.shift[:, ds(t, 1)],
                              ALU.mult, ALU.add)
    return ins


def finish_rows(v, c, stats, turn, store=True):
    for k in range(TT):
        ins = v.bn_stats(c.bn[:, k, :], c.xs[:, k, :])
    then(v, ins, stats, turn * 2 + 1)
    if store:
        v.tensor_scalar(c.X[:, ds(turn * TT, TT), :], c.xs[:], 1.0, None, ALU.mult)
    else:
        hold(v, c)
    for k in range(TT):
        ins = v.bn_aggr(c.mv[:, k, :], c.bn[:, k, :])
    then(v, ins, stats, turn * 2 + 2)
    v.tensor_scalar(c.MV[:, ds(turn * TT, TT), :], c.mv[:], 1.0, None, ALU.mult)


def hold(v, c, cell=1):
    v.tensor_copy(c.tick[:, cell:cell + 1], c.tick[:, 0:1])


def mean_square(v, out, mv, sem, turn, done):
    then(v, v.tensor_tensor(out[:], mv[:, :, 0], mv[:, :, 0], ALU.mult), sem, turn + 1)
    v.scalar_tensor_tensor(out[:], out[:], RMS_EPS, mv[:, :, 1], ALU.add, ALU.add).then_inc(done, 1)


def wait_past(eng, sem, value):
    if not isinstance(value, int) or value > 0:
        eng.wait_ge(sem, value)


def tiles4(ap):
    return ap.rearrange("p (k d) -> p k d", k=TT)


def phase_gnn0(nc, c):
    L, W = LAYOUT["gnn0"], c.block["gnn0"]
    w = {n: L.view(W, n) for n in L.at}
    conv2 = w["conv2"].rearrange("p (k o) -> p k o", k=CONV_TAPS)
    w_ih = w["w_ih"].rearrange("p (a g o) -> p a g o", a=2, g=3)
    w_hh = w["w_hh"].rearrange("p (g o) -> p g o", g=3)
    SEG = NODES + 2 * CONV_PAD
    with ExitStack() as ctx:
        def sb(name, shape):
            return ctx.enter_context(nc.sbuf_tensor("g0_" + name, shape, F32))

        def sem(name):
            return c.sem("g0_" + name)

        h = sb("h", [P, TT, D])
        hT = [sb(f"hT{i}", [P, TURN]) for i in range(2)]
        cpad = sb("cpad", [P, 2, SEG])
        adj = [sb(f"adj{i}", [P, 4, NODES]) for i in range(2)]
        xconv = sb("xconv", [P, TURN])
        sT, s2T, sqT = sb("sT", [3, TURN]), sb("s2T", [3, TURN]), sb("sqT", [3, TURN])
        minus1 = sb("minus1", [3, P])
        nsq = sb("nsq", [P, 4])
        A = sb("A", [P, 4, NODES])
        msg = sb("msg", [P, TT, D])
        nmp = sb("nmp", [P, TURN])
        ghb, q, e, outT = (sb(n, [P, TURN]) for n in ("ghb", "q", "e", "outT"))
        bnc = sb("bnc", [P, 12])
        scale1, shift1, scale2, shift2 = (bnc[:, i:i + 1] for i in range(4))
        rz_half = sb("rz_half", [P, 2])
        B = c.bank

        consts = sem("consts"); consts_pow = sem("consts_pow"); vlink0 = sem("vlink0")
        h_ready = sem("h_ready")
        hT_ps, hT_ready = sem("hT_ps"), sem("hT_ready")
        c1_ps, c1_ready = sem("c1_ps"), sem("c1_ready")
        s_ps, s_ready, s2_ready = sem("s_ps"), sem("s_ready"), sem("s2_ready")
        msg_ps, msg_ready = sem("msg_ps"), sem("msg_ready")
        nsq_ps, nsq_ready = sem("nsq_ps"), sem("nsq_ready")
        dist_ps, exp_ready, A_ready = sem("dist_ps"), sem("exp_ready"), sem("A_ready")
        adj_ready = [sem(f"adj_ready{i}") for i in range(2)]
        c2_ps, xpre_ready, xconv_ready = sem("c2_ps"), sem("xpre_ready"), sem("xconv_ready")
        nmp_ps, nmp_ready = sem("nmp_ps"), sem("nmp_ready")
        ghn_ps, r_ps, z_ps, n_ps = sem("ghn_ps"), sem("r_ps"), sem("z_ps"), sem("n_ps")
        r_ready, z_ready, npre_ready, n_ready = sem("r_ready"), sem("z_ready"), sem("npre_ready"), sem("n_ready")
        outT_ready, out_ps, x_done = sem("outT_ready"), sem("out_ps"), sem("x_done")
        msg_biased, stats = sem("msg_biased"), sem("stats")
        r_gh, h_minus_n, z_part = sem("r_gh"), sem("h_minus_n"), sem("z_part")

        with nc.Block() as block:
            @block.sync
            def _(sp):
                def load(t, par, first, last):
                    if not first and not (isinstance(t, int) and t == 1):
                        sp.wait_ge(A_ready, t - 1)
                    sp.dma_start(adj[par][:], c.adjT[t]).then_inc(adj_ready[par], 16)
                every_turn(sp, load)

            @block.gpsimd
            def _(g):
                g.wait_ge(consts, 1)
                g.tensor_tensor(bnc[:, 6:8], bnc[:, 4:6], c.minus_half[:, 0:2], ALU.pow).then_inc(consts_pow, 1)

            @block.vector
            def _(v):
                bn = w["bn"].rearrange("p (l k) -> p l k", l=2)
                v.memset(cpad[:], 0.0)
                v.memset(minus1[:], -1.0)
                v.tensor_scalar(bnc[:, 4:6], bn[:, :, 3], EPS, None, ALU.add).then_inc(consts, 1)
                v.tensor_tensor(bnc[:, 8:11], w["b_ih"], w["b_hh"], ALU.add).then_inc(vlink0, 1)
                v.wait_ge(vlink0, 1)
                v.tensor_scalar(rz_half[:], bnc[:, 8:10], 0.5, None, ALU.mult)
                v.wait_ge(consts_pow, 1)
                v.tensor_tensor(bnc[:, 6:8], bnc[:, 6:8], bn[:, :, 0], ALU.mult).then_inc(vlink0, 1)
                v.wait_ge(vlink0, 2)
                v.tensor_copy(bnc[:, 0:3:2], bnc[:, 6:8])
                v.tensor_tensor(bnc[:, 4:6], bn[:, :, 2], bnc[:, 6:8], ALU.mult).then_inc(vlink0, 1)
                v.wait_ge(vlink0, 3)
                v.tensor_tensor(bnc[:, 1:4:2], bn[:, :, 1], bnc[:, 4:6], ALU.subtract).then_inc(consts, 1)

                normalise(v, c, 0, h).then_inc(h_ready, 1)

                def residual(t):
                    v.wait_ge(out_ps, t + 1)
                    then(v, v.tensor_tensor(c.xs[:], c.X[:, ds(t * TT, TT), :], tiles4(B[0][:]), ALU.add),
                         x_done, t + 1)
                    finish_rows(v, c, stats, t)

                def turn(t, par, first, last):
                    v.wait_ge(s_ready, t + 1)
                    v.tensor_scalar(s2T[:], sT[:], 2.0, None, ALU.mult).then_inc(s2_ready, 1)
                    v.wait_ge(msg_ps, t + 1)
                    if not first:
                        v.wait_ge(nmp_ps, t)
                    then(v, v.tensor_tensor(msg[:], tiles4(B[3][:]), w["b_msg"][:, None, :].broadcast_to([P, TT, D]),
                                            ALU.add), msg_biased, t + 1)
                    v.tensor_scalar(msg[:], msg[:], 0.0, None, ALU.max).then_inc(msg_ready, 1)
                    v.wait_ge(ghn_ps, t + 1)
                    v.tensor_scalar(ghb[:], B[4][:], w["b_hh"][:, 2:3], 0.5, ALU.add, ALU.mult)
                    if not first:
                        residual(t - 1)
                    v.wait_ge(exp_ready, t + 1)
                    v.wait_ge(adj_ready[par], 8 * (t - par) + 16)
                    for j in range(2):
                        ins = v.tensor_tensor(A[:, 2 * j:2 * j + 2, :], B[5 + j][:].rearrange("p (m n) -> p m n", m=2),
                                              adj[par][:, 2 * j:2 * j + 2, :], ALU.mult)
                    ins.then_inc(A_ready, 1)
                    if not last:
                        v.wait_ge(hT_ps, t + 1)
                        normalise(v, c, t + 1, h).then_inc(h_ready, 1)
                    v.wait_ge(c2_ps, t + 1)
                    if not first:
                        v.wait_ge(xconv_ready, t)
                    v.scalar_tensor_tensor(q[:], B[1][:], scale2, hT[par][:], ALU.mult, ALU.add).then_inc(xpre_ready, 1)
                    v.wait_ge(r_ready, t + 1)
                    v.scalar_tensor_tensor(e[:], B[5][:], 1.0, ghb[:], ALU.add, ALU.mult).then_inc(r_gh, 1)
                    v.wait_ge(r_gh, t + 1)
                    v.wait_ge(n_ps, t + 1)
                    v.tensor_tensor(e[:], B[7][:], e[:], ALU.add).then_inc(npre_ready, 1)
                    v.wait_ge(n_ready, t + 1)
                    v.scalar_tensor_tensor(outT[:], B[7][:], -1.0, hT[par][:], ALU.mult, ALU.add).then_inc(h_minus_n, 1)
                    v.wait_ge(h_minus_n, t + 1)
                    v.wait_ge(z_ready, t + 1)
                    v.scalar_tensor_tensor(outT[:], B[6][:], 1.0, outT[:], ALU.add, ALU.mult).then_inc(z_part, 1)
                    v.wait_ge(z_part, t + 1)
                    v.scalar_tensor_tensor(outT[:], outT[:], 0.5, B[7][:], ALU.mult, ALU.add).then_inc(outT_ready, 1)
                every_turn(v, turn)
                residual(TURNS - 1)

            @block.scalar
            def _(a):
                def evac_hT(t, par):
                    a.wait_ge(hT_ps, t + 1)
                    a.activation(hT[par][:], B[0][:], ACT.Copy).then_inc(hT_ready, 1)
                a.wait_ge(consts, 2)
                evac_hT(0, 0)

                def turn(t, par, first, last):
                    a.wait_ge(c1_ps, t + 1)
                    for g in range(2):
                        ins = a.activation(cpad[:, g, CONV_PAD:CONV_PAD + NODES], B[1][:, g * NODES:(g + 1) * NODES],
                                           ACT.Relu, bias=shift1, scale=scale1)
                    ins.then_inc(c1_ready, 1)
                    a.wait_ge(s_ps, t + 1)
                    a.activation(sT[:], B[2][0:3, :], ACT.Identity, bias=w["b_se"])
                    a.activation(sqT[:], B[2][0:3, :], ACT.Square, bias=w["b_se"]).then_inc(s_ready, 1)
                    a.wait_ge(nsq_ps, t + 1)
                    a.activation(nsq[:], B[2][:, 0:4], ACT.Copy).then_inc(nsq_ready, 1)
                    a.wait_ge(nsq_ready, t + 1)
                    a.wait_ge(dist_ps, t + 1)
                    for k in range(4):
                        blk = B[5 + k // 2][:, (k % 2) * NODES:(k % 2 + 1) * NODES]
                        ins = a.activation(blk, blk, ACT.Exp, bias=nsq[:, k:k + 1])
                    ins.then_inc(exp_ready, 1)
                    if not last:
                        evac_hT(t + 1, 1 - par)
                    a.wait_ge(nmp_ps, t + 1)
                    a.activation(nmp[:], B[3][:], ACT.Copy).then_inc(nmp_ready, 1)
                    a.wait_ge(xpre_ready, t + 1)
                    a.activation(xconv[:], q[:], ACT.Relu, bias=shift2).then_inc(xconv_ready, 1)
                    a.wait_ge(r_ps, t + 1)
                    a.activation(B[5][:], B[5][:], ACT.Tanh, bias=rz_half[:, 0:1], scale=0.5).then_inc(r_ready, 1)
                    a.wait_ge(z_ps, t + 1)
                    a.activation(B[6][:], B[6][:], ACT.Tanh, bias=rz_half[:, 1:2], scale=0.5).then_inc(z_ready, 1)
                    a.wait_ge(npre_ready, t + 1)
                    a.activation(B[7][:], e[:], ACT.Tanh, bias=w["b_ih"][:, 2:3]).then_inc(n_ready, 1)
                every_turn(a, turn)

            @block.tensor
            def _(pe):
                mm = pe.matmul

                def to_features(t):
                    pe.wait_ge(h_ready, t + 1)
                    for k in range(TT):
                        ins = pe.transpose(B[0][:, k * P:(k + 1) * P], h[:, k, :], c.ident[:])
                    ins.then_inc(hT_ps, 1)

                def to_tokens(t):
                    pe.wait_ge(outT_ready, t + 1)
                    for k in range(TT):
                        ins = pe.transpose(B[0][:, k * P:(k + 1) * P], outT[:, k * P:(k + 1) * P], c.ident[:])
                    ins.then_inc(out_ps, 1)
                to_features(0)

                def turn(t, par, first, last):
                    hTp = hT[par]
                    pe.wait_ge(hT_ready, t + 1)
                    if not first:
                        pe.wait_ge(xpre_ready, t)
                    mm(B[1][:], w["conv1"], hTp[:], start=True, stop=True).then_inc(c1_ps, 1)
                    if not first:
                        pe.wait_ge(nsq_ready, t)
                    mm(B[2][0:3, :], w["w_se"], hTp[:], start=True, stop=True).then_inc(s_ps, 1)
                    if not first:
                        pe.wait_ge(nmp_ready, t)
                    for k in range(TT):
                        ins = mm(B[3][:, k * P:(k + 1) * P], hTp[:, k * P:(k + 1) * P], w["w_msg"], start=True, stop=True)
                    ins.then_inc(msg_ps, 1)
                    mm(B[4][:], w_hh[:, 2, :], hTp[:], start=True, stop=True).then_inc(ghn_ps, 1)
                    pe.wait_ge(c1_ready, t + 1)

                    def taps(a, b):
                        for k in range(a, b):
                            ins = mm(B[1][:].rearrange("p (g n) -> p g n", g=2), conv2[:, k, :], cpad[:, :, k:k + NODES],
                                     start=(k == 0), stop=(k == CONV_TAPS - 1))
                        return ins
                    taps(0, 6)
                    if not first:
                        to_tokens(t - 1)
                    pe.wait_ge(s_ready, t + 1)
                    pe.wait_ge(s2_ready, t + 1)
                    for k in range(4):
                        ins = mm(B[2][:, k:k + 1], sqT[:, k * P:(k + 1) * P], minus1[:, 0:1], start=True, stop=True)
                    ins.then_inc(nsq_ps, 1)
                    for k in range(4):
                        g = k // 2
                        blk = B[5 + g][:, (k % 2) * NODES:(k % 2 + 1) * NODES]
                        mm(blk, s2T[:, k * P:(k + 1) * P], sT[:, g * NODES:(g + 1) * NODES], start=True, stop=False)
                        ins = mm(blk, minus1[:], sqT[:, g * NODES:(g + 1) * NODES], start=False, stop=True)
                    ins.then_inc(dist_ps, 1)
                    taps(6, CONV_TAPS).then_inc(c2_ps, 1)
                    if not last:
                        if not first:
                            pe.wait_ge(x_done, t)
                        to_features(t + 1)
                    pe.wait_ge(A_ready, t + 1)
                    pe.wait_ge(msg_ready, t + 1)
                    for g in range(2):
                        for m in range(2):
                            ins = mm(B[3][:, g * NODES:(g + 1) * NODES], msg[:, 2 * g + m, :], A[:, 2 * g + m, :],
                                     start=(m == 0), stop=(m == 1))
                    ins.then_inc(nmp_ps, 1)
                    for gate in range(2):
                        mm(B[5 + gate][:], w_hh[:, gate, :], hTp[:], start=True, stop=False)
                    pe.wait_ge(nmp_ready, t + 1)
                    for gate in range(3):
                        mm(B[5 + gate][:], w_ih[:, 1, gate, :], nmp[:], start=(gate == 2), stop=False)
                    pe.wait_ge(xconv_ready, t + 1)
                    for gate, done in ((0, r_ps), (2, n_ps), (1, z_ps)):
                        mm(B[5 + gate][:], w_ih[:, 0, gate, :], xconv[:], start=False, stop=True).then_inc(done, 1)
                every_turn(pe, turn)
                to_tokens(TURNS - 1)


class Experts:
    def __init__(self, count, chunks, top, gated, eps=0.0, capacity=None):
        self.count, self.chunks, self.top, self.gated = count, chunks, top, gated
        self.eps, self.capacity = eps, capacity
        self.hidden = sum(chunks)


MOE = {
    "ffn0": Experts(16, (128, 128), 2, True),
    "ffn1": Experts(8, (128,) * 4, 1, False, capacity=int(np.ceil(1.25 * TILES * P / 8))),
    "ffn3": Experts(8, (128, 128, 85), 2, True, eps=1e-9),
}
FLT_MAX = 3.4028234e38


def moe_fields(m):
    f = {"gate_w": (P, m.count), "w1": (P, m.count * m.hidden), "w3": (P, m.count * len(m.chunks) * D)}
    if m.gated:
        f["w2"] = (P, m.count * m.hidden)
    return f


LAYOUT["ffn0"] = Layout(gate_b=(P, 16), **moe_fields(MOE["ffn0"]))
LAYOUT["ffn1"] = Layout(gate_b=(P, 8), b1=(P, 8 * 4), b2=(8, D), **moe_fields(MOE["ffn1"]))
LAYOUT["ffn3"] = Layout(ln2=(P, 1), **moe_fields(MOE["ffn3"]))


def phase_moe(nc, c, name):
    m, L = MOE[name], LAYOUT[name]
    W = c.block[name]
    w = {n: L.view(W, n) for n in L.at}
    E, NCH = m.count, len(m.chunks)
    U = E * NCH
    EY = E + (0 if m.gated else 1)
    w1 = w["w1"].rearrange("p (e h) -> p e h", e=E)
    w2 = w["w2"].rearrange("p (e h) -> p e h", e=E) if m.gated else None
    w3 = w["w3"].rearrange("p (e c d) -> p e c d", e=E, c=NCH)
    B = c.bank
    BH1, BH2, BY = (B[1], B[2]), (B[3], B[4]), (B[5], B[6])
    BR = B[7]
    with ExitStack() as ctx:
        def sb(n, shape, dt=F32):
            return ctx.enter_context(nc.sbuf_tensor(f"{name}_{n}", shape, dt))

        def sem(n):
            return c.sem(f"{name}_{n}")
        h = sb("h", [P, TT, D])
        hT = [sb(f"hT{i}", [P, TURN]) for i in range(2)]
        disp = [sb(f"disp{i}", [P, TT, E]) for i in range(2)]
        logits = sb("logits", [P, TT, E])
        top1 = sb("top1", [P, TT])
        probs = sb("probs", [P, TT, E + 8])
        replaced = sb("replaced", [P, TT, E + 8])
        best, chosen = sb("best", [P, TT, 8]), sb("chosen", [P, TT, 8])
        mask = sb("mask", [P, TT, E])
        psum_, rsum, den, rden = (sb(n, [P, TT]) for n in ("sum", "rsum", "den", "rden"))
        act = [sb(f"act{i}", [P, TURN]) for i in range(2)] if m.gated else None
        hid = [sb(f"hid{i}", [P, TURN]) for i in range(2 * NCH)]
        acc = sb("acc", [P, TT, D])
        if m.capacity:
            upto, ones = sb("upto", [P, P]), sb("ones", [P, P])
            before = sb("before", [P, TT + 1, E])
            rank, dispT = sb("rank", [P, TT, E]), [sb(f"dispT{i}", [E, TURN]) for i in range(2)]
            pos = sb("pos", [P, TT])
            finite, instead = sb("finite", [P, TT, D]), sb("instead", [P, TT, D])

        h_ready, hT_ps, hT_ready = sem("h_ready"), sem("hT_ps"), sem("hT_ready")
        logits_ps, logits_ready, exp_ready = sem("logits_ps"), sem("logits_ready"), sem("exp_ready")
        route, disp_ready = sem("route"), sem("disp_ready")
        h1_ps, h2_ps, act_ready, hid_ready = sem("h1_ps"), sem("h2_ps"), sem("act_ready"), sem("hid_ready")
        y_ps, y_used, stats, fill = sem("y_ps"), sem("y_used"), sem("stats"), sem("fill")
        setup = sem("setup")
        xs_ready = sem("xs_ready")
        if m.capacity:
            mask_ready, rank_ps, disp_done = sem("mask_ready"), sem("rank_ps"), sem("disp_done")
            dispT_ps, dispT_ready = sem("dispT_ps"), sem("dispT_ready")
            nan_fix = sem("nan_fix")
        ROUTE = 8 + (3 + TT if m.capacity else 2 + (m.eps > 0))

        with nc.Block() as block:
            if m.capacity:
                @block.gpsimd
                def _(g):
                    g.memset(ones[:], 1.0)
                    g.memset(upto[:], 1.0).then_inc(setup, 1)
                    g.wait_ge(setup, 1)
                    g.affine_select(out=upto[:], in_=upto[:], compare_op=ALU.is_ge, fill=0.0, base=0,
                                    pattern=[[1, P]], channel_multiplier=-1).then_inc(setup, 1)

            @block.vector
            def _(v):
                v.memset(probs[:, :, E:E + 8], -1.0)
                v.memset(chosen[:], -1.0).then_inc(fill, 1)
                v.wait_ge(fill, 1)
                if m.capacity:
                    v.memset(before[:], 0.0).then_inc(fill, 1)
                    v.wait_ge(fill, 2)
                normalise(v, c, 0, h).then_inc(h_ready, 1)

                def route_logits(t):
                    n = t * ROUTE
                    v.wait_ge(logits_ps, t + 1)
                    wait_past(v, exp_ready, t)
                    lp = BR[:, 0:TT * E].rearrange("p (k e) -> p k e", k=TT)
                    if "gate_b" in w:
                        then(v, v.tensor_tensor(logits[:], lp, w["gate_b"][:, None, :].broadcast_to([P, TT, E]), ALU.add), route, n + 1)
                    else:
                        then(v, v.tensor_copy(logits[:], lp), route, n + 1)
                    then(v, v.tensor_reduce(top1[:], logits[:], AX.X, ALU.max), route, n + 2)
                    v.tensor_tensor(logits[:], logits[:], top1[:, :, None].broadcast_to([P, TT, E]), ALU.subtract).then_inc(logits_ready, 1)

                def route_weights(t, par):
                    n = t * ROUTE + 2
                    p = probs[:, :, 0:E]
                    v.wait_ge(exp_ready, t + 1)
                    then(v, v.tensor_reduce(psum_[:], p, AX.X, ALU.add), route, n + 1)
                    then(v, v.reciprocal(rsum[:], psum_[:]), route, n + 2)
                    then(v, v.tensor_tensor(p, p, rsum[:, :, None].broadcast_to([P, TT, E]), ALU.mult), route, n + 3)
                    hold(v, c)
                    for k in range(TT):
                        ins = v.max(best[:, k, :], probs[:, k, 0:E])
                    then(v, ins, route, n + 4)
                    then(v, v.tensor_copy(chosen[:, :, 0:m.top], best[:, :, 0:m.top]), route, n + 5)
                    hold(v, c)
                    for k in range(TT):
                        ins = v.match_replace(replaced[:, k, :], chosen[:, k, :], probs[:, k, :], -2.0)
                    then(v, ins, route, n + 6)
                    n = n + 6
                    if m.capacity:
                        v.tensor_scalar(mask[:], replaced[:, :, 0:E], -1.5, None, ALU.is_lt).then_inc(mask_ready, 1)
                        v.wait_ge(mask_ready, t + 1)
                        for k in range(TT):
                            then(v, v.tensor_tensor(before[:, k + 1, :], before[:, k, :], mask[:, k, :], ALU.add), route, n + k + 1)
                        n = n + TT
                        v.wait_ge(rank_ps, t + 1)
                        then(v, v.tensor_tensor(rank[:], BR[:, 0:TT * E].rearrange("p (k e) -> p k e", k=TT), mask[:], ALU.mult), route, n + 1)
                        v.tensor_copy(before[:, 0, :], before[:, TT, :])
                        then(v, v.tensor_reduce(pos[:], rank[:], AX.X, ALU.add), route, n + 2)
                        v.tensor_tensor(mask[:], mask[:], p, ALU.mult)
                        then(v, v.tensor_scalar(pos[:], pos[:], float(m.capacity), None, ALU.is_le), route, n + 3)
                        v.tensor_tensor(disp[par][:], mask[:], pos[:, :, None].broadcast_to([P, TT, E]), ALU.mult).then_inc(disp_done, 1)
                    else:
                        v.tensor_scalar(mask[:], replaced[:, :, 0:E], -1.5, None, ALU.is_lt)
                        then(v, v.tensor_tensor(den[:], best[:, :, 0], best[:, :, 1], ALU.add), route, n + 1)
                        if m.eps:
                            then(v, v.tensor_scalar(den[:], den[:], m.eps, None, ALU.add), route, n + 2)
                            n = n + 1
                        v.reciprocal(rden[:], den[:])
                        then(v, v.tensor_tensor(mask[:], mask[:], p, ALU.mult), route, n + 2)
                        then(v, v.tensor_tensor(disp[par][:], mask[:], rden[:, :, None].broadcast_to([P, TT, E]), ALU.mult),
                             disp_ready, t + 1)

                route_logits(0)
                route_weights(0, 0)

                def use_y(t, par, e):
                    v.wait_ge(y_ps, t * EY + e + 1)
                    y = tiles4(BY[(t * EY + e) % 2 if isinstance(t, int) else (par * EY + e) % 2][:])
                    wait_past(v, y_used, t * EY + e)
                    if e == E:
                        ins = v.tensor_tensor(acc[:], acc[:], y, ALU.add)
                    else:
                        for k in range(TT):
                            if e == 0:
                                ins = v.tensor_scalar(acc[:, k, :], y[:, k, :], disp[par][:, k, e:e + 1], None, ALU.mult)
                            else:
                                ins = v.scalar_tensor_tensor(acc[:, k, :], y[:, k, :], disp[par][:, k, e:e + 1],
                                                             acc[:, k, :], ALU.mult, ALU.add)
                    ins.then_inc(y_used, 1)

                def turn(t, par, first, last):
                    if m.capacity:
                        v.wait_ge(disp_done, t + 1)
                    for e in range(E):
                        for ch in range(NCH):
                            u, rows = e * NCH + ch, m.chunks[ch]
                            if m.gated:
                                v.wait_ge(act_ready, t * U + u + 1)
                                v.wait_ge(h2_ps, t * U + u + 1)
                                wait_past(v, y_ps, t * EY + e - 1)
                                bh2 = BH2[(par * U + u) % 2]
                                v.tensor_tensor(hid[(e % 2) * NCH + ch][0:rows, :], act[(par * U + u) % 2][0:rows, :],
                                                bh2[0:rows, :], ALU.mult).then_inc(hid_ready, 1)
                        if e > 0:
                            use_y(t, par, e - 1)
                        if not last:
                            if e == 1:
                                v.wait_ge(hT_ps, t + 1)
                                normalise(v, c, t + 1, h).then_inc(h_ready, 1)
                            if e == 3:
                                route_logits(t + 1)
                            if e == 5:
                                route_weights(t + 1, 1 - par)
                    use_y(t, par, E - 1)
                    if EY > E:
                        use_y(t, par, E)
                    v.wait_ge(y_used, t * EY + EY)
                    if m.capacity:
                        v.tensor_scalar(instead[:], acc[:], FLT_MAX, 1e4, ALU.is_gt, ALU.mult)
                        v.tensor_scalar(c.xs[:], acc[:], -FLT_MAX, -1e4, ALU.is_lt, ALU.mult)
                        v.tensor_scalar(finite[:], acc[:], FLT_MAX, None, ALU.is_le).then_inc(nan_fix, 1)
                        v.wait_ge(nan_fix, t * 3 + 1)
                        v.scalar_tensor_tensor(finite[:], acc[:], -FLT_MAX, finite[:], ALU.is_ge, ALU.mult)
                        then(v, v.tensor_tensor(instead[:], instead[:], c.xs[:], ALU.add), nan_fix, t * 3 + 2)
                        hold(v, c)
                        then(v, v.copy_predicated(instead[:], finite[:].bitcast(I32), acc[:]), nan_fix, t * 3 + 3)
                    y = instead if m.capacity else acc
                    then(v, v.tensor_tensor(c.xs[:], c.X[:, ds(t * TT, TT), :], y[:], ALU.add), xs_ready, t + 1)
                    finish_rows(v, c, stats, t)
                every_turn(v, turn)

            @block.scalar
            def _(a):
                def evac_hT(t, par):
                    a.wait_ge(hT_ps, t + 1)
                    if "ln2" in w:
                        a.activation(hT[par][:], B[0][:], ACT.Copy, scale=w["ln2"]).then_inc(hT_ready, 1)
                    else:
                        a.activation(hT[par][:], B[0][:], ACT.Copy).then_inc(hT_ready, 1)

                def softmax_exp(t):
                    a.wait_ge(logits_ready, t + 1)
                    a.activation(probs[:, :, 0:E], logits[:], ACT.Exp).then_inc(exp_ready, 1)

                def evac_dispT(t, par):
                    a.wait_ge(dispT_ps, t + 1)
                    a.activation(dispT[par][:], BR[0:E, :], ACT.Copy).then_inc(dispT_ready, 1)
                a.wait_ge(fill, 1)
                evac_hT(0, 0)
                softmax_exp(0)
                if m.capacity:
                    evac_dispT(0, 0)

                def turn(t, par, first, last):
                    for e in range(E):
                        for ch in range(NCH):
                            u, rows = e * NCH + ch, m.chunks[ch]
                            a.wait_ge(h1_ps, t * U + u + 1)
                            bh1 = BH1[(par * U + u) % 2][0:rows, :]
                            if m.gated:
                                wait_past(a, hid_ready, t * U + u - 1)
                                a.activation(act[(par * U + u) % 2][0:rows, :], bh1, ACT.Silu).then_inc(act_ready, 1)
                            else:
                                wait_past(a, y_ps, t * EY + e - 1)
                                a.activation(hid[(e % 2) * NCH + ch][0:rows, :], bh1, ACT.Relu,
                                             bias=w["b1"][:, u:u + 1]).then_inc(act_ready, 1)
                        if not last:
                            if e == 2:
                                evac_hT(t + 1, 1 - par)
                            if e == 4:
                                softmax_exp(t + 1)
                            if e == 7 and m.capacity:
                                evac_dispT(t + 1, 1 - par)
                every_turn(a, turn)

            @block.tensor
            def _(pe):
                mm = pe.matmul

                def to_features(t):
                    pe.wait_ge(h_ready, t + 1)
                    for k in range(TT):
                        ins = pe.transpose(B[0][:, k * P:(k + 1) * P], h[:, k, :], c.ident[:])
                    ins.then_inc(hT_ps, 1)

                def router(t, par):
                    pe.wait_ge(hT_ready, t + 1)
                    for k in range(TT):
                        ins = mm(BR[:, k * E:(k + 1) * E], hT[par][:, k * P:(k + 1) * P], w["gate_w"], start=True, stop=True)
                    ins.then_inc(logits_ps, 1)

                def ranks(t):
                    pe.wait_ge(route, t * ROUTE + 8 + TT)
                    for k in range(TT):
                        mm(BR[:, k * E:(k + 1) * E], upto[:], mask[:, k, :], start=True, stop=False)
                        ins = mm(BR[:, k * E:(k + 1) * E], ones[:], before[:, k, :], start=False, stop=True)
                    ins.then_inc(rank_ps, 1)

                def transpose_disp(t, par):
                    pe.wait_ge(disp_done, t + 1)
                    for k in range(TT):
                        ins = pe.transpose(BR[0:E, k * P:(k + 1) * P], disp[par][:, k, :], c.ident[:])
                    ins.then_inc(dispT_ps, 1)
                to_features(0)
                router(0, 0)
                if m.capacity:
                    pe.wait_ge(setup, 2)
                    ranks(0)
                    transpose_disp(0, 0)

                def second(t, par, e):
                    wait_past(pe, y_used, t * EY + e - 1)
                    y = BY[(par * EY + e) % 2]
                    if e == E:
                        pe.wait_ge(dispT_ready, t + 1)
                        for k in range(TT):
                            ins = mm(y[:, k * P:(k + 1) * P], dispT[par][:, k * P:(k + 1) * P], w["b2"], start=True, stop=True)
                    else:
                        pe.wait_ge(hid_ready if m.gated else act_ready, t * U + e * NCH + NCH)
                        for k in range(TT):
                            for ch in range(NCH):
                                rows = m.chunks[ch]
                                ins = mm(y[:, k * P:(k + 1) * P], hid[(e % 2) * NCH + ch][0:rows, k * P:(k + 1) * P],
                                         w3[0:rows, e, ch, :], start=(ch == 0), stop=(ch == NCH - 1))
                    ins.then_inc(y_ps, 1)

                def turn(t, par, first, last):
                    for e in range(E):
                        at = 0
                        for ch in range(NCH):
                            u, rows = e * NCH + ch, m.chunks[ch]
                            wait_past(pe, act_ready, t * U + u - 1)
                            mm(BH1[(par * U + u) % 2][0:rows, :], w1[:, e, at:at + rows], hT[par][:], start=True, stop=True).then_inc(h1_ps, 1)
                            if m.gated:
                                wait_past(pe, hid_ready, t * U + u - 1)
                                mm(BH2[(par * U + u) % 2][0:rows, :], w2[:, e, at:at + rows], hT[par][:], start=True, stop=True).then_inc(h2_ps, 1)
                            at += rows
                        if e > 0:
                            second(t, par, e - 1)
                        if not last:
                            if e == 2:
                                to_features(t + 1)
                            if e == 3:
                                router(t + 1, 1 - par)
                            if e == 6 and m.capacity:
                                ranks(t + 1)
                            if e == 7 and m.capacity:
                                transpose_disp(t + 1, 1 - par)
                    second(t, par, E - 1)
                    if EY > E:
                        second(t, par, E)
                every_turn(pe, turn)


LAYOUT["gnn1"] = Layout(theta=(P, D), w_t=(P, D), w_h=(P, D), b_t=(P, D))


def phase_gnn1(nc, c):
    L = LAYOUT["gnn1"]
    W = c.block["gnn1"]
    w = {n: L.view(W, n) for n in L.at}
    B = c.bank
    with ExitStack() as ctx:
        def sb(n, shape, dt=F32):
            return ctx.enter_context(nc.sbuf_tensor(f"g1_{n}", shape, dt))

        def sem(n):
            return c.sem(f"g1_{n}")
        h = sb("h", [P, TT, D])
        hT = [sb(f"hT{i}", [P, TURN]) for i in range(2)]
        adj = [sb(f"adj{i}", [P, 4, NODES]) for i in range(2)]
        one = sb("one", [P, 1])
        deg = sb("deg", [P, TT])
        norm = [sb(f"norm{i}", [P, TT]) for i in range(2)]
        f = [sb(f"f{i}", [P, TT, D]) for i in range(2)]
        gpre = [sb(f"gpre{i}", [P, TT, D]) for i in range(2)]
        het = [sb(f"het{i}", [P, TT, D]) for i in range(2)]
        diff, neg, pos = sb("diff", [P, TT, D]), sb("neg", [P, TURN]), sb("pos", [P, TURN])

        one_ready = sem("one_ready")
        adj_ready = [sem(f"adj_ready{i}") for i in range(2)]
        h_ready, hT_ps, hT_ready = sem("h_ready"), sem("hT_ps"), sem("hT_ready")
        deg_ps, deg_ready, norm_ready = sem("deg_ps"), sem("deg_ready"), sem("norm_ready")
        f_ps, f_ready, gate_ps, gpre_ready = sem("f_ps"), sem("f_ready"), sem("gate_ps"), sem("gpre_ready")
        het_ps, het_ready = sem("het_ps"), sem("het_ready")
        gate_ready, agg_ps, diff_ready = sem("gate_ready"), sem("agg_ps"), sem("diff_ready")
        scaled, mixed, neg_ready, exp_ready = sem("scaled"), sem("mixed"), sem("neg_ready"), sem("exp_ready")
        elu_ready, x_sum, stats = sem("elu_ready"), sem("x_sum"), sem("stats")

        with nc.Block() as block:
            @block.sync
            def _(sp):
                def load(t, par, first, last):
                    wait_past(sp, agg_ps, t - 1)
                    sp.dma_start(adj[par][:], c.adjT[t]).then_inc(adj_ready[par], 16)
                every_turn(sp, load)

            @block.gpsimd
            def _(g):
                def degree_norm(t, par):
                    g.wait_ge(deg_ready, t + 1)
                    g.tensor_tensor(norm[par][:], deg[:], c.minus_half[:, 0:TT], ALU.pow).then_inc(norm_ready, 1)
                degree_norm(0, 0)

                def turn(t, par, first, last):
                    if not last:
                        degree_norm(t + 1, 1 - par)
                every_turn(g, turn)

            @block.vector
            def _(v):
                v.memset(one[:], 1.0).then_inc(one_ready, 1)

                def front(t, par):
                    v.wait_ge(deg_ps, t + 1)
                    wait_past(v, norm_ready, t)
                    v.tensor_scalar(deg[:], B[4][:, 0:TT], 1e-6, None, ALU.add).then_inc(deg_ready, 1)
                    v.wait_ge(gate_ps, t + 1)
                    v.tensor_tensor(gpre[par][:], tiles4(B[2][:]), w["b_t"][:, None, :].broadcast_to([P, TT, D]),
                                    ALU.add).then_inc(gpre_ready, 1)
                    v.wait_ge(norm_ready, t + 1)
                    v.wait_ge(f_ps, t + 1)
                    for k in range(TT):
                        ins = v.tensor_scalar(f[par][:, k, :], B[1][:, k * P:(k + 1) * P], norm[par][:, k:k + 1], None, ALU.mult)
                    ins.then_inc(f_ready, 1)
                normalise(v, c, 0, h).then_inc(h_ready, 1)
                front(0, 0)

                def turn(t, par, first, last):
                    if not last:
                        v.wait_ge(hT_ps, t + 1)
                        normalise(v, c, t + 1, h).then_inc(h_ready, 1)
                        front(t + 1, 1 - par)
                    v.wait_ge(agg_ps, t + 1)
                    v.wait_ge(het_ready, t + 1)
                    for k in range(TT):
                        ins = v.scalar_tensor_tensor(diff[:, k, :], B[5][:, k * P:(k + 1) * P], norm[par][:, k:k + 1],
                                                     het[par][:, k, :], ALU.mult, ALU.subtract)
                    then(v, ins, diff_ready, t + 1)
                    v.wait_ge(gate_ready, t + 1)
                    g6 = tiles4(B[6][:])
                    then(v, v.scalar_tensor_tensor(g6, g6, 1.0, diff[:], ALU.add, ALU.mult), scaled, t + 1)
                    then(v, v.scalar_tensor_tensor(g6, g6, 0.5, het[par][:], ALU.mult, ALU.add), mixed, t + 1)
                    v.tensor_scalar(pos[:], B[6][:], 0.0, None, ALU.max)
                    v.tensor_scalar(neg[:], B[6][:], 0.0, None, ALU.min).then_inc(neg_ready, 1)
                    v.wait_ge(exp_ready, t + 1)
                    then(v, v.scalar_tensor_tensor(B[7][:], B[7][:], -1.0, pos[:], ALU.add, ALU.add), elu_ready, t + 1)
                    then(v, v.tensor_tensor(c.xs[:], tiles4(B[7][:]), c.X[:, ds(t * TT, TT), :], ALU.add), x_sum, t + 1)
                    finish_rows(v, c, stats, t)
                every_turn(v, turn)

            @block.scalar
            def _(a):
                def front(t, par):
                    a.wait_ge(hT_ps, t + 1)
                    a.activation(hT[par][:], B[0][:], ACT.Copy).then_inc(hT_ready, 1)
                    a.wait_ge(het_ps, t + 1)
                    a.activation(het[par][:], tiles4(B[3][:]), ACT.Copy).then_inc(het_ready, 1)
                front(0, 0)

                def turn(t, par, first, last):
                    a.wait_ge(gpre_ready, t + 1)
                    wait_past(a, neg_ready, t)
                    a.activation(B[6][:], gpre[par][:].rearrange("p k d -> p (k d)"), ACT.Tanh, scale=0.5).then_inc(gate_ready, 1)
                    if not last:
                        front(t + 1, 1 - par)
                    a.wait_ge(neg_ready, t + 1)
                    a.activation(B[7][:], neg[:], ACT.Exp).then_inc(exp_ready, 1)
                every_turn(a, turn)

            @block.tensor
            def _(pe):
                mm = pe.matmul

                def to_features(t):
                    pe.wait_ge(h_ready, t + 1)
                    wait_past(pe, hT_ready, t)
                    for k in range(TT):
                        ins = pe.transpose(B[0][:, k * P:(k + 1) * P], h[:, k, :], c.ident[:])
                    ins.then_inc(hT_ps, 1)

                def front(t, par):
                    to_features(t)
                    pe.wait_ge(adj_ready[par], 8 * (t - par) + 16)
                    wait_past(pe, deg_ready, t)
                    for k in range(TT):
                        g, n = k // 2, k % 2
                        for m in range(2):
                            ins = mm(B[4][:, k:k + 1], adj[par][:, 2 * g + m, n * P:(n + 1) * P], one[:],
                                     start=(m == 0), stop=(m == 1))
                    ins.then_inc(deg_ps, 1)
                    pe.wait_ge(hT_ready, t + 1)
                    for bank, weight, done, used in ((B[1], "theta", f_ps, f_ready), (B[2], "w_t", gate_ps, gpre_ready),
                                                     (B[3], "w_h", het_ps, het_ready)):
                        wait_past(pe, used, t)
                        for k in range(TT):
                            ins = mm(bank[:, k * P:(k + 1) * P], hT[par][:, k * P:(k + 1) * P], w[weight], start=True, stop=True)
                        ins.then_inc(done, 1)
                pe.wait_ge(one_ready, 1)
                front(0, 0)

                def turn(t, par, first, last):
                    if not last:
                        front(t + 1, 1 - par)
                    pe.wait_ge(f_ready, t + 1)
                    wait_past(pe, diff_ready, t)
                    for k in range(TT):
                        g, n = k // 2, k % 2
                        for m in range(2):
                            ins = mm(B[5][:, k * P:(k + 1) * P], adj[par][:, 2 * g + m, n * P:(n + 1) * P],
                                     f[par][:, 2 * g + m, :], start=(m == 0), stop=(m == 1))
                    ins.then_inc(agg_ps, 1)
                every_turn(pe, turn)


LAYOUT["gnn2"] = Layout(w_rel=(P, D), w_root=(P, D), b_rel=(P, D), gamma=(P, D), beta=(P, D))


def phase_gnn2(nc, c):
    L = LAYOUT["gnn2"]
    W = c.block["gnn2"]
    w = {n: L.view(W, n) for n in L.at}
    B = c.bank

    def wide(ap):
        return ap[:, None, :].broadcast_to([P, TT, D])
    with ExitStack() as ctx:
        def sb(n, shape, dt=F32):
            return ctx.enter_context(nc.sbuf_tensor(f"g2_{n}", shape, dt))

        def sem(n):
            return c.sem(f"g2_{n}")
        u = [sb(f"u{i}", [P, TT, D]) for i in range(2)]
        hn, hg = sb("hn", [P, TT, D]), sb("hg", [P, TT, D])
        h = [sb(f"h{i}", [P, TT, D]) for i in range(2)]
        hT = [sb(f"hT{i}", [P, TURN]) for i in range(2)]
        adj = [sb(f"adj{i}", [P, 4, NODES]) for i in range(2)]
        aggT = sb("aggT", [P, TURN])
        bn2, mv2 = sb("bn2", [P, TT, 6]), sb("mv2", [P, TT, 2])
        ve2, rstd2, shift2 = sb("ve2", [P, TT]), sb("rstd2", [P, TT]), sb("shift2", [P, TT])

        adj_ready = [sem(f"adj_ready{i}") for i in range(2)]
        norm2, ve2_ready, rstd2_ready = sem("norm2"), sem("ve2_ready"), sem("rstd2_ready")
        hn_ready, hg_ready, h_ready = sem("hn_ready"), sem("hg_ready"), sem("h_ready")
        hT_ps, hT_ready, agg_ps, agg_ready = sem("hT_ps"), sem("hT_ready"), sem("agg_ps"), sem("agg_ready")
        conv_ps, tail, x_sum, stats = sem("conv_ps"), sem("tail"), sem("x_sum"), sem("stats")

        with nc.Block() as block:
            @block.sync
            def _(sp):
                def load(t, par, first, last):
                    wait_past(sp, agg_ps, t - 1)
                    sp.dma_start(adj[par][:], c.adjT[t]).then_inc(adj_ready[par], 16)
                every_turn(sp, load)

            @block.gpsimd
            def _(g):
                def front(t, par):
                    g.wait_ge(ve2_ready, t + 1)
                    g.tensor_tensor(rstd2[:], ve2[:], c.minus_half[:, 0:TT], ALU.pow).then_inc(rstd2_ready, 1)
                    g.wait_ge(hn_ready, t + 1)
                    then(g, g.tensor_tensor(hg[:], hn[:], wide(w["gamma"]), ALU.mult), hg_ready, t + 1)
                    wait_past(g, conv_ps, t - 1)
                    g.tensor_tensor(h[par][:], hg[:], wide(w["beta"]), ALU.add).then_inc(h_ready, 1)
                front(0, 0)

                def turn(t, par, first, last):
                    if not last:
                        front(t + 1, 1 - par)
                every_turn(g, turn)

            @block.vector
            def _(v):
                def front(t, par):
                    n = t * 4
                    then(v, normalise(v, c, t, u[par]), norm2, n + 1)
                    for k in range(TT):
                        ins = v.bn_stats(bn2[:, k, :], u[par][:, k, :])
                    then(v, ins, norm2, n + 2)
                    hold(v, c)
                    for k in range(TT):
                        ins = v.bn_aggr(mv2[:, k, :], bn2[:, k, :])
                    then(v, ins, norm2, n + 3)
                    v.tensor_scalar(ve2[:], mv2[:, :, 1], EPS, None, ALU.add).then_inc(ve2_ready, 1)
                    v.wait_ge(rstd2_ready, t + 1)
                    then(v, v.scalar_tensor_tensor(shift2[:], mv2[:, :, 0], -1.0, rstd2[:], ALU.mult, ALU.mult), norm2, n + 4)
                    wait_past(v, hg_ready, t)
                    for k in range(TT):
                        ins = v.tensor_scalar(hn[:, k, :], u[par][:, k, :], rstd2[:, k:k + 1], shift2[:, k:k + 1], ALU.mult, ALU.add)
                    ins.then_inc(hn_ready, 1)
                front(0, 0)

                def turn(t, par, first, last):
                    if not last:
                        front(t + 1, 1 - par)
                    v.wait_ge(conv_ps, t + 1)
                    conv = tiles4(B[2 + par][:])
                    then(v, v.tensor_tensor(conv, conv, wide(w["b_rel"]), ALU.add), tail, 2 * t + 1)
                    then(v, v.scalar_tensor_tensor(conv, conv, 0.0, u[par][:], ALU.max, ALU.add), tail, 2 * t + 2)
                    then(v, v.tensor_tensor(c.xs[:], conv, c.X[:, ds(t * TT, TT), :], ALU.add), x_sum, t + 1)
                    finish_rows(v, c, stats, t)
                every_turn(v, turn)

            @block.scalar
            def _(a):
                def turn(t, par, first, last):
                    a.wait_ge(hT_ps, t + 1)
                    a.activation(hT[par][:], B[0][:], ACT.Copy).then_inc(hT_ready, 1)
                    a.wait_ge(agg_ps, t + 1)
                    a.activation(aggT[:], B[1][:], ACT.Copy).then_inc(agg_ready, 1)
                every_turn(a, turn)

            @block.tensor
            def _(pe):
                mm = pe.matmul

                def turn(t, par, first, last):
                    pe.wait_ge(h_ready, t + 1)
                    wait_past(pe, hT_ready, t)
                    for k in range(TT):
                        ins = pe.transpose(B[0][:, k * P:(k + 1) * P], h[par][:, k, :], c.ident[:])
                    ins.then_inc(hT_ps, 1)
                    pe.wait_ge(adj_ready[par], 8 * (t - par) + 16)
                    wait_past(pe, agg_ready, t)
                    for g in range(2):
                        for m in range(2):
                            ins = mm(B[1][:, g * NODES:(g + 1) * NODES], h[par][:, 2 * g + m, :], adj[par][:, 2 * g + m, :],
                                     start=(m == 0), stop=(m == 1))
                    ins.then_inc(agg_ps, 1)
                    wait_past(pe, x_sum, t - 1)
                    pe.wait_ge(hT_ready, t + 1)
                    pe.wait_ge(agg_ready, t + 1)
                    for k in range(TT):
                        mm(B[2 + par][:, k * P:(k + 1) * P], aggT[:, k * P:(k + 1) * P], w["w_rel"], start=True, stop=False)
                        ins = mm(B[2 + par][:, k * P:(k + 1) * P], hT[par][:, k * P:(k + 1) * P], w["w_root"], start=False, stop=True)
                    ins.then_inc(conv_ps, 1)
                every_turn(pe, turn)


HEADS2, HD2, SL = 8, 64, 64
IN2 = HEADS2 * HD2
KC = IN2 // P
NS2, TAPS2 = 64, 3
PROJ2 = 2 * IN2 + 2 * NS2 + 2 * HEADS2
LAYOUT["ffn2"] = Layout(
    w_fx=(P, IN2), b_fx=(P, IN2), w_x=(P, IN2), b_x=(P, KC), w_slice=(P, P), b_slice=(P, IN2), temp=(P, HEADS2),
    in_w=(P, KC * PROJ2), conv_x=(P, KC * TAPS2), convb_x=(P, KC), conv_bc=(NS2, 2 * TAPS2), convb_bc=(NS2, 2),
    dt_bias=(P, 2 * HEADS2), a_log=(P, 2 * HEADS2), skip=(P, HEADS2), fcd=(P, KC * HEADS2), norm_w=(P, IN2),
    hy_out=(P, KC * IN2), out_w=(P, KC * D), out_b=(P, D), masks=(P, 2 * P))


def phase_ffn2(nc, c):
    L = LAYOUT["ffn2"]
    W = c.block["ffn2"]
    w = {n: L.view(W, n) for n in L.at}
    in_w = w["in_w"].rearrange("p (k n) -> p k n", k=KC)
    conv_x = w["conv_x"].rearrange("p (k n) -> p k n", k=KC)
    conv_bc = w["conv_bc"].rearrange("p (k n) -> p k n", k=2)
    hy_out = w["hy_out"].rearrange("p (k n) -> p k n", k=KC)
    out_w = w["out_w"].rearrange("p (k n) -> p k n", k=KC)
    fcd = w["fcd"].rearrange("p (k n) -> p k n", k=KC)
    masks = w["masks"].rearrange("p (a t) -> p a t", a=2)
    B = c.bank

    def heads(ap):
        return ap.rearrange("p (h c) -> p h c", h=HEADS2)

    def per_head(ap, n):
        return ap[:, :, None].broadcast_to([P, ap.shape[1], n])
    with ExitStack() as ctx:
        def sb(n, shape, dt=F32):
            return ctx.enter_context(nc.sbuf_tensor(f"f2_{n}", shape, dt))

        def sem(n):
            return c.sem(f"f2_{n}")
        h, hT, xmT = sb("h", [P, TT, D]), sb("hT", [P, TURN]), sb("xmT", [P, KC, TURN])
        fx = [sb(f"fx{i}", [P, TT, IN2]) for i in range(2)]
        sw = [sb(f"sw{i}", [P, TT, IN2]) for i in range(2)]
        swT = sb("swT", [P, TT, KC, P])
        mx, sm, rsm = sb("mx", [P, HEADS2]), sb("sm", [P, HEADS2]), sb("rsm", [P, HEADS2])
        itemp, slice_w, slice_b = sb("itemp", [P, HEADS2]), sb("slice_w", [P, KC, P]), sb("slice_b", [P, IN2])
        ones, neg_a = sb("ones", [P, P]), sb("neg_a", [P, 2 * HEADS2])
        sn = sb("sn", [P, 2, KC, SL])
        stT = sb("stT", [P, KC, 2, SL])
        tz, sz = sb("tz", [P, IN2]), sb("sz", [P, IN2])
        xpad, xc, tx = sb("xpad", [P, KC, 2, TAPS2 - 1 + SL]), sb("xc", [P, KC, 2, SL]), sb("tx", [P, IN2])
        xT = sb("xT", [P, KC, P])
        bcpad, bc, tbc = sb("bcpad", [NS2, 2, 2, TAPS2 - 1 + SL]), sb("bc", [NS2, 2, 2, SL]), sb("tbc", [NS2, 2 * P])
        Bt, Cpad = sb("Bt", [NS2, P]), sb("Cpad", [NS2, P + 2])
        dtr, u, m, e, e2, r, s, s2, poly, dt, am = (sb(n, [P, 2 * HEADS2]) for n in (
            "dtr", "u", "m", "e", "e2", "r", "s", "s2", "poly", "dt", "am"))
        gm = sb("gm", [P, 2, P])
        xtok = sb("xtok", [P, IN2])
        xdt = [sb(f"xdt{i}", [P, IN2]) for i in range(2)]
        a_run = [sb(f"a_run{i}", [P, HEADS2, P]) for i in range(2)]
        decay = [c.spare["ffn2"][:, q * 4 * P:(q + 1) * 4 * P].rearrange("p (h t) -> p h t", h=4) for q in range(4)]
        g8, term, yg, yn = sb("g8", [P, HEADS2]), sb("term", [P, IN2]), sb("yg", [P, IN2]), sb("yn", [P, IN2])
        ms, ve, rstd = sb("ms", [P, 1]), sb("ve", [P, 1]), sb("rstdy", [P, 1])
        ygT, otT = sb("ygT", [P, KC, P]), sb("otT", [P, KC, 2, P])
        pm = sb("pm", [P, 2, KC, D])

        (setup, a_exp, h_ready, hT_ps, hT_ready, fx_ps, fx_ready, xm_ps, xm_ready, lg_ps, soft, lg_ready, lg_exp,
         sw_ready, st_ps, stn, stT_ready, z_ps, tz_ready, sz_ready, x_ps, xpad_ready, bcd_ps, bcd_ready, conv,
         xc_ready, bc_ready, tx_ready, tbc_ready, xT_ready, bct_ready, sp, spm_ready, spe_ready, dt_ready, G_ps,
         gm_ready, xt_ps, xtok_ready, fcd_ps, g8_ready, term_ready, a_run_ready, xdt_ready, D_ps, D_exp,
         decay_ready, y_ps, y_sum, yg_ready, ms_ready, ve_ready, rstd_ready, yn_ready, yT_ps, ygT_ready, ot_ps,
         otT_ready, pm_ps, pm_ready, swT_ps, swT_ready, fin_ps, x_sum, x_done, stats) = (sem(n) for n in (
             "setup a_exp h_ready hT_ps hT_ready fx_ps fx_ready xm_ps xm_ready lg_ps soft lg_ready lg_exp "
             "sw_ready st_ps stn stT_ready z_ps tz_ready sz_ready x_ps xpad_ready bcd_ps bcd_ready conv "
             "xc_ready bc_ready tx_ready tbc_ready xT_ready bct_ready sp spm_ready spe_ready dt_ready G_ps "
             "gm_ready xt_ps xtok_ready fcd_ps g8_ready term_ready a_run_ready xdt_ready D_ps D_exp "
             "decay_ready y_ps y_sum yg_ready ms_ready ve_ready rstd_ready yn_ready yT_ps ygT_ready ot_ps "
             "otT_ready pm_ps pm_ready swT_ps swT_ready fin_ps x_sum x_done stats").split())

        with nc.Block() as block:
            @block.gpsimd
            def _(g):
                def turn(t, par, first, last):
                    for d in range(2):
                        g.wait_ge(dt_ready, t + 1)
                        g.tensor_tensor(a_run[d][:], per_head(am[:, d * HEADS2:(d + 1) * HEADS2], P),
                                        masks[:, d, None, :].broadcast_to([P, HEADS2, P]), ALU.mult).then_inc(a_run_ready, 1)
                        g.wait_ge(xtok_ready, t + 1)
                        g.tensor_tensor(heads(xdt[d][:]), heads(xtok[:]), per_head(dt[:, d * HEADS2:(d + 1) * HEADS2], HD2),
                                        ALU.mult).then_inc(xdt_ready, 1)
                    g.wait_ge(g8_ready, t + 1)
                    g.tensor_tensor(heads(term[:]), heads(xtok[:]), per_head(g8[:], HD2), ALU.mult).then_inc(term_ready, 1)
                    g.wait_ge(ve_ready, t + 1)
                    g.tensor_tensor(rstd[:], ve[:], c.minus_half[:, 0:1], ALU.pow).then_inc(rstd_ready, 1)
                every_turn(g, turn)

            @block.vector
            def _(v):
                for z in (xpad, bcpad, Cpad, otT):
                    v.memset(z[:], 0.0)
                v.memset(ones[:], 1.0)
                then(v, v.tensor_scalar(itemp[:], w["temp"], 1e-6, None, ALU.max), setup, 1)
                then(v, v.reciprocal(itemp[:], itemp[:]), setup, 2)
                for j in range(KC):
                    v.tensor_tensor(slice_w[:, j, :].rearrange("p (a g) -> p a g", a=2),
                                    w["w_slice"].rearrange("p (a g) -> p a g", a=2), per_head(itemp[:, 2 * j:2 * j + 2], SL), ALU.mult)
                v.tensor_tensor(heads(slice_b[:]), heads(w["b_slice"]), per_head(itemp[:], SL), ALU.mult)
                for n in ("conv_x", "convb_x", "conv_bc", "convb_bc"):
                    v.tensor_scalar(w[n], w[n], 0.5, None, ALU.mult)
                v.wait_ge(a_exp, 1)
                v.tensor_scalar(neg_a[:], neg_a[:], -1.0, None, ALU.mult).then_inc(setup, 1)
                v.wait_ge(setup, 3)

                def fx_piece(t, par, k):
                    v.wait_ge(fx_ps, t * TT + k + 1)
                    v.tensor_tensor(fx[par][:, k, :], B[1][:], w["b_fx"], ALU.add).then_inc(fx_ready, 1)

                def soft_a(t, k):
                    n = (t * TT + k) * 4
                    v.wait_ge(lg_ps, t * TT + k + 1)
                    b3 = heads(B[3][:])
                    then(v, v.tensor_tensor(B[3][:], B[3][:], slice_b[:], ALU.add), soft, n + 1)
                    then(v, v.tensor_reduce(mx[:], b3, AX.X, ALU.max), soft, n + 2)
                    v.tensor_tensor(b3, b3, per_head(mx[:], SL), ALU.subtract).then_inc(lg_ready, 1)

                def soft_b(t, par, k):
                    n = (t * TT + k) * 4 + 2
                    v.wait_ge(lg_exp, t * TT + k + 1)
                    b3 = heads(B[3][:])
                    then(v, v.tensor_reduce(sm[:], b3, AX.X, ALU.add), soft, n + 1)
                    then(v, v.reciprocal(rsm[:], sm[:]), soft, n + 2)
                    v.tensor_tensor(heads(sw[par][:, k, :]), b3, per_head(rsm[:], SL), ALU.mult).then_inc(sw_ready, 1)

                def pooled(t, g):
                    n = (t * 2 + g) * 2
                    v.wait_ge(st_ps, t * 2 + g + 1)
                    num, den = (B[4 + 2 * g + i][:].rearrange("p (k a s) -> p k a s", k=KC, a=2) for i in range(2))
                    for a in range(2):
                        rows_ = slice(a * HD2, (a + 1) * HD2)
                        ins = v.tensor_scalar(sn[rows_, g], den[rows_, :, a, :], 1e-5, None, ALU.add)
                    then(v, ins, stn, n + 1)
                    then(v, v.reciprocal(sn[:, g], sn[:, g]), stn, n + 2)
                    for a in range(2):
                        rows_ = slice(a * HD2, (a + 1) * HD2)
                        ins = v.tensor_tensor(stT[rows_, :, g, :], num[rows_, :, a, :], sn[rows_, g], ALU.mult)
                    ins.then_inc(stT_ready, 1)

                def convolve(t, first_time, pad, weights, bias, out, k_range, done, n):
                    for tap in range(TAPS2 - 1, -1, -1):
                        for k in k_range:
                            src = pad[:, k, :, tap:tap + SL]
                            if tap == TAPS2 - 1:
                                ins = v.tensor_scalar(out[:, k], src, weights[:, k, tap:tap + 1], bias[:, k:k + 1], ALU.mult, ALU.add)
                            else:
                                ins = v.scalar_tensor_tensor(out[:, k], src, weights[:, k, tap:tap + 1], out[:, k], ALU.mult, ALU.add)
                        if tap:
                            n += 1
                            then(v, ins, conv, n)
                        else:
                            ins.then_inc(done, 1)

                normalise(v, c, 0, h).then_inc(h_ready, 1)
                for k in range(TT):
                    fx_piece(0, 0, k)
                for k in range(TT):
                    soft_a(0, k)
                    soft_b(0, 0, k)

                def turn(t, par, first, last):
                    more = not last
                    if more:
                        v.wait_ge(hT_ps, t + 1)
                        normalise(v, c, t + 1, h).then_inc(h_ready, 1)
                    pooled(t, 0)
                    pooled(t, 1)
                    v.wait_ge(tz_ready, t + 1)
                    v.scalar_tensor_tensor(sz[:], tz[:], 1.0, B[4][:], ALU.add, ALU.mult).then_inc(sz_ready, 1)
                    if more:
                        fx_piece(t + 1, 1 - par, 0)
                        fx_piece(t + 1, 1 - par, 1)
                    v.wait_ge(xpad_ready, t + 1)
                    convolve(t, first, xpad, conv_x, w["convb_x"], xc, range(KC), xc_ready, t * 4)
                    v.wait_ge(bcd_ready, t + 1)
                    convolve(t, first, bcpad, conv_bc, w["convb_bc"], bc, range(2), bc_ready, t * 4 + 2)
                    n = t * 14
                    then(v, v.tensor_tensor(u[:], dtr[:], w["dt_bias"], ALU.add), sp, n + 1)
                    v.scalar_tensor_tensor(m[:], u[:], -1.0, u[:], ALU.mult, ALU.min).then_inc(spm_ready, 1)
                    v.wait_ge(tx_ready, t + 1)
                    v.wait_ge(xc_ready, t + 1)
                    v.scalar_tensor_tensor(xT[:].rearrange("p k n -> p (k n)"), tx[:], 1.0, xc[:].rearrange("p k a s -> p (k a s)"),
                                           ALU.add, ALU.mult).then_inc(xT_ready, 1)
                    v.wait_ge(tbc_ready, t + 1)
                    v.wait_ge(bc_ready, t + 1)
                    bcf = bc[:].rearrange("p b a s -> p b (a s)")
                    v.scalar_tensor_tensor(Bt[:], tbc[:, 0:P], 1.0, bcf[:, 0, :], ALU.add, ALU.mult)
                    v.scalar_tensor_tensor(Cpad[:, 1:P + 1], tbc[:, P:2 * P], 1.0, bcf[:, 1, :], ALU.add, ALU.mult).then_inc(bct_ready, 1)
                    v.wait_ge(spe_ready, t + 1)
                    then(v, v.tensor_scalar(e2[:], e[:], 2.0, None, ALU.add), sp, n + 2)
                    then(v, v.reciprocal(r[:], e2[:]), sp, n + 3)
                    then(v, v.tensor_tensor(s[:], e[:], r[:], ALU.mult), sp, n + 4)
                    then(v, v.tensor_tensor(s2[:], s[:], s[:], ALU.mult), sp, n + 5)
                    then(v, v.tensor_scalar(poly[:], s2[:], 2.0 / 15, None, ALU.mult), sp, n + 6)
                    for i, odd in enumerate((13, 11, 9, 7, 5, 3)):
                        then(v, v.scalar_tensor_tensor(poly[:], poly[:], 2.0 / odd, s2[:], ALU.add, ALU.mult), sp, n + 7 + i)
                    then(v, v.scalar_tensor_tensor(s[:], poly[:], 2.0, s[:], ALU.add, ALU.mult), sp, n + 13)
                    then(v, v.scalar_tensor_tensor(dt[:], u[:], 0.0, s[:], ALU.max, ALU.add), sp, n + 14)
                    v.tensor_tensor(am[:], dt[:], neg_a[:], ALU.mult).then_inc(dt_ready, 1)
                    v.wait_ge(G_ps, t + 1)
                    v.tensor_tensor(gm[:], B[7][:, 0:2 * P].rearrange("p (a n) -> p a n", a=2), masks, ALU.mult).then_inc(gm_ready, 1)
                    v.wait_ge(fcd_ps, t + 1)
                    v.tensor_tensor(g8[:], B[4][:, 0:HEADS2], w["skip"], ALU.add).then_inc(g8_ready, 1)
                    v.wait_ge(gm_ready, t + 1)
                    if more:
                        fx_piece(t + 1, 1 - par, 2)
                        fx_piece(t + 1, 1 - par, 3)

                    def weigh(q):
                        v.wait_ge(D_exp, t * 4 + q + 1)
                        v.tensor_tensor(decay[q][:], B[6 + q % 2][:].rearrange("p (a n) -> p a n", a=4),
                                        gm[:, q // 2, None, :].broadcast_to([P, 4, P]), ALU.mult).then_inc(decay_ready, 1)
                    if more:
                        soft_a(t + 1, 0)
                    weigh(0)
                    weigh(1)
                    if more:
                        soft_b(t + 1, 1 - par, 0)
                        soft_a(t + 1, 1)
                    weigh(2)
                    weigh(3)
                    if more:
                        soft_b(t + 1, 1 - par, 1)
                    v.wait_ge(y_ps, t + 1)
                    v.wait_ge(term_ready, t + 1)
                    then(v, v.tensor_tensor(B[5][:], B[5][:], term[:], ALU.add), y_sum, t + 1)
                    v.scalar_tensor_tensor(yg[:], B[5][:], 0.5, sz[:], ALU.mult, ALU.mult).then_inc(yg_ready, 1)
                    if more:
                        soft_a(t + 1, 2)
                    v.wait_ge(ms_ready, t + 1)
                    v.tensor_scalar(ve[:], ms[:], 1.0 / IN2, 1e-5, ALU.mult, ALU.add).then_inc(ve_ready, 1)
                    if more:
                        soft_b(t + 1, 1 - par, 2)
                    v.wait_ge(rstd_ready, t + 1)
                    v.scalar_tensor_tensor(yn[:], yg[:], rstd[:], w["norm_w"], ALU.mult, ALU.mult).then_inc(yn_ready, 1)
                    if more:
                        soft_a(t + 1, 3)
                        soft_b(t + 1, 1 - par, 3)
                    v.wait_ge(fin_ps, t + 1)
                    then(v, v.tensor_tensor(c.xs[:], tiles4(B[4][:]), c.X[:, ds(t * TT, TT), :], ALU.add), x_sum, t + 1)
                    then(v, v.tensor_tensor(c.xs[:], c.xs[:], w["out_b"][:, None, :].broadcast_to([P, TT, D]), ALU.add), x_done, t + 1)
                    finish_rows(v, c, stats, t)
                every_turn(v, turn)

            @block.scalar
            def _(a):
                a.activation(neg_a[:], w["a_log"], ACT.Exp).then_inc(a_exp, 1)

                def evac_hT(t):
                    a.wait_ge(hT_ps, t + 1)
                    a.activation(hT[:], B[0][:], ACT.Copy).then_inc(hT_ready, 1)

                def xm_piece(t, j):
                    a.wait_ge(xm_ps, t * KC + j + 1)
                    a.activation(xmT[:, j, :], B[2][:], ACT.Identity, bias=w["b_x"][:, j:j + 1]).then_inc(xm_ready, 1)

                def exp_piece(t, k):
                    a.wait_ge(lg_ready, t * TT + k + 1)
                    a.activation(B[3][:], B[3][:], ACT.Exp).then_inc(lg_exp, 1)

                def swT_piece(t, k):
                    a.wait_ge(swT_ps, t * TT + k + 1)
                    a.activation(swT[:, k], B[0][:].rearrange("p (j n) -> p j n", j=KC), ACT.Copy).then_inc(swT_ready, 1)

                evac_hT(0)
                for j in range(KC):
                    xm_piece(0, j)
                for k in range(TT):
                    exp_piece(0, k)

                def turn(t, par, first, last):
                    more = not last
                    if more:
                        evac_hT(t + 1)
                    swT_piece(t, 0)
                    a.wait_ge(z_ps, t + 1)
                    a.activation(tz[:], B[4][:], ACT.Tanh, scale=0.5).then_inc(tz_ready, 1)
                    a.wait_ge(x_ps, t + 1)
                    a.activation(xpad[:, :, :, TAPS2 - 1:], B[5][:].rearrange("p (k a s) -> p k a s", k=KC, a=2), ACT.Copy).then_inc(xpad_ready, 1)
                    a.wait_ge(bcd_ps, t + 1)
                    a.activation(bcpad[:, :, :, TAPS2 - 1:], B[6][0:NS2, 0:2 * P].rearrange("p (k a s) -> p k a s", k=2, a=2), ACT.Copy)
                    a.activation(dtr[:], B[6][:, 2 * P:2 * P + 2 * HEADS2], ACT.Copy).then_inc(bcd_ready, 1)
                    if more:
                        xm_piece(t + 1, 0)
                        xm_piece(t + 1, 1)
                    a.wait_ge(xc_ready, t + 1)
                    a.activation(tx[:], xc[:].rearrange("p k a s -> p (k a s)"), ACT.Tanh).then_inc(tx_ready, 1)
                    a.wait_ge(bc_ready, t + 1)
                    a.activation(tbc[:], bc[:].rearrange("p b a s -> p (b a s)"), ACT.Tanh).then_inc(tbc_ready, 1)
                    a.wait_ge(spm_ready, t + 1)
                    a.activation(e[:], m[:], ACT.Exp).then_inc(spe_ready, 1)
                    a.wait_ge(xt_ps, t + 1)
                    a.activation(xtok[:], B[5][:], ACT.Copy).then_inc(xtok_ready, 1)
                    if more:
                        xm_piece(t + 1, 2)
                        xm_piece(t + 1, 3)
                        exp_piece(t + 1, 0)
                    swT_piece(t, 1)

                    def decay_exp(q):
                        a.wait_ge(D_ps, t * 4 + q + 1)
                        a.activation(B[6 + q % 2][:], B[6 + q % 2][:], ACT.Exp).then_inc(D_exp, 1)
                    decay_exp(0)
                    decay_exp(1)
                    if more:
                        exp_piece(t + 1, 1)
                    decay_exp(2)
                    decay_exp(3)
                    swT_piece(t, 2)
                    a.wait_ge(yg_ready, t + 1)
                    a.activation(tx[:], yg[:], ACT.Square, accum_out=ms[:]).then_inc(ms_ready, 1)
                    if more:
                        exp_piece(t + 1, 2)
                    swT_piece(t, 3)
                    a.wait_ge(yT_ps, t + 1)
                    a.activation(ygT[:].rearrange("p k n -> p (k n)"), B[4][:], ACT.Copy).then_inc(ygT_ready, 1)
                    if more:
                        exp_piece(t + 1, 3)
                    a.wait_ge(ot_ps, t + 1)
                    for hh in range(2):
                        rows_ = slice(hh * HD2, (hh + 1) * HD2)
                        ins = a.activation(otT[rows_, :, :, hh * SL:(hh + 1) * SL],
                                           B[5][rows_, :].rearrange("p (k a s) -> p k a s", k=KC, a=2), ACT.Copy)
                    ins.then_inc(otT_ready, 1)
                    for g in range(2):
                        a.wait_ge(pm_ps, t * 2 + g + 1)
                        a.activation(pm[:, g].rearrange("p k d -> p (k d)"), B[6 + g][:], ACT.Copy).then_inc(pm_ready, 1)
                every_turn(a, turn)

            @block.tensor
            def _(pe):
                mm = pe.matmul

                def to_features(t):
                    pe.wait_ge(h_ready, t + 1)
                    wait_past(pe, swT_ready, t * TT - TT)
                    for k in range(TT):
                        ins = pe.transpose(B[0][:, k * P:(k + 1) * P], h[:, k, :], c.ident[:])
                    ins.then_inc(hT_ps, 1)

                def fx_piece(t, k):
                    pe.wait_ge(hT_ready, t + 1)
                    wait_past(pe, fx_ready, t * TT + k)
                    mm(B[1][:], hT[:, k * P:(k + 1) * P], w["w_fx"], start=True, stop=True).then_inc(fx_ps, 1)

                def xm_piece(t, j):
                    wait_past(pe, xm_ready, t * KC + j)
                    mm(B[2][:], w["w_x"][:, j * P:(j + 1) * P], hT[:], start=True, stop=True).then_inc(xm_ps, 1)

                def lg_piece(t, k):
                    pe.wait_ge(xm_ready, t * KC + KC)
                    wait_past(pe, sw_ready, t * TT + k)
                    for j in range(KC):
                        ins = mm(B[3][:, j * P:(j + 1) * P], xmT[:, j, k * P:(k + 1) * P], slice_w[:, j, :], start=True, stop=True)
                    ins.then_inc(lg_ps, 1)

                def swT_piece(t, par, k, hT_turn):
                    if k == 0:
                        pe.wait_ge(hT_ready, hT_turn)
                    wait_past(pe, swT_ready, t * TT + k)
                    for j in range(KC):
                        ins = pe.transpose(B[0][:, j * P:(j + 1) * P], sw[par][:, k, j * P:(j + 1) * P], c.ident[:])
                    ins.then_inc(swT_ps, 1)

                pe.wait_ge(setup, 3)
                to_features(0)
                for k in range(TT):
                    fx_piece(0, k)
                    xm_piece(0, k)
                for k in range(TT):
                    lg_piece(0, k)

                def turn(t, par, first, last):
                    more = not last
                    pe.wait_ge(sw_ready, t * TT + TT)
                    pe.wait_ge(fx_ready, t * TT + TT)
                    wait_past(pe, x_sum, t)
                    for g in range(2):
                        for j in range(KC):
                            for k in range(2):
                                mm(B[4 + 2 * g][:, j * P:(j + 1) * P], fx[par][:, 2 * g + k, j * P:(j + 1) * P],
                                   sw[par][:, 2 * g + k, j * P:(j + 1) * P], start=(k == 0), stop=(k == 1))
                        for k in range(2):
                            ins = mm(B[5 + 2 * g][:], ones[:], sw[par][:, 2 * g + k, :], start=(k == 0), stop=(k == 1))
                        ins.then_inc(st_ps, 1)
                    if more:
                        to_features(t + 1)
                    swT_piece(t, par, 0, t + 2 if more else t + 1)
                    pe.wait_ge(stT_ready, t * 2 + 2)

                    def tokens(ap):
                        return ap.rearrange("p a s -> p (a s)")
                    for k in range(KC):
                        ins = mm(B[4][:], tokens(stT[:, k]), in_w[:, k, 0:IN2], start=(k == 0), stop=(k == KC - 1))
                    ins.then_inc(z_ps, 1)
                    for j in range(KC):
                        for k in range(KC):
                            ins = mm(B[5][:, j * P:(j + 1) * P], in_w[:, k, IN2 + j * P:IN2 + (j + 1) * P], tokens(stT[:, k]),
                                     start=(k == 0), stop=(k == KC - 1))
                    ins.then_inc(x_ps, 1)
                    for j in range(2):
                        for k in range(KC):
                            mm(B[6][0:NS2, j * P:(j + 1) * P], in_w[:, k, 2 * IN2 + j * NS2:2 * IN2 + (j + 1) * NS2], tokens(stT[:, k]),
                               start=(k == 0), stop=(k == KC - 1))
                    for k in range(KC):
                        ins = mm(B[6][:, 2 * P:2 * P + 2 * HEADS2], tokens(stT[:, k]), in_w[:, k, 2 * IN2 + 2 * NS2:PROJ2],
                                 start=(k == 0), stop=(k == KC - 1))
                    ins.then_inc(bcd_ps, 1)
                    if more:
                        for k in range(2):
                            fx_piece(t + 1, k)
                            xm_piece(t + 1, k)
                    pe.wait_ge(bct_ready, t + 1)
                    for d in range(2):
                        ins = mm(B[7][:, d * P:(d + 1) * P], Bt[:], Cpad[:, 2 * d:2 * d + P], start=True, stop=True)
                    ins.then_inc(G_ps, 1)
                    pe.wait_ge(xT_ready, t + 1)
                    for k in range(KC):
                        ins = pe.transpose(B[5][:, k * P:(k + 1) * P], xT[:, k, :], c.ident[:])
                    ins.then_inc(xt_ps, 1)
                    pe.wait_ge(sz_ready, t + 1)
                    for k in range(KC):
                        ins = mm(B[4][:, 0:HEADS2], xT[:, k, :], fcd[:, k, :], start=(k == 0), stop=(k == KC - 1))
                    ins.then_inc(fcd_ps, 1)
                    if more:
                        for k in range(2, 4):
                            fx_piece(t + 1, k)
                            xm_piece(t + 1, k)
                        lg_piece(t + 1, 0)
                    swT_piece(t, par, 1, None)

                    def decays(q):
                        d = q // 2
                        pe.wait_ge(a_run_ready, t * 2 + d + 1)
                        if q == 0:
                            pe.wait_ge(gm_ready, t + 1)
                        if q >= 2:
                            pe.wait_ge(decay_ready, t * 4 + q - 1)
                        mm(B[6 + q % 2][:], masks[:, 1 - d, :], a_run[d][:, (q % 2) * 4:(q % 2) * 4 + 4, :].rearrange("p a n -> p (a n)"),
                           start=True, stop=True).then_inc(D_ps, 1)
                    decays(0)
                    decays(1)
                    if more:
                        lg_piece(t + 1, 1)
                    decays(2)
                    decays(3)
                    swT_piece(t, par, 2, None)
                    pe.wait_ge(decay_ready, t * 4 + 4)
                    pe.wait_ge(xdt_ready, t * 2 + 2)
                    for hd in range(HEADS2):
                        for d in range(2):
                            ins = mm(B[5][:, hd * HD2:(hd + 1) * HD2], decay[2 * d + hd // 4][:, hd % 4, :],
                                     xdt[d][:, hd * HD2:(hd + 1) * HD2], start=(d == 0), stop=(d == 1))
                    ins.then_inc(y_ps, 1)
                    if more:
                        lg_piece(t + 1, 2)
                    swT_piece(t, par, 3, None)
                    pe.wait_ge(yn_ready, t + 1)
                    pe.wait_ge(g8_ready, t + 1)
                    for k in range(KC):
                        ins = pe.transpose(B[4][:, k * P:(k + 1) * P], yn[:, k * P:(k + 1) * P], c.ident[:])
                    ins.then_inc(yT_ps, 1)
                    if more:
                        lg_piece(t + 1, 3)
                    pe.wait_ge(ygT_ready, t + 1)
                    for j in range(KC):
                        for k in range(KC):
                            ins = mm(B[5][:, j * P:(j + 1) * P], hy_out[:, k, j * P:(j + 1) * P], ygT[:, k, :],
                                     start=(k == 0), stop=(k == KC - 1))
                    ins.then_inc(ot_ps, 1)
                    pe.wait_ge(otT_ready, t + 1)
                    for g in range(2):
                        for j in range(KC):
                            ins = mm(B[6 + g][:, j * P:(j + 1) * P], otT[:, j, g, :], out_w[:, j, :], start=True, stop=True)
                        ins.then_inc(pm_ps, 1)
                    pe.wait_ge(swT_ready, t * TT + TT)
                    for k in range(TT):
                        pe.wait_ge(pm_ready, t * 2 + k // 2 + 1)
                        for j in range(KC):
                            ins = mm(B[4][:, k * P:(k + 1) * P], swT[:, k, j, :], pm[:, k // 2, j, :], start=(j == 0), stop=(j == KC - 1))
                    ins.then_inc(fin_ps, 1)
                every_turn(pe, turn)


HD_G, HD_A = 16, 32
LAYOUT["gnn3"] = Layout(wq=(P, D), wk=(P, D), wv=(P, D), qmask=(P, 8), sel=(P, P), wo=(P, 2 * D), bo=(P, D))
LAYOUT["att3"] = Layout(ln1=(P, 1), wq=(P, D), wq_rot=(P, D), wk=(P, D), wk_rot=(P, D), wv=(P, D), cos=(P, NODES),
                        sin=(P, NODES), qmask=(P, 4), far=(P, 384), wo=(P, D))


def phase_attention(nc, c, name):
    L = LAYOUT[name]
    W = c.block[name]
    w = {n: L.view(W, n) for n in L.at}
    B = c.bank
    causal = name == "att3"
    NH = 4 if causal else 8
    U = 2 * NH
    SPAN = [(0, 128), (128, 256)] if causal else [(0, 256), (256, 256)]
    BLOCKS = [(0, 0, 0), (1, 0, 128), (1, 1, 256)] if causal else [(0, 0, 0), (1, 0, 128), (0, 1, 256), (1, 1, 384)]
    WIDTH = 384 if causal else 512
    SCORE_BANKS = [B[2], B[3], B[5]]
    bank_of = [u % 3 for u in range(U)]
    if U == 16:
        bank_of[15] = 1
    back = []
    for u in range(U):
        k = 1
        while bank_of[(u - k) % U] != bank_of[u]:
            k += 1
        back.append(k)
    LAG_T, LAG_PV = 2, 3
    if causal:
        AT = dict(evac=2, norm_o=3, final=4, rows=4, front_n=4, front_h=5, t=5, hT=5, q=6, rope_q=6, k=7, rope_k=7, v=7, vevac=7)
    else:
        AT = dict(evac=2, sel=4, norm_o=5, final=6, rows=7, front_n=8, t=9, hT=9, q=10, k=11, v=15)
    with ExitStack() as ctx:
        def sb(n, shape, dt=F32):
            return ctx.enter_context(nc.sbuf_tensor(f"{name}_{n}", shape, dt))

        def sem(n):
            return c.sem(f"{name}_{n}")
        u_ = [sb(f"u{i}", [P, TT, D]) for i in range(2 if causal else 1)]
        h = sb("h", [P, TT, D]) if causal else u_[0]
        hT = sb("hT", [P, TURN])
        qm = [sb(f"qm{i}", [P, NH, TURN]) for i in range(2)]
        kT = [sb(f"kT{i}", [P, TURN]) for i in range(2)]
        VW = 32
        vv = [sb(f"v{i}", [P, TT, NH, VW]) for i in range(2)]
        low = [sb(f"low{u}", [P, 2]) for u in range(4)]
        prob = [sb(f"prob{u}", [P, 512]) for u in range(4)]
        probT = [sb(f"probT{u}", [P, 512]) for u in range(2)]
        if causal:
            ones, t1, qk = sb("ones", [P, VW]), sb("t1", [P, TURN]), sb("qk", [P, TURN])
            bn2, mv2, ve2, rs2 = sb("bn2", [P, TT, 6]), sb("mv2", [P, TT, 2]), sb("ve2", [P, TT]), sb("rs2", [P, TT])
            rsum, on = sb("rsum", [P, TURN]), [sb("on", [P, TURN])]
        else:
            nla = [sb(f"nla{i}", [P, 4, NODES]) for i in range(2)]
            tiny, minus1 = sb("tiny", [P, 1]), sb("minus1", [P, 1])
            oe, on = ([sb(f"{n}{i}", [P, TURN]) for i in range(2)] for n in ("oe", "on"))

        (fill, h_ready, hT_ps, hT_ready, q_ps, q_ready, k_ps, k_ready, v_ps, v_ready, sc_ps, low_ready, exp_ready, pt_ps,
         pt_ready, pv_ps, on_ready, fin_ps, x_sum, x_done, stats) = (sem(n) for n in (
             "fill h_ready hT_ps hT_ready q_ps q_ready k_ps k_ready v_ps v_ready sc_ps low_ready exp_ready pt_ps "
             "pt_ready pv_ps on_ready fin_ps x_sum x_done stats").split())
        if causal:
            (rms, ve2_ready, rs2_ready, rope, recip_done, o_free) = (sem(n) for n in "rms ve2_ready rs2_ready rope recip_done o_free".split())
        else:
            adj_ready = [sem(f"adj_ready{i}") for i in range(2)]
            (minus1_ready, log_ready, nla_ready, oe0_ready, oe1_ready, sum_ps, recip_done) = (sem(n) for n in
                "minus1_ready log_ready nla_ready oe0_ready oe1_ready sum_ps recip_done".split())

        def lagged(t, u, lag, first, do):
            if u >= lag:
                do(t, u - lag)
            elif not first:
                do(t - 1, u - lag + U)

        with nc.Block() as block:
            @block.sync
            def _(sp):
                if not causal:
                    def load(t, par, first, last):
                        if not first:
                            wait_past(sp, low_ready, (t - 1) * U)
                        sp.dma_start(nla[par][:], c.adj[t]).then_inc(adj_ready[par], 16)
                    every_turn(sp, load)

            @block.gpsimd
            def _(g):
                def front(t, par):
                    if causal:
                        g.wait_ge(ve2_ready, t + 1)
                        g.tensor_tensor(rs2[:], ve2[:], c.minus_half[:, 0:TT], ALU.pow).then_inc(rs2_ready, 1)
                    else:
                        g.wait_ge(log_ready, t + 1)
                        g.tensor_tensor(nla[par][:], nla[par][:], minus1[:, 0:1, None].broadcast_to([P, 4, NODES]),
                                        ALU.mult).then_inc(nla_ready, 1)
                if not causal:
                    g.memset(minus1[:], -1.0).then_inc(minus1_ready, 1)
                    g.wait_ge(minus1_ready, 1)
                front(0, 0)

                def turn(t, par, first, last):
                    if not last:
                        front(t + 1, 1 - par)
                every_turn(g, turn)

            @block.vector
            def _(v):
                if causal:
                    v.memset(ones[:], 1.0).then_inc(fill, 1)
                else:
                    v.memset(tiny[:], 1e-6)
                    v.memset(vv[0][:, :, :, HD_G:], 1.0)
                    v.memset(vv[1][:, :, :, HD_G:], 1.0).then_inc(fill, 1)

                def front_n(t, par):
                    if not causal:
                        wait_past(v, hT_ps, t)
                        normalise(v, c, t, h).then_inc(h_ready, 1)
                        return
                    then(v, normalise(v, c, t, u_[par]), rms, t * 3 + 1)
                    for k in range(TT):
                        ins = v.bn_stats(bn2[:, k, :], u_[par][:, k, :])
                    then(v, ins, rms, t * 3 + 2)
                    hold(v, c)
                    for k in range(TT):
                        ins = v.bn_aggr(mv2[:, k, :], bn2[:, k, :])
                    then(v, ins, rms, t * 3 + 3)
                    mean_square(v, ve2, mv2, rms2, t, ve2_ready)

                def front_h(t, par):
                    v.wait_ge(rs2_ready, t + 1)
                    wait_past(v, hT_ps, t)
                    for k in range(TT):
                        ins = v.tensor_scalar(h[:, k, :], u_[par][:, k, :], rs2[:, k:k + 1], None, ALU.mult)
                    ins.then_inc(h_ready, 1)

                def rope_into(t, n, ps, done, out):
                    v.wait_ge(ps, t + 1)

                    def two(ap):
                        return ap.rearrange("p (g n) -> p g n", g=2)
                    wide = [w[x][:, None, :].broadcast_to([P, 2, NODES]) for x in ("cos", "sin")]
                    v.tensor_tensor(two(t1[:]), two(B[1][:]), wide[0], ALU.mult)
                    then(v, v.tensor_tensor(two(B[0][:]), two(B[0][:]), wide[1], ALU.mult), rope, n + 1)
                    return v.tensor_tensor(out[:], B[0][:], t1[:], ALU.add)

                def rope_q(t, par):
                    then(v, rope_into(t, t * 3, q_ps, None, qk), rope, t * 3 + 2)
                    for i in range(NH):
                        ins = v.tensor_scalar(qm[par][:, i, :], qk[:], w["qmask"][:, i:i + 1], None, ALU.mult)
                    ins.then_inc(q_ready, 1)

                def rope_k(t, par):
                    rope_into(t, t * 3 + 2, k_ps, None, kT[par]).then_inc(k_ready, 1)

                def scores_low(t, par, u):
                    n, g = t * U + u, u // NH
                    v.wait_ge(sc_ps, n + 1)
                    hold(v, c, 2 + u % 4)
                    bank = SCORE_BANKS[bank_of[u]]
                    for qt, (c0, keys) in enumerate(SPAN):
                        blk = bank[:, c0:c0 + keys]
                        other = w["far"][:, c0:c0 + keys] if causal else nla[par][:, 2 * g + qt, :]
                        ins = v.tensor_tensor_reduce(blk, blk, other, 1.0, FLT_MAX, ALU.add, ALU.min, low[u % 4][:, qt:qt + 1])
                    ins.then_inc(low_ready, 1)

                def evac_T(t, u):
                    n = t * U + u
                    v.wait_ge(pt_ps, n + 1)
                    wait_past(v, pv_ps, n - 1)
                    v.tensor_copy(probT[u % 2][:, 0:WIDTH], B[4][:, 0:WIDTH]).then_inc(pt_ready, 1)

                def norm_o(t, par):
                    if causal:
                        v.wait_ge(pv_ps, (t + 1) * U)
                        then(v, v.reciprocal(rsum[:], B[7][:]), recip_done, t + 1)
                        v.tensor_tensor(on[0][:], B[6][:], rsum[:], ALU.mult).then_inc(on_ready, 1)
                    else:
                        v.wait_ge(sum_ps, t + 1)
                        v.reciprocal(B[0][:], B[0][:])
                        then(v, v.reciprocal(B[1][:], B[1][:]), recip_done, t + 1)
                        v.tensor_tensor(on[0][:], B[0][:], oe[0][:], ALU.mult)
                        v.tensor_tensor(on[1][:], B[1][:], oe[1][:], ALU.mult).then_inc(on_ready, 1)

                def new_rows(t, par):
                    v.wait_ge(fin_ps, t + 1)
                    rows_ = ds(t * TT, TT)
                    if causal:
                        then(v, v.tensor_tensor(c.xs[:], tiles4(B[0][:]), u_[par][:], ALU.add), x_sum, t + 1)
                        v.tensor_tensor(c.X[:, rows_, :], c.X[:, rows_, :], c.xs[:], ALU.add)
                        v.tensor_scalar(c.X1[:, rows_, :], c.xs[:], 1.0, None, ALU.mult)
                        finish_rows(v, c, stats, t, store=False)
                    else:
                        then(v, v.tensor_tensor(c.xs[:], tiles4(B[0][:]), c.X[:, rows_, :], ALU.add), x_sum, t + 1)
                        then(v, v.tensor_tensor(c.xs[:], c.xs[:], w["bo"][:, None, :].broadcast_to([P, TT, D]), ALU.add), x_done, t + 1)
                        finish_rows(v, c, stats, t)

                rms2 = sem("rms2") if causal else None
                front_n(0, 0)
                if causal:
                    front_h(0, 0)
                    rope_q(0, 0)
                    rope_k(0, 0)

                def tail(t, par, u):
                    if u == AT["evac"] and not causal:
                        v.wait_ge(pv_ps, (t + 1) * U)
                        v.tensor_copy(oe[1][:], B[7][:]).then_inc(oe1_ready, 1)
                    if u == AT["norm_o"]:
                        norm_o(t, par)
                    if u == AT["rows"]:
                        new_rows(t, par)

                def turn(t, par, first, last):
                    for u in range(U):
                        if not causal and u == 0:
                            v.wait_ge(nla_ready, t + 1)
                        scores_low(t, par, u)
                        lagged(t, u, LAG_T, first, evac_T)
                        if not first:
                            tail(t - 1, 1 - par, u)
                        if not last:
                            if u == AT["front_n"]:
                                front_n(t + 1, 1 - par)
                            if causal and u == AT["front_h"]:
                                front_h(t + 1, 1 - par)
                            if causal and u == AT["rope_q"]:
                                rope_q(t + 1, 1 - par)
                            if causal and u == AT["rope_k"]:
                                rope_k(t + 1, 1 - par)
                every_turn(v, turn)
                for u in range(U - LAG_T, U):
                    evac_T(TURNS - 1, u)
                for u in range(U):
                    tail(TURNS - 1, 1, u)

            @block.scalar
            def _(a):
                def log_adj(t, par):
                    a.wait_ge(adj_ready[par], 8 * (t - par) + 16)
                    a.activation(nla[par][:], nla[par][:], ACT.Ln, bias=tiny[:]).then_inc(log_ready, 1)

                def evac_hT(t, par):
                    a.wait_ge(hT_ps, t + 1)
                    if causal:
                        a.activation(hT[:], B[0][:], ACT.Copy, scale=w["ln1"]).then_inc(hT_ready, 1)
                    else:
                        a.activation(hT[:], B[0][:], ACT.Copy).then_inc(hT_ready, 1)

                def evac_q(t, par, i):
                    a.wait_ge(q_ps, t + 1)
                    a.activation(qm[par][:, i, :], B[1][:], ACT.Copy, scale=w["qmask"][:, i:i + 1]).then_inc(q_ready, 1)

                def evac_k(t, par):
                    a.wait_ge(k_ps, t + 1)
                    a.activation(kT[par][:], B[0][:], ACT.Copy).then_inc(k_ready, 1)

                def evac_v(t, par):
                    a.wait_ge(v_ps, t + 1)
                    width = VW if causal else HD_G
                    a.activation(vv[par][:, :, :, 0:width], B[1][:].rearrange("p (k i d) -> p k i d", k=TT, i=NH), ACT.Copy).then_inc(v_ready, 1)

                def exp(t, u):
                    n = t * U + u
                    a.wait_ge(low_ready, n + 1)
                    wait_past(a, pt_ps, n - 3)
                    bank = SCORE_BANKS[bank_of[u]]
                    for qt, (c0, keys) in enumerate(SPAN):
                        ins = a.activation(prob[u % 4][:, c0:c0 + keys], bank[:, c0:c0 + keys], ACT.Exp,
                                           bias=low[u % 4][:, qt:qt + 1], scale=-1.0)
                    ins.then_inc(exp_ready, 1)

                a.wait_ge(fill, 1)
                if not causal:
                    log_adj(0, 0)
                evac_hT(0, 0)
                if not causal:
                    for i in range(NH):
                        evac_q(0, 0, i)
                    evac_k(0, 0)
                evac_v(0, 0)

                def turn(t, par, first, last):
                    for u in range(U):
                        exp(t, u)
                        if not causal and not first and u == AT["evac"]:
                            a.wait_ge(pv_ps, t * U)
                            a.activation(oe[0][:], B[6][:], ACT.Copy).then_inc(oe0_ready, 1)
                        if not last:
                            if not causal:
                                if u == AT["front_n"]:
                                    log_adj(t + 1, 1 - par)
                                if AT["k"] <= u < AT["k"] + NH // 2:
                                    evac_q(t + 1, 1 - par, 2 * (u - AT["k"]))
                                    evac_q(t + 1, 1 - par, 2 * (u - AT["k"]) + 1)
                                if u == AT["k"] + NH // 2 - 1:
                                    evac_k(t + 1, 1 - par)
                            if u == AT["hT"]:
                                evac_hT(t + 1, 1 - par)
                            if u == AT["v"]:
                                evac_v(t + 1, 1 - par)
                every_turn(a, turn)
                if not causal:
                    a.wait_ge(pv_ps, TURNS * U)
                    a.activation(oe[0][:], B[6][:], ACT.Copy).then_inc(oe0_ready, 1)

            @block.tensor
            def _(pe):
                mm = pe.matmul
                QN = 1 if causal else NH

                def to_features(t):
                    pe.wait_ge(h_ready, t + 1)
                    wait_past(pe, x_sum, t - 1)
                    for k in range(TT):
                        ins = pe.transpose(B[0][:, k * P:(k + 1) * P], h[:, k, :], c.ident[:])
                    ins.then_inc(hT_ps, 1)

                def q_proj(t):
                    pe.wait_ge(hT_ready, t + 1)
                    wait_past(pe, v_ready, t)
                    if not causal:
                        wait_past(pe, on_ready, t - 1)
                    ins = mm(B[1][:], w["wq"], hT[:], start=True, stop=True)
                    if causal:
                        ins = mm(B[0][:], w["wq_rot"], hT[:], start=True, stop=True)
                    ins.then_inc(q_ps, 1)

                def k_proj(t):
                    if causal:
                        pe.wait_ge(q_ready, t + 1)
                        mm(B[1][:], w["wk"], hT[:], start=True, stop=True)
                        ins = mm(B[0][:], w["wk_rot"], hT[:], start=True, stop=True)
                    else:
                        ins = mm(B[0][:], w["wk"], hT[:], start=True, stop=True)
                    ins.then_inc(k_ps, 1)

                def v_proj(t):
                    if causal:
                        pe.wait_ge(k_ready, t + 1)
                    else:
                        pe.wait_ge(q_ready, t * NH + NH)
                    for k in range(TT):
                        ins = mm(B[1][:, k * P:(k + 1) * P], hT[:, k * P:(k + 1) * P], w["wv"], start=True, stop=True)
                    ins.then_inc(v_ps, 1)

                def scores(t, par, u):
                    n, g, i = t * U + u, u // NH, u % NH
                    if u == 0:
                        pe.wait_ge(q_ready, (t + 1) * QN)
                        pe.wait_ge(k_ready, t + 1)
                    wait_past(pe, exp_ready, n - back[u] + 1)
                    for qt, (c0, keys) in enumerate(SPAN):
                        q0 = g * NODES + qt * P
                        ins = mm(SCORE_BANKS[bank_of[u]][:, c0:c0 + keys], qm[par][:, i, q0:q0 + P],
                                 kT[par][:, g * NODES:g * NODES + keys], start=True, stop=True)
                    ins.then_inc(sc_ps, 1)

                def turn_T(t, u):
                    n = t * U + u
                    pe.wait_ge(exp_ready, n + 1)
                    wait_past(pe, pt_ready, n)
                    for qt, kt, col in BLOCKS:
                        src = SPAN[qt][0] + kt * P
                        ins = pe.transpose(B[4][:, col:col + P], prob[u % 4][:, src:src + P], c.ident[:])
                    ins.then_inc(pt_ps, 1)

                def product_v(par_of):
                    def do(t, u):
                        n, g, i = t * U + u, u // NH, u % NH
                        par = par_of(t, u)
                        pe.wait_ge(pt_ready, n + 1)
                        if u == 0:
                            pe.wait_ge(v_ready, t + 1)
                            if causal:
                                wait_past(pe, on_ready, t)
                            else:
                                wait_past(pe, oe0_ready, t)
                                wait_past(pe, oe1_ready, t)
                        q = 32 * (i % 4)
                        pT = probT[u % 2]
                        outs = [(B[6], None), (B[7], ones)] if causal else [(B[6 + i // 4], None)]
                        for bank, stat in outs:
                            for kt in range(2):
                                lhs = vv[par][:, 2 * g + kt, i, :] if stat is None else stat[:]
                                if causal and kt == 1:
                                    dst, src = bank[q:q + 32, g * NODES + P:(g + 1) * NODES], pT[:, 256:384]
                                else:
                                    dst, src = bank[q:q + 32, g * NODES:(g + 1) * NODES], pT[:, kt * 256:kt * 256 + 256]
                                ins = mm(dst, lhs, src, start=(kt == 0), stop=(kt == 1), skip_group_check=True)
                        ins.then_inc(pv_ps, 1)
                    return do

                def sums(t):
                    pe.wait_ge(oe0_ready, t + 1)
                    pe.wait_ge(oe1_ready, t + 1)
                    mm(B[0][:], w["sel"], oe[0][:], start=True, stop=True)
                    mm(B[1][:], w["sel"], oe[1][:], start=True, stop=True).then_inc(sum_ps, 1)

                def final(t):
                    pe.wait_ge(on_ready, t + 1)
                    wo = w["wo"].rearrange("p (j o) -> p j o", o=D)
                    for k in range(TT):
                        for j in range(len(on)):
                            ins = mm(B[0][:, k * P:(k + 1) * P], on[j][:, k * P:(k + 1) * P], wo[:, j, :],
                                     start=(j == 0), stop=(j == len(on) - 1))
                    ins.then_inc(fin_ps, 1)

                def tail(t, u):
                    if not causal and u == AT["sel"]:
                        sums(t)
                    if u == AT["final"]:
                        final(t)

                pe.wait_ge(fill, 1)
                to_features(0)
                q_proj(0)
                k_proj(0)
                v_proj(0)

                def turn(t, par, first, last):
                    pv = product_v(lambda tt, uu: par if tt is t else 1 - par)
                    for u in range(U):
                        scores(t, par, u)
                        lagged(t, u, LAG_T, first, turn_T)
                        lagged(t, u, LAG_PV, first, pv)
                        if not first:
                            tail(t - 1, u)
                        if not last:
                            if u == AT["t"]:
                                to_features(t + 1)
                            if u == AT["q"]:
                                q_proj(t + 1)
                            if u == AT["k"]:
                                k_proj(t + 1)
                            if u == AT["v"]:
                                v_proj(t + 1)
                every_turn(pe, turn)
                last_pv = product_v(lambda tt, uu: 1)
                for u in range(U, U + LAG_PV):
                    if u - LAG_T < U:
                        turn_T(TURNS - 1, u - LAG_T)
                    last_pv(TURNS - 1, u - LAG_PV)
                for u in range(U):
                    tail(TURNS - 1, u)


PHASES = {"gnn0": phase_gnn0, "gnn1": phase_gnn1, "gnn2": phase_gnn2,
          "ffn2": phase_ffn2,
          "gnn3": lambda nc, c: phase_attention(nc, c, "gnn3"), "att3": lambda nc, c: phase_attention(nc, c, "att3")}
PHASES.update({n: (lambda nc, c, n=n: phase_moe(nc, c, n)) for n in MOE})


def program(nc, dram, order):
    with ExitStack() as ctx:
        c = Core()
        c.order, c.dram = order, dram
        c.adjT, c.adj = (dram[n].rearrange("(t k p) n -> t p k n", p=P, k=4) for n in ("adjT", "adj"))

        def sb(name, shape, dt=F32):
            return ctx.enter_context(nc.sbuf_tensor(name, shape, dt))
        c.sem = lambda name: ctx.enter_context(nc.semaphore(name))
        c.X = sb("X", [P, TILES, D])
        c.MV, c.bn, c.mv = sb("MV", [P, TILES, 2]), sb("bn", [P, TT, 6]), sb("mv", [P, TT, 2])
        c.xs = sb("xs", [P, TT, D])
        c.tick = sb("tick", [P, 6])
        c.var_eps, c.rstd, c.shift, c.minus_half = (sb(n, [P, TILES]) for n in ("var_eps", "rstd", "shift", "minus_half"))
        c.ident = sb("ident", [P, P])
        cols = [LAYOUT[n].cols for n in order] + [0]
        size = max(cols[k] + cols[k + 1] + SPARE.get(order[k], 0) for k in range(len(order)))
        arena = sb("constants", [P, size])
        c.block = {n: arena[:, 0:cols[k]] if k % 2 == 0 else arena[:, size - cols[k]:size] for k, n in enumerate(order)}
        c.spare = {}
        for k, n in enumerate(order):
            if n in SPARE:
                low = cols[k] if k % 2 == 0 else cols[k + 1]
                c.spare[n] = arena[:, low:low + SPARE[n]]
        c.bank = [ctx.enter_context(nc.psum_tensor(f"bank{i}", [P, 512], F32)) for i in range(8)]
        c.w_ready = {n: c.sem("w_ready_" + n) for n in order}
        x_in, zeroed, ident_ready, xs_ready, stats, x_out = (
            c.sem(n) for n in ("x_in", "zeroed", "ident_ready", "xs_ready", "stats", "x_out"))
        x_tiles = dram["x"].rearrange("(t p) d -> p t d", p=P)
        out_tiles = dram["out"].rearrange("(t p) d -> p t d", p=P)

        with nc.Block() as block:
            @block.sync
            def _(sp):
                for k in range(4):
                    sp.dma_start(c.X[:, 16 * k:16 * k + 16, :], x_tiles[:, 16 * k:16 * k + 16, :]).then_inc(x_in, 16)
                    sp.wait_ge(x_in, 16 * k + 16)

            @block.gpsimd
            def _(g):
                g.memset(c.minus_half[:], -0.5)
                g.memset(c.tick[:], 0.0)
                g.memset(c.ident[:], 0.0).then_inc(zeroed, 1)
                g.wait_ge(zeroed, 1)
                g.affine_select(out=c.ident[:], in_=c.ident[:], compare_op=ALU.not_equal, fill=1.0, base=0,
                                pattern=[[-1, P]], channel_multiplier=1).then_inc(ident_ready, 1)

            @block.vector
            def _(v):
                for k in range(4):
                    v.wait_ge(x_in, 16 * k + 16)
                    with v.Fori(4 * k, 4 * k + 4) as t:
                        then(v, v.tensor_scalar(c.xs[:], c.X[:, ds(t * TT, TT), :], 1.0, None, ALU.mult),
                             xs_ready, t + 1)
                        finish_rows(v, c, stats, t)

        for k, name in enumerate(order):
            if name == "att3":
                c.X1 = sb("X1", [P, TILES, D])
            c.src = c.X1 if name == "ffn3" else c.X
            with ExitStack() as phase:
                used = []

                def sem(n):
                    used.append(phase.enter_context(nc.semaphore(n)))
                    return used[-1]
                c.sem = sem
                begin_phase(nc, c, name, order[k + 1] if k + 1 < len(order) else None)
                PHASES[name](nc, c)
                with nc.Block() as block:
                    @block.gpsimd
                    def _(g):
                        for one in used:
                            g.sem_clear(one)

        with nc.Block() as block:
            @block.sync
            def _(sp):
                for k in range(4):
                    sp.dma_start(out_tiles[:, 16 * k:16 * k + 16, :], c.X[:, 16 * k:16 * k + 16, :]).then_inc(x_out, 16)
                sp.wait_ge(x_out, 64)


def rows(a):
    return np.broadcast_to(np.reshape(a, (1, -1)), (P, np.size(a)))


def layout_arrays(inp):
    g = {k: np.asarray(v) for k, v in inp.items()}
    out = {}

    def of(prefix):
        return {k[len(prefix):]: v for k, v in g.items() if k.startswith(prefix)}
    a = of("L0_gnn_")
    out["gnn0"] = dict(
        conv1=a["conv1_w"][:, :, 0].T, conv2=a["conv2_w"].transpose(1, 2, 0), w_se=a["w_se"].T, b_se=a["b_se"],
        bn=np.stack([a[f"bn{l}_{k}"] for l in (1, 2) for k in "gbmv"], 1), w_msg=a["w_msg"].T, b_msg=rows(a["b_msg"]),
        w_ih=a["w_ih"].reshape(3, D, 2, D).transpose(3, 2, 0, 1), w_hh=a["w_hh"].reshape(3, D, D).transpose(2, 0, 1),
        b_ih=a["b_ih"].reshape(3, D).T, b_hh=a["b_hh"].reshape(3, D).T)
    for name, prefix in (("ffn0", "L0_ffn_"), ("ffn1", "L1_ffn_")):
        a, m = of(prefix), MOE[name]
        out[name] = dict(gate_w=a["gate_w"], gate_b=rows(a["gate_b"]), w1=a["w1"].transpose(1, 0, 2))
        second = a["w3"] if m.gated else a["w2"]
        out[name]["w3"] = second.reshape(m.count, len(m.chunks), P, D).transpose(2, 0, 1, 3)
        if m.gated:
            out[name]["w2"] = a["w2"].transpose(1, 0, 2)
        else:
            out[name]["b1"] = a["b1"].reshape(m.count, len(m.chunks), P).transpose(2, 0, 1)
            out[name]["b2"] = a["b2"]
    a = of("L1_gnn_")
    out["gnn1"] = dict(theta=a["theta"], w_t=a["W_t"], w_h=a["W_h"], b_t=rows(a["b_t"]))
    a = of("L2_gnn_")
    out["gnn2"] = dict(w_rel=a["W_rel"], w_root=a["W_root"], b_rel=rows(a["b_rel"]), gamma=rows(a["ln_gamma"]), beta=rows(a["ln_beta"]))
    a = of("L2_ffn_")
    diagonal = np.zeros((P, P), np.float32)
    for k in range(2):
        diagonal[k * SL:(k + 1) * SL, k * SL:(k + 1) * SL] = a["W_slice"].T

    def chunks(m):
        return m.reshape(KC, P, -1).transpose(1, 0, 2)
    i = np.arange(P)
    same = i[:, None] // SL == i[None, :] // SL
    conv, cb = a["hy_conv_w"], a["hy_conv_b"]
    out["ffn2"] = dict(
        w_fx=a["W_fx"].T, b_fx=rows(a["b_fx"]), w_x=a["W_x"].T, b_x=a["b_x"].reshape(KC, P).T, w_slice=diagonal,
        b_slice=rows(np.tile(a["b_slice"], HEADS2)), temp=rows(a["temperature"]), in_w=chunks(a["hy_in_w"].T),
        conv_x=chunks(conv[:IN2]), convb_x=cb[:IN2].reshape(KC, P).T,
        conv_bc=conv[IN2:].reshape(2, NS2, TAPS2).transpose(1, 0, 2), convb_bc=cb[IN2:].reshape(2, NS2).T,
        dt_bias=rows(np.tile(a["hy_dt_bias"], 2)), a_log=rows(np.tile(a["hy_A_log"], 2)), skip=rows(a["hy_D"]),
        fcd=chunks(a["hy_fcD_w"].T), norm_w=rows(a["hy_norm_w"]), hy_out=chunks(a["hy_out_w"].T),
        out_w=chunks(a["out_w"].T), out_b=rows(a["out_b"]),
        masks=np.stack([same & (i[:, None] < i[None, :]), same & (i[:, None] > i[None, :])], 1).astype(np.float32))
    a = of("L3_gnn_")
    i = np.arange(P)
    head = (i[:, None] // HD_G == np.arange(8)[None, :])
    sel = (i[:, None] == i[None, :] // 32 * 32 + HD_G)
    wo = np.zeros((2, 4, 32, D), np.float32)
    wo[:, :, 0:HD_G] = a["Wo"].T.reshape(2, 4, HD_G, D)
    out["gnn3"] = dict(wq=a["Wq"].T, wk=a["Wk"].T, wv=a["Wv"].T, qmask=head * np.float32(-HD_G ** -0.5),
                       sel=sel.astype(np.float32), wo=wo.reshape(2, P, D).transpose(1, 0, 2), bo=rows(a["bo"]))
    a = of("L3_ffn_")
    d = np.arange(P) % HD_A
    turned = np.arange(P) // HD_A * HD_A + (d + HD_A // 2) % HD_A
    kv = np.arange(P) // HD_A // 2 * HD_A + d
    angle = np.outer(1.0 / 10000.0 ** (np.arange(0, HD_A, 2, dtype=np.float32) / HD_A),
                     np.arange(NODES, dtype=np.float32))[d % (HD_A // 2)]
    q, k_ = np.arange(P)[:, None], np.arange(NODES)[None, :]
    far = np.concatenate([k_[:, :P] > q, k_ > q + P], 1) * np.float32(1e30)
    out["att3"] = dict(
        ln1=a["ln1_w"], wq=a["wq"].T, wq_rot=a["wq"].T[:, turned], wk=a["wk"].T[:, kv], wk_rot=a["wk"].T[:, kv[turned]],
        wv=a["wv"].T[:, kv], cos=np.cos(angle), sin=np.sin(angle) * np.where(d < HD_A // 2, -1, 1)[:, None],
        qmask=(np.arange(P)[:, None] // HD_A == np.arange(4)[None, :]) * np.float32(-HD_A ** -0.5), far=far, wo=a["wo"].T)
    m = MOE["ffn3"]
    second = np.zeros((m.count, 3 * P, D), np.float32)
    second[:, 0:m.hidden] = a["w2"].transpose(0, 2, 1)
    out["ffn3"] = dict(ln2=a["ln2_w"], gate_w=a["router_w"].T, w1=a["w1"].transpose(2, 0, 1), w2=a["w3"].transpose(2, 0, 1),
                       w3=second.reshape(m.count, 3, P, D).transpose(2, 0, 1, 3))
    return {n: LAYOUT[n].pack(out[n]) for n in out}


ORDER = ["gnn0", "ffn0", "gnn1", "ffn1", "gnn2", "ffn2", "gnn3", "att3", "ffn3"]


def kernel(**inputs):
    import concourse.bacc as _bacc
    from concourse.bass_utils import run_bass_kernel_spmd as _run

    adj = np.asarray(inputs["adj"])
    arrays = {"x": np.ascontiguousarray(np.asarray(inputs["x"]).reshape(-1, D)),
              "adj": np.ascontiguousarray(adj.reshape(-1, NODES)),
              "adjT": np.ascontiguousarray(adj.transpose(0, 2, 1).reshape(-1, NODES))}
    arrays.update(layout_arrays(inputs))
    nc = _bacc.Bacc("TRN2", target_bir_lowering=False, num_devices=1)
    dram = {n: nc.dram_tensor("in_" + n, a.shape, F32, kind="ExternalInput").ap() for n, a in arrays.items()}
    dram["out"] = nc.dram_tensor("out", (GRAPHS * NODES, D), F32, kind="ExternalOutput").ap()
    program(nc, dram, ORDER)
    r = _run(nc, [{"in_" + n: a for n, a in arrays.items()}], core_ids=[0])
    return np.reshape(r.results[0]["out"], (GRAPHS, NODES, D))
```

```python
from contextlib import ExitStack

import numpy as np

import concourse.bass as bass
from concourse import mybir

F32 = mybir.dt.float32
I32 = mybir.dt.int32
U32 = mybir.dt.uint32
ALU = mybir.AluOpType
ACT = mybir.ActivationFunctionType
AX = mybir.AxisListType
ds = bass.ds

P = 128
D = 128
GRAPHS, NODES = 32, 256
TILES = GRAPHS * NODES // P
TURN = 512
TT = TURN // P
TURNS = GRAPHS * NODES // TURN
EPS = 1e-5
RMS_EPS = 1e-6


def every_turn(eng, body, count=TURNS):
    body(0, 0, True, False)
    body(1, 1, False, False)
    with eng.Fori(2, count - 3, 2) as t:
        body(t, 0, False, False)
        body(t + 1, 1, False, False)
    body(count - 2, 0, False, False)
    body(count - 1, 1, False, True)


def then(eng, ins, sem, value):
    ins.then_inc(sem, 1)
    eng.wait_ge(sem, value)


CONV_TAPS, CONV_PAD = 17, 8


class Layout:

    def __init__(self, **fields):
        self.at, self.cols = {}, 0
        for name, (rows, cols) in fields.items():
            self.at[name] = (self.cols, rows, cols)
            self.cols += cols

    def view(self, region, name):
        c, rows, cols = self.at[name]
        return region[0:rows, c:c + cols]

    def pack(self, arrays):
        out = np.zeros((P, self.cols), np.float32)
        for name, (c, rows, cols) in self.at.items():
            out[0:rows, c:c + cols] = np.reshape(arrays[name], (rows, cols))
        return out


LAYOUT = {}
LAYOUT["gnn0"] = Layout(
    conv1=(P, D), conv2=(P, CONV_TAPS * D), w_se=(P, 3), b_se=(3, 1), bn=(P, 8),
    w_msg=(P, D), b_msg=(P, D), w_ih=(P, 6 * D), w_hh=(P, 3 * D), b_ih=(P, 3), b_hh=(P, 3))


SPARE = {"ffn2": 24 * P}


class Core:
    pass


def begin_phase(nc, c, name, nxt):
    s = {k: c.sem(f"{name}_{k}") for k in ("var_eps", "rstd", "squared")}
    k = c.order.index(name)
    with nc.Block() as block:
        @block.sync
        def _(sp):
            if k == 0:
                sp.dma_start(c.block[name], c.dram[name]).then_inc(c.w_ready[name], 16)
            if nxt:
                sp.dma_start(c.block[nxt], c.dram[nxt]).then_inc(c.w_ready[nxt], 16)
            sp.wait_ge(c.w_ready[name], 16)

        @block.vector
        def _(v):
            if name == "ffn3":
                mean_square(v, c.var_eps, c.MV, s["squared"], 0, s["var_eps"])
                v.memset(c.shift[:], 0.0)
            else:
                v.tensor_scalar(c.var_eps[:], c.MV[:, :, 1], EPS, None, ALU.add).then_inc(s["var_eps"], 1)
                v.wait_ge(s["rstd"], 1)
                v.scalar_tensor_tensor(c.shift[:], c.MV[:, :, 0], -1.0, c.rstd[:], ALU.mult, ALU.mult)

        @block.gpsimd
        def _(g):
            g.wait_ge(s["var_eps"], 1)
            g.tensor_tensor(c.rstd[:], c.var_eps[:], c.minus_half[:], ALU.pow).then_inc(s["rstd"], 1)


def normalise(v, c, turn, h):
    for k in range(TT):
        t = turn * TT + k
        ins = v.tensor_scalar(h[:, k, :], c.src[:, t, :], c.rstd[:, ds(t, 1)], c.shift[:, ds(t, 1)],
                              ALU.mult, ALU.add)
    return ins


def finish_rows(v, c, stats, turn, store=True):
    for k in range(TT):
        ins = v.bn_stats(c.bn[:, k, :], c.xs[:, k, :])
    then(v, ins, stats, turn * 2 + 1)
    if store:
        v.tensor_scalar(c.X[:, ds(turn * TT, TT), :], c.xs[:], 1.0, None, ALU.mult)
    else:
        hold(v, c)
    for k in range(TT):
        ins = v.bn_aggr(c.mv[:, k, :], c.bn[:, k, :])
    then(v, ins, stats, turn * 2 + 2)
    v.tensor_scalar(c.MV[:, ds(turn * TT, TT), :], c.mv[:], 1.0, None, ALU.mult)


def hold(v, c, cell=1):
    v.tensor_copy(c.tick[:, cell:cell + 1], c.tick[:, 0:1])


def mean_square(v, out, mv, sem, turn, done):
    then(v, v.tensor_tensor(out[:], mv[:, :, 0], mv[:, :, 0], ALU.mult), sem, turn + 1)
    v.scalar_tensor_tensor(out[:], out[:], RMS_EPS, mv[:, :, 1], ALU.add, ALU.add).then_inc(done, 1)


def wait_past(eng, sem, value):
    if not isinstance(value, int) or value > 0:
        eng.wait_ge(sem, value)


def tiles4(ap):
    return ap.rearrange("p (k d) -> p k d", k=TT)


def phase_gnn0(nc, c):
    L, W = LAYOUT["gnn0"], c.block["gnn0"]
    w = {n: L.view(W, n) for n in L.at}
    conv2 = w["conv2"].rearrange("p (k o) -> p k o", k=CONV_TAPS)
    w_ih = w["w_ih"].rearrange("p (a g o) -> p a g o", a=2, g=3)
    w_hh = w["w_hh"].rearrange("p (g o) -> p g o", g=3)
    SEG = NODES + 2 * CONV_PAD
    with ExitStack() as ctx:
        def sb(name, shape):
            return ctx.enter_context(nc.sbuf_tensor("g0_" + name, shape, F32))

        def sem(name):
            return c.sem("g0_" + name)

        h = sb("h", [P, TT, D])
        hT = [sb(f"hT{i}", [P, TURN]) for i in range(2)]
        cpad = sb("cpad", [P, 2, SEG])
        adj = [sb(f"adj{i}", [P, 4, NODES]) for i in range(2)]
        xconv = sb("xconv", [P, TURN])
        sT, s2T, sqT = sb("sT", [3, TURN]), sb("s2T", [3, TURN]), sb("sqT", [3, TURN])
        minus1 = sb("minus1", [3, P])
        nsq = sb("nsq", [P, 4])
        A = sb("A", [P, 4, NODES])
        msg = sb("msg", [P, TT, D])
        nmp = sb("nmp", [P, TURN])
        ghb, q, e, outT = (sb(n, [P, TURN]) for n in ("ghb", "q", "e", "outT"))
        bnc = sb("bnc", [P, 12])
        scale1, shift1, scale2, shift2 = (bnc[:, i:i + 1] for i in range(4))
        rz_half = sb("rz_half", [P, 2])
        B = c.bank

        consts = sem("consts"); consts_pow = sem("consts_pow"); vlink0 = sem("vlink0")
        h_ready = sem("h_ready")
        hT_ps, hT_ready = sem("hT_ps"), sem("hT_ready")
        c1_ps, c1_ready = sem("c1_ps"), sem("c1_ready")
        s_ps, s_ready, s2_ready = sem("s_ps"), sem("s_ready"), sem("s2_ready")
        msg_ps, msg_ready = sem("msg_ps"), sem("msg_ready")
        nsq_ps, nsq_ready = sem("nsq_ps"), sem("nsq_ready")
        dist_ps, exp_ready, A_ready = sem("dist_ps"), sem("exp_ready"), sem("A_ready")
        adj_ready = [sem(f"adj_ready{i}") for i in range(2)]
        c2_ps, xpre_ready, xconv_ready = sem("c2_ps"), sem("xpre_ready"), sem("xconv_ready")
        nmp_ps, nmp_ready = sem("nmp_ps"), sem("nmp_ready")
        ghn_ps, r_ps, z_ps, n_ps = sem("ghn_ps"), sem("r_ps"), sem("z_ps"), sem("n_ps")
        r_ready, z_ready, npre_ready, n_ready = sem("r_ready"), sem("z_ready"), sem("npre_ready"), sem("n_ready")
        outT_ready, out_ps, x_done = sem("outT_ready"), sem("out_ps"), sem("x_done")
        msg_biased, stats = sem("msg_biased"), sem("stats")
        r_gh, h_minus_n, z_part = sem("r_gh"), sem("h_minus_n"), sem("z_part")

        with nc.Block() as block:
            @block.sync
            def _(sp):
                def load(t, par, first, last):
                    if not first and not (isinstance(t, int) and t == 1):
                        sp.wait_ge(A_ready, t - 1)
                    sp.dma_start(adj[par][:], c.adjT[t]).then_inc(adj_ready[par], 16)
                every_turn(sp, load)

            @block.gpsimd
            def _(g):
                g.wait_ge(consts, 1)
                g.tensor_tensor(bnc[:, 6:8], bnc[:, 4:6], c.minus_half[:, 0:2], ALU.pow).then_inc(consts_pow, 1)

            @block.vector
            def _(v):
                bn = w["bn"].rearrange("p (l k) -> p l k", l=2)
                v.memset(cpad[:], 0.0)
                v.memset(minus1[:], -1.0)
                v.tensor_scalar(bnc[:, 4:6], bn[:, :, 3], EPS, None, ALU.add).then_inc(consts, 1)
                v.tensor_tensor(bnc[:, 8:11], w["b_ih"], w["b_hh"], ALU.add).then_inc(vlink0, 1)
                v.wait_ge(vlink0, 1)
                v.tensor_scalar(rz_half[:], bnc[:, 8:10], 0.5, None, ALU.mult)
                v.wait_ge(consts_pow, 1)
                v.tensor_tensor(bnc[:, 6:8], bnc[:, 6:8], bn[:, :, 0], ALU.mult).then_inc(vlink0, 1)
                v.wait_ge(vlink0, 2)
                v.tensor_copy(bnc[:, 0:3:2], bnc[:, 6:8])
                v.tensor_tensor(bnc[:, 4:6], bn[:, :, 2], bnc[:, 6:8], ALU.mult).then_inc(vlink0, 1)
                v.wait_ge(vlink0, 3)
                v.tensor_tensor(bnc[:, 1:4:2], bn[:, :, 1], bnc[:, 4:6], ALU.subtract).then_inc(consts, 1)

                normalise(v, c, 0, h).then_inc(h_ready, 1)

                def residual(t):
                    v.wait_ge(out_ps, t + 1)
                    then(v, v.tensor_tensor(c.xs[:], c.X[:, ds(t * TT, TT), :], tiles4(B[0][:]), ALU.add),
                         x_done, t + 1)
                    finish_rows(v, c, stats, t)

                def turn(t, par, first, last):
                    v.wait_ge(s_ready, t + 1)
                    v.tensor_scalar(s2T[:], sT[:], 2.0, None, ALU.mult).then_inc(s2_ready, 1)
                    v.wait_ge(msg_ps, t + 1)
                    if not first:
                        v.wait_ge(nmp_ps, t)
                    then(v, v.tensor_tensor(msg[:], tiles4(B[3][:]), w["b_msg"][:, None, :].broadcast_to([P, TT, D]),
                                            ALU.add), msg_biased, t + 1)
                    v.tensor_scalar(msg[:], msg[:], 0.0, None, ALU.max).then_inc(msg_ready, 1)
                    v.wait_ge(ghn_ps, t + 1)
                    v.tensor_scalar(ghb[:], B[4][:], w["b_hh"][:, 2:3], 0.5, ALU.add, ALU.mult)
                    if not first:
                        residual(t - 1)
                    v.wait_ge(exp_ready, t + 1)
                    v.wait_ge(adj_ready[par], 8 * (t - par) + 16)
                    for j in range(2):
                        ins = v.tensor_tensor(A[:, 2 * j:2 * j + 2, :], B[5 + j][:].rearrange("p (m n) -> p m n", m=2),
                                              adj[par][:, 2 * j:2 * j + 2, :], ALU.mult)
                    ins.then_inc(A_ready, 1)
                    if not last:
                        v.wait_ge(hT_ps, t + 1)
                        normalise(v, c, t + 1, h).then_inc(h_ready, 1)
                    v.wait_ge(c2_ps, t + 1)
                    if not first:
                        v.wait_ge(xconv_ready, t)
                    v.scalar_tensor_tensor(q[:], B[1][:], scale2, hT[par][:], ALU.mult, ALU.add).then_inc(xpre_ready, 1)
                    v.wait_ge(r_ready, t + 1)
                    v.scalar_tensor_tensor(e[:], B[5][:], 1.0, ghb[:], ALU.add, ALU.mult).then_inc(r_gh, 1)
                    v.wait_ge(r_gh, t + 1)
                    v.wait_ge(n_ps, t + 1)
                    v.tensor_tensor(e[:], B[7][:], e[:], ALU.add).then_inc(npre_ready, 1)
                    v.wait_ge(n_ready, t + 1)
                    v.scalar_tensor_tensor(outT[:], B[7][:], -1.0, hT[par][:], ALU.mult, ALU.add).then_inc(h_minus_n, 1)
                    v.wait_ge(h_minus_n, t + 1)
                    v.wait_ge(z_ready, t + 1)
                    v.scalar_tensor_tensor(outT[:], B[6][:], 1.0, outT[:], ALU.add, ALU.mult).then_inc(z_part, 1)
                    v.wait_ge(z_part, t + 1)
                    v.scalar_tensor_tensor(outT[:], outT[:], 0.5, B[7][:], ALU.mult, ALU.add).then_inc(outT_ready, 1)
                every_turn(v, turn)
                residual(TURNS - 1)

            @block.scalar
            def _(a):
                def evac_hT(t, par):
                    a.wait_ge(hT_ps, t + 1)
                    a.activation(hT[par][:], B[0][:], ACT.Copy).then_inc(hT_ready, 1)
                a.wait_ge(consts, 2)
                evac_hT(0, 0)

                def turn(t, par, first, last):
                    a.wait_ge(c1_ps, t + 1)
                    for g in range(2):
                        ins = a.activation(cpad[:, g, CONV_PAD:CONV_PAD + NODES], B[1][:, g * NODES:(g + 1) * NODES],
                                           ACT.Relu, bias=shift1, scale=scale1)
                    ins.then_inc(c1_ready, 1)
                    a.wait_ge(s_ps, t + 1)
                    a.activation(sT[:], B[2][0:3, :], ACT.Identity, bias=w["b_se"])
                    a.activation(sqT[:], B[2][0:3, :], ACT.Square, bias=w["b_se"]).then_inc(s_ready, 1)
                    a.wait_ge(nsq_ps, t + 1)
                    a.activation(nsq[:], B[2][:, 0:4], ACT.Copy).then_inc(nsq_ready, 1)
                    a.wait_ge(nsq_ready, t + 1)
                    a.wait_ge(dist_ps, t + 1)
                    for k in range(4):
                        blk = B[5 + k // 2][:, (k % 2) * NODES:(k % 2 + 1) * NODES]
                        ins = a.activation(blk, blk, ACT.Exp, bias=nsq[:, k:k + 1])
                    ins.then_inc(exp_ready, 1)
                    if not last:
                        evac_hT(t + 1, 1 - par)
                    a.wait_ge(nmp_ps, t + 1)
                    a.activation(nmp[:], B[3][:], ACT.Copy).then_inc(nmp_ready, 1)
                    a.wait_ge(xpre_ready, t + 1)
                    a.activation(xconv[:], q[:], ACT.Relu, bias=shift2).then_inc(xconv_ready, 1)
                    a.wait_ge(r_ps, t + 1)
                    a.activation(B[5][:], B[5][:], ACT.Tanh, bias=rz_half[:, 0:1], scale=0.5).then_inc(r_ready, 1)
                    a.wait_ge(z_ps, t + 1)
                    a.activation(B[6][:], B[6][:], ACT.Tanh, bias=rz_half[:, 1:2], scale=0.5).then_inc(z_ready, 1)
                    a.wait_ge(npre_ready, t + 1)
                    a.activation(B[7][:], e[:], ACT.Tanh, bias=w["b_ih"][:, 2:3]).then_inc(n_ready, 1)
                every_turn(a, turn)

            @block.tensor
            def _(pe):
                mm = pe.matmul

                def to_features(t):
                    pe.wait_ge(h_ready, t + 1)
                    for k in range(TT):
                        ins = pe.transpose(B[0][:, k * P:(k + 1) * P], h[:, k, :], c.ident[:])
                    ins.then_inc(hT_ps, 1)

                def to_tokens(t):
                    pe.wait_ge(outT_ready, t + 1)
                    for k in range(TT):
                        ins = pe.transpose(B[0][:, k * P:(k + 1) * P], outT[:, k * P:(k + 1) * P], c.ident[:])
                    ins.then_inc(out_ps, 1)
                to_features(0)

                def turn(t, par, first, last):
                    hTp = hT[par]
                    pe.wait_ge(hT_ready, t + 1)
                    if not first:
                        pe.wait_ge(xpre_ready, t)
                    mm(B[1][:], w["conv1"], hTp[:], start=True, stop=True).then_inc(c1_ps, 1)
                    if not first:
                        pe.wait_ge(nsq_ready, t)
                    mm(B[2][0:3, :], w["w_se"], hTp[:], start=True, stop=True).then_inc(s_ps, 1)
                    if not first:
                        pe.wait_ge(nmp_ready, t)
                    for k in range(TT):
                        ins = mm(B[3][:, k * P:(k + 1) * P], hTp[:, k * P:(k + 1) * P], w["w_msg"], start=True, stop=True)
                    ins.then_inc(msg_ps, 1)
                    mm(B[4][:], w_hh[:, 2, :], hTp[:], start=True, stop=True).then_inc(ghn_ps, 1)
                    pe.wait_ge(c1_ready, t + 1)

                    def taps(a, b):
                        for k in range(a, b):
                            ins = mm(B[1][:].rearrange("p (g n) -> p g n", g=2), conv2[:, k, :], cpad[:, :, k:k + NODES],
                                     start=(k == 0), stop=(k == CONV_TAPS - 1))
                        return ins
                    taps(0, 6)
                    if not first:
                        to_tokens(t - 1)
                    pe.wait_ge(s_ready, t + 1)
                    pe.wait_ge(s2_ready, t + 1)
                    for k in range(4):
                        ins = mm(B[2][:, k:k + 1], sqT[:, k * P:(k + 1) * P], minus1[:, 0:1], start=True, stop=True)
                    ins.then_inc(nsq_ps, 1)
                    for k in range(4):
                        g = k // 2
                        blk = B[5 + g][:, (k % 2) * NODES:(k % 2 + 1) * NODES]
                        mm(blk, s2T[:, k * P:(k + 1) * P], sT[:, g * NODES:(g + 1) * NODES], start=True, stop=False)
                        ins = mm(blk, minus1[:], sqT[:, g * NODES:(g + 1) * NODES], start=False, stop=True)
                    ins.then_inc(dist_ps, 1)
                    taps(6, CONV_TAPS).then_inc(c2_ps, 1)
                    if not last:
                        if not first:
                            pe.wait_ge(x_done, t)
                        to_features(t + 1)
                    pe.wait_ge(A_ready, t + 1)
                    pe.wait_ge(msg_ready, t + 1)
                    for g in range(2):
                        for m in range(2):
                            ins = mm(B[3][:, g * NODES:(g + 1) * NODES], msg[:, 2 * g + m, :], A[:, 2 * g + m, :],
                                     start=(m == 0), stop=(m == 1))
                    ins.then_inc(nmp_ps, 1)
                    for gate in range(2):
                        mm(B[5 + gate][:], w_hh[:, gate, :], hTp[:], start=True, stop=False)
                    pe.wait_ge(nmp_ready, t + 1)
                    for gate in range(3):
                        mm(B[5 + gate][:], w_ih[:, 1, gate, :], nmp[:], start=(gate == 2), stop=False)
                    pe.wait_ge(xconv_ready, t + 1)
                    for gate, done in ((0, r_ps), (2, n_ps), (1, z_ps)):
                        mm(B[5 + gate][:], w_ih[:, 0, gate, :], xconv[:], start=False, stop=True).then_inc(done, 1)
                every_turn(pe, turn)
                to_tokens(TURNS - 1)


class Experts:
    def __init__(self, count, hidden, top, gated, eps=0.0, capacity=None):
        self.count, self.hidden, self.top, self.gated = count, hidden, top, gated
        self.eps, self.capacity = eps, capacity
        self.chunks = -(-hidden // P)
        self.tiles = top * TILES + count
        assert self.tiles % 8 == 0
        self.width = 2 * hidden if gated else hidden


MOE = {
    "ffn0": Experts(16, 256, 2, True),
    "ffn1": Experts(8, 512, 1, False, capacity=int(np.ceil(1.25 * TILES * P / 8))),
    "ffn3": Experts(8, 341, 2, True, eps=1e-9),
}
FLT_MAX = 3.4028234e38
TOKENS = TILES * P


def moe_fields(m):
    return {"gate_w": (P, m.count), "w1": (P, m.count * m.width), "w3": (P, m.count * m.chunks * D),
            "order": (P, m.count), "tile_no": (P, m.tiles), "lane_no": (P, P), "token1": (P, TILES),
            "spare1": (P, m.tiles)}


LAYOUT["ffn0"] = Layout(gate_b=(P, 16), **moe_fields(MOE["ffn0"]))
LAYOUT["ffn1"] = Layout(gate_b=(P, 8), b1=(P, 8 * 512), b2=(P, 8 * D), **moe_fields(MOE["ffn1"]))
LAYOUT["ffn3"] = Layout(ln2=(P, 1), **moe_fields(MOE["ffn3"]))


def phase_moe(nc, c, name):
    m, L = MOE[name], LAYOUT[name]
    w = {n: L.view(c.block[name], n) for n in L.at}
    with ExitStack() as ctx:
        def sb(n, shape, dt=F32):
            return ctx.enter_context(nc.sbuf_tensor(f"{name}_{n}", shape, dt))
        r = Core()
        r.logits = sb("logits", [P, TILES, m.count])
        r.gate = [sb(f"gate{k}", [P, TILES]) for k in range(m.top)]
        r.lane = [sb(f"lane{k}", [P, TILES]) for k in range(m.top)]
        r.tile = [sb(f"tile{k}", [P, TILES]) for k in range(m.top)]
        r.expert = sb("expert", [1, m.tiles], I32)
        r.source, r.target = sb("source", [P, m.tiles]), sb("target", [P, m.tiles])
        moe_router(nc, c, name, m, w, r)
        moe_slots(nc, c, name, m, w, r)
        moe_inverse(nc, c, name, m, w, r)
        moe_experts(nc, c, name, m, w, r)
        moe_combine(nc, c, name, m, w, r)


def moe_router(nc, c, name, m, w, r):
    E, B = m.count, c.bank
    with ExitStack() as ctx:
        def sb(n, shape, dt=F32):
            return ctx.enter_context(nc.sbuf_tensor(f"{name}_r_{n}", shape, dt))

        def sem(n):
            return c.sem(f"{name}_r_{n}")
        h = [sb(f"h{i}", [P, TT, D]) for i in range(2)]
        hT = [sb(f"hT{i}", [P, TURN]) for i in range(2)]
        h_ready, hT_ps, hT_ready, logits_ps, logits_ready = (sem(n) for n in "h_ready hT_ps hT_ready logits_ps logits_ready".split())
        stored = [sem(f"stored{i}") for i in range(2)]
        with nc.Block() as block:
            @block.sync
            def _(sp):
                def store(t, par, first, last):
                    sp.wait_ge(h_ready, t + 1)
                    sp.dma_start(c.h_turns[t], h[par][:]).then_inc(stored[par], 16)
                every_turn(sp, store)
                for par in range(2):
                    sp.wait_ge(stored[par], 16 * TURNS // 2)

            @block.vector
            def _(v):
                def front(t, par):
                    wait_past(v, hT_ps, t - 1)
                    wait_past(v, stored[par], 8 * (t - par))
                    normalise(v, c, t, h[par]).then_inc(h_ready, 1)
                front(0, 0)

                def turn(t, par, first, last):
                    if not last:
                        front(t + 1, 1 - par)
                    v.wait_ge(logits_ps, t + 1)
                    ps = B[2 + par][:, 0:TT * E].rearrange("p (k e) -> p k e", k=TT)
                    out = r.logits[:, ds(t * TT, TT), :]
                    if "gate_b" in w:
                        ins = v.tensor_tensor(out, ps, w["gate_b"][:, None, :].broadcast_to([P, TT, E]), ALU.add)
                    else:
                        ins = v.tensor_scalar(out, ps, 1.0, None, ALU.mult)
                    ins.then_inc(logits_ready, 1)
                every_turn(v, turn)

            @block.scalar
            def _(a):
                def turn(t, par, first, last):
                    a.wait_ge(hT_ps, t + 1)
                    wait_past(a, logits_ps, t - 1)
                    if "ln2" in w:
                        a.activation(hT[par][:], B[par][:], ACT.Copy, scale=w["ln2"]).then_inc(hT_ready, 1)
                    else:
                        a.activation(hT[par][:], B[par][:], ACT.Copy).then_inc(hT_ready, 1)
                every_turn(a, turn)

            @block.tensor
            def _(pe):
                def to_features(t, par):
                    pe.wait_ge(h_ready, t + 1)
                    wait_past(pe, hT_ready, t - 1)
                    for k in range(TT):
                        ins = pe.transpose(B[par][:, k * P:(k + 1) * P], h[par][:, k, :], c.ident[:])
                    ins.then_inc(hT_ps, 1)
                to_features(0, 0)

                def turn(t, par, first, last):
                    if not last:
                        to_features(t + 1, 1 - par)
                    pe.wait_ge(hT_ready, t + 1)
                    wait_past(pe, logits_ready, t - 1)
                    for k in range(TT):
                        ins = pe.matmul(B[2 + par][:, k * E:(k + 1) * E], hT[par][:, k * P:(k + 1) * P], w["gate_w"],
                                        start=True, stop=True)
                    ins.then_inc(logits_ps, 1)
                every_turn(pe, turn)


def moe_slots(nc, c, name, m, w, r):
    E, B = m.count, c.bank
    N = TILES * E
    halves = [(i * 512, min(512, N - i * 512)) for i in range(-(-N // 512))]
    with ExitStack() as ctx:
        def sb(n, shape, dt=F32):
            return ctx.enter_context(nc.sbuf_tensor(f"{name}_s_{n}", shape, dt))

        def sem(n):
            return c.sem(f"{name}_s_{n}")
        probs, eq, rank = (sb(n, [P, TILES, E]) for n in ("probs", "eq", "rank"))
        hot = [sb(f"hot{k}", [P, TILES, E]) for k in range(m.top)]
        chosen = sb("chosen", [P, TILES, E]) if m.top > 1 else hot[0]
        scan = [sb(f"scan{i}", [P, TILES, E]) for i in range(2)]
        key, den, slot = sb("key", [P, TILES]), sb("den", [P, TILES]), sb("slot", [P, TILES])
        best = [sb(f"best{k}", [P, TILES]) for k in range(m.top)]
        slot_i, lane_i = sb("slot_i", [P, TILES], U32), sb("lane_i", [P, TILES], U32)
        count_i, whole_i = sb("count_i", [P, E], U32), sb("whole_i", [P, E], U32)
        padded, base = sb("padded", [P, E]), sb("base", [P, E])
        ends = [sb(f"ends{i}", [P, E]) for i in range(2)]
        passed, tile_expert = sb("passed", [1, m.tiles, E]), sb("tile_expert", [1, m.tiles])
        upto, ones = sb("upto", [P, P]), sb("ones", [P, P])
        step, filled, upto_ready, shifted, exp_ready, chosen_ready, rank_ps = (
            sem(n) for n in "step filled upto_ready shifted exp_ready chosen_ready rank_ps".split())

        def tiles_(ap):
            return ap[:, :, None].broadcast_to([P, TILES, E])

        def experts_(ap):
            return ap[:, None, :].broadcast_to([P, TILES, E])

        def flat(ap):
            return ap.rearrange("p t e -> p (t e)")
        with nc.Block() as block:
            @block.gpsimd
            def _(g):
                g.memset(ones[:], 1.0)
                g.memset(upto[:], 1.0).then_inc(filled, 1)
                g.wait_ge(filled, 1)
                g.affine_select(out=upto[:], in_=upto[:], compare_op=ALU.is_ge, fill=0.0, base=0,
                                pattern=[[1, P]], channel_multiplier=-1).then_inc(upto_ready, 1)

            @block.scalar
            def _(a):
                a.wait_ge(shifted, 1)
                a.activation(probs[:], r.logits[:], ACT.Exp).then_inc(exp_ready, 1)

            @block.tensor
            def _(pe):
                pe.wait_ge(upto_ready, 1)
                pe.wait_ge(chosen_ready, 1)
                for i, (at, n) in enumerate(halves):
                    cols = flat(chosen[:])[:, at:at + n]
                    pe.matmul(B[i][:, 0:n], upto[:], cols, start=True, stop=True)
                    ins = pe.matmul(B[2 + i][:, 0:n], ones[:], cols, start=True, stop=True)
                ins.then_inc(rank_ps, 1)

            @block.vector
            def _(v):
                n = 0

                def done(ins):
                    nonlocal n
                    n += 1
                    then(v, ins, step, n)
                done(v.tensor_reduce(key[:], r.logits[:], AX.X, ALU.max))
                v.tensor_tensor(r.logits[:], r.logits[:], tiles_(key), ALU.subtract).then_inc(shifted, 1)
                v.wait_ge(exp_ready, 1)
                done(v.tensor_reduce(den[:], probs[:], AX.X, ALU.add))
                done(v.reciprocal(den[:], den[:]))
                done(v.tensor_tensor(probs[:], probs[:], tiles_(den), ALU.mult))
                for k in range(m.top):
                    done(v.tensor_reduce(best[k][:], probs[:], AX.X, ALU.max))
                    done(v.tensor_tensor(eq[:], probs[:], tiles_(best[k]), ALU.is_equal))
                    done(v.tensor_tensor(eq[:], eq[:], experts_(w["order"]), ALU.mult))
                    done(v.tensor_reduce(key[:], eq[:], AX.X, ALU.max))
                    done(v.tensor_tensor(hot[k][:], experts_(w["order"]), tiles_(key), ALU.is_equal))
                    if k + 1 < m.top:
                        done(v.scalar_tensor_tensor(probs[:], hot[k][:], -2.0, probs[:], ALU.mult, ALU.add))
                if m.top > 1:
                    v.tensor_tensor(chosen[:], hot[0][:], hot[1][:], ALU.add).then_inc(chosen_ready, 1)
                    done(v.tensor_tensor(den[:], best[0][:], best[1][:], ALU.add))
                    if m.eps:
                        done(v.tensor_scalar(den[:], den[:], m.eps, None, ALU.add))
                    done(v.reciprocal(den[:], den[:]))
                    for k in range(m.top):
                        ins = v.tensor_tensor(r.gate[k][:], best[k][:], den[:], ALU.mult)
                    done(ins)
                else:
                    v.tensor_copy(r.gate[0][:], best[0][:]).then_inc(chosen_ready, 1)
                v.wait_ge(rank_ps, 1)
                for i, (at, k) in enumerate(halves):
                    v.tensor_copy(flat(rank[:])[:, at:at + k], B[i][:, 0:k])
                    ins = v.tensor_copy(flat(scan[0][:])[:, at:at + k], B[2 + i][:, 0:k])
                done(ins)
                v.tensor_tensor(rank[:], rank[:], scan[0][:], ALU.subtract)
                now, far = 0, 1
                while far < TILES:
                    v.tensor_copy(scan[1 - now][:, 0:far, :], scan[now][:, 0:far, :])
                    done(v.tensor_tensor(scan[1 - now][:, far:, :], scan[now][:, far:, :], scan[now][:, 0:TILES - far, :], ALU.add))
                    now, far = 1 - now, far * 2
                total = scan[now]
                v.tensor_tensor(rank[:], rank[:], total[:], ALU.add)
                done(v.tensor_scalar(count_i[:], total[:, TILES - 1, :], float(P - 1), None, ALU.add))
                done(v.tensor_scalar(whole_i[:], count_i[:], 2 ** 32 - P, None, ALU.bitwise_and))
                v.tensor_copy(padded[:], whole_i[:])
                done(v.tensor_copy(ends[0][:], whole_i[:]))
                at, far = 0, 1
                while far < E:
                    v.tensor_copy(ends[1 - at][:, 0:far], ends[at][:, 0:far])
                    done(v.tensor_tensor(ends[1 - at][:, far:], ends[at][:, far:], ends[at][:, 0:E - far], ALU.add))
                    at, far = 1 - at, far * 2
                end = ends[at]
                done(v.tensor_tensor(base[:], end[:], padded[:], ALU.subtract))
                if m.capacity:
                    done(v.tensor_tensor(eq[:], rank[:], hot[0][:], ALU.mult))
                    done(v.tensor_reduce(key[:], eq[:], AX.X, ALU.add))
                    done(v.tensor_scalar(key[:], key[:], float(m.capacity), None, ALU.is_le))
                    v.tensor_tensor(r.gate[0][:], best[0][:], key[:], ALU.mult)
                done(v.tensor_tensor(rank[:], rank[:], experts_(base), ALU.add))
                for k in range(m.top):
                    done(v.tensor_tensor(eq[:], rank[:], hot[k][:], ALU.mult))
                    done(v.tensor_reduce(slot[:], eq[:], AX.X, ALU.add))
                    done(v.tensor_scalar(slot[:], slot[:], -1.0, None, ALU.add))
                    done(v.tensor_copy(slot_i[:], slot[:]))
                    done(v.tensor_scalar(lane_i[:], slot_i[:], P - 1, None, ALU.bitwise_and))
                    done(v.tensor_copy(r.lane[k][:], lane_i[:]))
                    done(v.tensor_tensor(slot[:], slot[:], r.lane[k][:], ALU.subtract))
                    done(v.tensor_scalar(r.tile[k][:], slot[:], 1.0 / P, None, ALU.mult))
                done(v.tensor_scalar(tile_expert[:], w["tile_no"][0:1, :], float(P), None, ALU.mult))
                done(v.tensor_tensor(passed[:], end[0:1, None, :].broadcast_to([1, m.tiles, E]),
                                     tile_expert[:, :, None].broadcast_to([1, m.tiles, E]), ALU.is_le))
                done(v.tensor_reduce(tile_expert[:], passed[:], AX.X, ALU.add))
                v.tensor_scalar(r.expert[:], tile_expert[:], float(E - 1), None, ALU.min)


def moe_inverse(nc, c, name, m, w, r):
    B = c.bank
    STEPS = TT * m.top
    with ExitStack() as ctx:
        def sb(n, shape, dt=F32):
            return ctx.enter_context(nc.sbuf_tensor(f"{name}_i_{n}", shape, dt))

        def sem(n):
            return c.sem(f"{name}_i_{n}")
        pair1 = [w["token1"]] + [sb(f"pair{k}", [P, TILES]) for k in range(1, m.top)]
        lanes = [sb(f"lanes{i}", [P, STEPS, P]) for i in range(2)]
        tiles = [sb(f"tiles{i}", [P, STEPS, m.tiles]) for i in range(2)]
        empty, number_i, wrapped_i = sb("empty", [P, m.tiles]), sb("number_i", [P, m.tiles], U32), sb("wrapped_i", [P, m.tiles], U32)
        pairs, hot_ready, used_ps, step = sem("pairs"), sem("hot_ready"), sem("used_ps"), sem("step")
        with nc.Block() as block:
            @block.vector
            def _(v):
                if m.top > 1:
                    then(v, v.tensor_scalar(pair1[1][:], w["token1"], float(TOKENS), None, ALU.add), pairs, 1)

                def turn(t, par, first, last):
                    wait_past(v, used_ps, t - 1)
                    for i in range(STEPS):
                        at, k = ds(t * TT + i % TT, 1), i // TT
                        v.tensor_scalar(lanes[par][:, i, :], w["lane_no"], r.lane[k][:, at], None, ALU.is_equal)
                        ins = v.tensor_scalar(tiles[par][:, i, :], w["tile_no"], r.tile[k][:, at], pair1[k][:, at],
                                              ALU.is_equal, ALU.mult)
                    ins.then_inc(hot_ready, 1)
                every_turn(v, turn)
                v.wait_ge(used_ps, TURNS)
                found = B[0][:, 0:m.tiles]
                v.tensor_scalar(empty[:], found, 0.0, None, ALU.is_equal)
                then(v, v.tensor_scalar(number_i[:], found, -1.0, 0.0, ALU.add, ALU.max), step, 1)
                v.tensor_scalar(wrapped_i[:], number_i[:], TOKENS - 1, None, ALU.bitwise_and)
                then(v, v.tensor_tensor(empty[:], empty[:], w["spare1"], ALU.mult), step, 2)
                v.tensor_copy(r.source[:], wrapped_i[:])
                v.scalar_tensor_tensor(r.target[:], found, -1.0, empty[:], ALU.add, ALU.add)

            @block.tensor
            def _(pe):
                def turn(t, par, first, last):
                    pe.wait_ge(hot_ready, t + 1)
                    for i in range(STEPS):
                        ins = pe.matmul(B[0][:, 0:m.tiles], lanes[par][:, i, :], tiles[par][:, i, :],
                                        start=(first and i == 0), stop=(last and i == STEPS - 1))
                    ins.then_inc(used_ps, 1)
                every_turn(pe, turn)


def moe_experts(nc, c, name, m, w, r):
    E, NCH, B = m.count, m.chunks, c.bank
    Q = 4
    QUADS = m.tiles // Q
    split = m.width > 512
    w1 = w["w1"].rearrange("p (e h) -> p e h", e=E)
    w3 = w["w3"].rearrange("p (e c d) -> p e c d", e=E, c=NCH)
    LAG_T, LAG_Y = 2, 3
    with ExitStack() as ctx:
        def sb(n, shape, dt=F32):
            return ctx.enter_context(nc.sbuf_tensor(f"{name}_e_{n}", shape, dt))

        def sem(n):
            return c.sem(f"{name}_e_{n}")
        rows_in = [sb(f"rows_in{i}", [P, Q, D]) for i in range(2)]
        rows_out = [sb(f"rows_out{i}", [P, Q, D]) for i in range(2)]
        gather_at = [sb(f"gather_at{i}", [P, Q], U32) for i in range(2)]
        scatter_at = [sb(f"scatter_at{i}", [P, Q], U32) for i in range(2)]
        xT = [sb(f"xT{i}", [P, Q * P]) for i in range(2)]
        act = [sb(f"act{i}", [P, m.hidden]) for i in range(2)] if m.gated else None
        hid = [sb(f"hid{i}", [P, NCH * P]) for i in range(Q)]
        hidT = [sb(f"hidT{i}", [P, NCH * P]) for i in range(2)]
        cells = sb("cells", [P, 2])
        (filled, gather_set, xT_ps, xT_ready, h_ps, act_ready, hid_ready, hidT_ps, hidT_ready, y_ps,
         y_ready, held) = (sem(n) for n in (
             "filled gather_set xT_ps xT_ready h_ps act_ready hid_ready hidT_ps hidT_ready y_ps "
             "y_ready held").split())
        gathered, scattered = ([c.dma_sem[name, n, i] for i in range(2)] for n in ("gathered", "scattered"))

        def first_banks(k):
            if split:
                i = 1 + 2 * (k % 2)
                return B[i][:, 0:m.hidden], B[i + 1][:, 0:m.hidden]
            return B[1 + k][:, 0:m.hidden], B[1 + k][:, m.hidden:m.width]

        def tile_expert(eng, q, k):
            return eng.value_load(r.expert[0:1, ds(q * Q + k, 1)], min_val=0, max_val=E - 1)

        def unit_before(q, par, k, lag):
            return (q, par, k - lag) if k >= lag else (q - 1, 1 - par, k - lag + Q)

        def near_end(q):
            return isinstance(q, int) and q >= QUADS - 2

        with nc.Block() as block:
            @block.gpsimd
            def _(g):
                g.wait_ge(filled, 1)

                def hold_pool(count):
                    wait_past(g, held, count)
                    g.tensor_tensor(cells[:, 1:2], cells[:, 0:1], cells[:, 0:1], ALU.add).then_inc(held, 1)

                def gather(q, par, count):
                    g.wait_ge(gather_set, q + 1)
                    wait_past(g, xT_ps, q - 1)
                    hold_pool(count)
                    for k in range(Q):
                        g.indirect_dma_start(rows_in[par][:, k, :], None, c.h_rows,
                                             bass.IndirectOffsetOnAxis(gather_at[par][:, k:k + 1], 0)).then_inc(gathered[par], 16)

                def scatter(q, par, count):
                    g.wait_ge(y_ready, q + 1)
                    hold_pool(count)
                    for k in range(Q):
                        g.indirect_dma_start(c.y_rows, bass.IndirectOffsetOnAxis(scatter_at[par][:, k:k + 1], 0),
                                             rows_out[par][:, k, :], None).then_inc(scattered[par], 16)
                gather(0, 0, 0)
                gather(1, 1, 1)

                def quad(q, par, first, last):
                    if not near_end(q):
                        gather(q + 2, par, 2 if first else 2 * q + 1)
                    if not first:
                        scatter(q - 1, 1 - par, 2 * q if last else 2 * q + 1 if near_end(q) else 2 * q + 2)
                every_turn(g, quad, QUADS)
                scatter(QUADS - 1, 1, 2 * QUADS - 1)
                for par in range(2):
                    g.wait_ge(scattered[par], 16 * Q * (QUADS // 2))

            @block.vector
            def _(v):
                v.memset(cells[:], 0.0)
                for one in hid:
                    ins = v.memset(one[:], 0.0)
                ins.then_inc(filled, 1)

                def set_rows(q, par):
                    at = ds(q * Q, Q)
                    wait_past(v, gathered[par], 8 * Q * (q - par))
                    v.tensor_scalar(gather_at[par][:], r.source[:, at], 0.0, None, ALU.add).then_inc(gather_set, 1)

                v.wait_ge(filled, 1)
                set_rows(0, 0)
                set_rows(1, 1)

                def results(q, par):
                    experts = [] if m.gated else [tile_expert(v, q, k) for k in range(Q)]
                    wait_past(v, scattered[par], 8 * Q * (q - par))
                    v.tensor_scalar(scatter_at[par][:], r.target[:, ds(q * Q, Q)], 0.0, None, ALU.add)
                    v.wait_ge(y_ps, (q + 1) * Q)
                    y = B[6 + par][:].rearrange("p (k d) -> p k d", k=Q)
                    if m.gated:
                        ins = v.tensor_copy(rows_out[par][:], y)
                    else:
                        b2 = w["b2"].rearrange("p (e d) -> p e d", e=E)
                        for k in range(Q):
                            ins = v.tensor_tensor(rows_out[par][:, k:k + 1, :], y[:, k:k + 1, :], b2[:, ds(experts[k], 1), :], ALU.add)
                    ins.then_inc(y_ready, 1)

                def quad(q, par, first, last):
                    for k in range(Q):
                        u = q * Q + k
                        gate, up = first_banks(k)
                        if not m.gated:
                            e = tile_expert(v, q, k)
                        wait_past(v, hidT_ps, u - Q + 1)
                        if m.gated:
                            v.wait_ge(act_ready, u + 1)
                            v.tensor_tensor(hid[k][:, 0:m.hidden], act[k % 2][:], up, ALU.mult).then_inc(hid_ready, 1)
                        else:
                            b1 = w["b1"].rearrange("p (e h) -> p e h", e=E)[:, ds(e, 1), :]
                            v.wait_ge(h_ps, u + 1)
                            v.tensor_tensor(hid[k][:, None, :], gate[:, None, :], b1, ALU.add).then_inc(hid_ready, 1)
                        if k == 0 and not near_end(q):
                            set_rows(q + 2, par)
                        if k == 3 and not first:
                            results(q - 1, 1 - par)
                every_turn(v, quad, QUADS)
                results(QUADS - 1, 1)

            @block.scalar
            def _(a):
                def evac_xT(q, par):
                    a.wait_ge(xT_ps, q + 1)
                    wait_past(a, h_ps, (q - 1) * Q)
                    if "ln2" in w:
                        a.activation(xT[par][:], B[0][:], ACT.Copy, scale=w["ln2"]).then_inc(xT_ready, 1)
                    else:
                        a.activation(xT[par][:], B[0][:], ACT.Copy).then_inc(xT_ready, 1)
                evac_xT(0, 0)

                def evac_hidT(q, par, k):
                    u = q * Q + k
                    a.wait_ge(hidT_ps, u + 1)
                    wait_past(a, y_ps, u - 1)
                    a.activation(hidT[k % 2][:], B[5][:, 0:NCH * P], ACT.Copy if m.gated else ACT.Relu).then_inc(hidT_ready, 1)

                def quad(q, par, first, last):
                    for k in range(Q):
                        u = q * Q + k
                        gate, up = first_banks(k)
                        if m.gated:
                            a.wait_ge(h_ps, u + 1)
                            wait_past(a, hid_ready, u - 1)
                            a.activation(act[k % 2][:], gate, ACT.Silu).then_inc(act_ready, 1)
                        if not (first and k < LAG_T):
                            evac_hidT(*unit_before(q, par, k, LAG_T))
                        if k == 1 and not last:
                            evac_xT(q + 1, 1 - par)
                every_turn(a, quad, QUADS)
                for k in range(LAG_T):
                    evac_hidT(*unit_before(QUADS, 0, k, LAG_T))

            @block.tensor
            def _(pe):
                def to_features(q, par):
                    pe.wait_ge(gathered[par], 8 * Q * (q - par) + 16 * Q)
                    wait_past(pe, xT_ready, q)
                    for k in range(Q):
                        ins = pe.transpose(B[0][:, k * P:(k + 1) * P], rows_in[par][:, k, :], c.ident[:])
                    ins.then_inc(xT_ps, 1)

                def first_product(q, par, k):
                    u = q * Q + k
                    e = tile_expert(pe, q, k)
                    if k == 0:
                        pe.wait_ge(xT_ready, q + 1)
                    wait_past(pe, hid_ready, u - (2 if split else Q) + 1)
                    gate, up = first_banks(k)
                    x = xT[par][:, k * P:(k + 1) * P]
                    weights = w1[:, ds(e, 1), :].rearrange("p e h -> p (e h)")
                    if split:
                        pe.matmul(gate, x, weights[:, 0:m.hidden], start=True, stop=True)
                        ins = pe.matmul(up, x, weights[:, m.hidden:m.width], start=True, stop=True)
                    else:
                        ins = pe.matmul(B[1 + k][:, 0:m.width], x, weights, start=True, stop=True)
                    ins.then_inc(h_ps, 1)

                def transpose_hidden(q, par, k):
                    u = q * Q + k
                    pe.wait_ge(hid_ready, u + 1)
                    wait_past(pe, hidT_ready, u)
                    for ch in range(NCH):
                        ins = pe.transpose(B[5][:, ch * P:(ch + 1) * P], hid[k][:, ch * P:(ch + 1) * P], c.ident[:])
                    ins.then_inc(hidT_ps, 1)

                def second_product(q, par, k):
                    u = q * Q + k
                    e = tile_expert(pe, q, k)
                    pe.wait_ge(hidT_ready, u + 1)
                    if k == 0:
                        wait_past(pe, y_ready, q - 1)
                    for ch in range(NCH):
                        weights = w3[:, ds(e, 1), ch, :].rearrange("p e d -> p (e d)")
                        ins = pe.matmul(B[6 + par][:, k * D:(k + 1) * D], hidT[k % 2][:, ch * P:(ch + 1) * P], weights,
                                        start=(ch == 0), stop=(ch == NCH - 1))
                    ins.then_inc(y_ps, 1)
                to_features(0, 0)

                def quad(q, par, first, last):
                    for k in range(Q):
                        first_product(q, par, k)
                        if k == 0 and not last:
                            to_features(q + 1, 1 - par)
                        if not (first and k < LAG_T):
                            transpose_hidden(*unit_before(q, par, k, LAG_T))
                        if not (first and k < LAG_Y):
                            second_product(*unit_before(q, par, k, LAG_Y))
                every_turn(pe, quad, QUADS)
                for k in range(LAG_Y):
                    if k < LAG_T:
                        transpose_hidden(*unit_before(QUADS, 0, k, LAG_T))
                    second_product(*unit_before(QUADS, 0, k, LAG_Y))


def moe_combine(nc, c, name, m, w, r):
    with ExitStack() as ctx:
        def sb(n, shape, dt=F32):
            return ctx.enter_context(nc.sbuf_tensor(f"{name}_c_{n}", shape, dt))

        def sem(n):
            return c.sem(f"{name}_c_{n}")
        y = [[sb(f"y{i}{k}", [P, TT, D]) for k in range(m.top)] for i in range(2)]
        loaded = [sem(f"loaded{i}") for i in range(2)]
        summed, used, stats, xs_ready = sem("summed"), sem("used"), sem("stats"), sem("xs_ready")
        if m.capacity:
            acc, finite, instead = (sb(n, [P, TT, D]) for n in ("acc", "finite", "instead"))
            nan_fix = sem("nan_fix")
        with nc.Block() as block:
            @block.sync
            def _(sp):
                def load(t, par, first, last):
                    wait_past(sp, used, t - 1)
                    for k in range(m.top):
                        sp.dma_start(y[par][k][:], c.y_turns[k * TURNS + t]).then_inc(loaded[par], 16)
                every_turn(sp, load)

            @block.vector
            def _(v):
                def turn(t, par, first, last):
                    rows_ = ds(t * TT, TT)
                    v.wait_ge(loaded[par], 8 * m.top * (t - par) + 16 * m.top)
                    gates = [r.gate[k] for k in range(m.top)]
                    if m.capacity:
                        for k in range(TT):
                            ins = v.tensor_scalar(acc[:, k, :], y[par][0][:, k, :], gates[0][:, ds(t * TT + k, 1)], None, ALU.mult)
                        ins.then_inc(used, 1)
                        v.wait_ge(used, t + 1)
                        v.tensor_scalar(instead[:], acc[:], FLT_MAX, 1e4, ALU.is_gt, ALU.mult)
                        v.tensor_scalar(c.xs[:], acc[:], -FLT_MAX, -1e4, ALU.is_lt, ALU.mult)
                        v.tensor_scalar(finite[:], acc[:], FLT_MAX, None, ALU.is_le).then_inc(nan_fix, 1)
                        v.wait_ge(nan_fix, t * 3 + 1)
                        v.scalar_tensor_tensor(finite[:], acc[:], -FLT_MAX, finite[:], ALU.is_ge, ALU.mult)
                        then(v, v.tensor_tensor(instead[:], instead[:], c.xs[:], ALU.add), nan_fix, t * 3 + 2)
                        hold(v, c)
                        then(v, v.copy_predicated(instead[:], finite[:].bitcast(I32), acc[:]), nan_fix, t * 3 + 3)
                        then(v, v.tensor_tensor(c.xs[:], c.X[:, rows_, :], instead[:], ALU.add), xs_ready, t + 1)
                    else:
                        for k in range(TT):
                            ins = v.tensor_scalar(y[par][0][:, k, :], y[par][0][:, k, :], gates[0][:, ds(t * TT + k, 1)], None, ALU.mult)
                        then(v, ins, summed, 2 * t + 1)
                        for k in range(TT):
                            ins = v.scalar_tensor_tensor(y[par][0][:, k, :], y[par][1][:, k, :], gates[1][:, ds(t * TT + k, 1)],
                                                         y[par][0][:, k, :], ALU.mult, ALU.add)
                        then(v, ins, summed, 2 * t + 2)
                        v.tensor_tensor(c.xs[:], c.X[:, rows_, :], y[par][0][:], ALU.add).then_inc(used, 1)
                        v.wait_ge(used, t + 1)
                    finish_rows(v, c, stats, t)
                every_turn(v, turn)


LAYOUT["gnn1"] = Layout(theta=(P, D), w_t=(P, D), w_h=(P, D), b_t=(P, D))


def phase_gnn1(nc, c):
    L = LAYOUT["gnn1"]
    W = c.block["gnn1"]
    w = {n: L.view(W, n) for n in L.at}
    B = c.bank
    with ExitStack() as ctx:
        def sb(n, shape, dt=F32):
            return ctx.enter_context(nc.sbuf_tensor(f"g1_{n}", shape, dt))

        def sem(n):
            return c.sem(f"g1_{n}")
        h = sb("h", [P, TT, D])
        hT = [sb(f"hT{i}", [P, TURN]) for i in range(2)]
        adj = [sb(f"adj{i}", [P, 4, NODES]) for i in range(2)]
        one = sb("one", [P, 1])
        deg = sb("deg", [P, TT])
        norm = [sb(f"norm{i}", [P, TT]) for i in range(2)]
        f = [sb(f"f{i}", [P, TT, D]) for i in range(2)]
        gpre = [sb(f"gpre{i}", [P, TT, D]) for i in range(2)]
        het = [sb(f"het{i}", [P, TT, D]) for i in range(2)]
        diff, neg, pos = sb("diff", [P, TT, D]), sb("neg", [P, TURN]), sb("pos", [P, TURN])

        one_ready = sem("one_ready")
        adj_ready = [sem(f"adj_ready{i}") for i in range(2)]
        h_ready, hT_ps, hT_ready = sem("h_ready"), sem("hT_ps"), sem("hT_ready")
        deg_ps, deg_ready, norm_ready = sem("deg_ps"), sem("deg_ready"), sem("norm_ready")
        f_ps, f_ready, gate_ps, gpre_ready = sem("f_ps"), sem("f_ready"), sem("gate_ps"), sem("gpre_ready")
        het_ps, het_ready = sem("het_ps"), sem("het_ready")
        gate_ready, agg_ps, diff_ready = sem("gate_ready"), sem("agg_ps"), sem("diff_ready")
        scaled, mixed, neg_ready, exp_ready = sem("scaled"), sem("mixed"), sem("neg_ready"), sem("exp_ready")
        elu_ready, x_sum, stats = sem("elu_ready"), sem("x_sum"), sem("stats")

        with nc.Block() as block:
            @block.sync
            def _(sp):
                def load(t, par, first, last):
                    wait_past(sp, agg_ps, t - 1)
                    sp.dma_start(adj[par][:], c.adjT[t]).then_inc(adj_ready[par], 16)
                every_turn(sp, load)

            @block.gpsimd
            def _(g):
                def degree_norm(t, par):
                    g.wait_ge(deg_ready, t + 1)
                    g.tensor_tensor(norm[par][:], deg[:], c.minus_half[:, 0:TT], ALU.pow).then_inc(norm_ready, 1)
                degree_norm(0, 0)

                def turn(t, par, first, last):
                    if not last:
                        degree_norm(t + 1, 1 - par)
                every_turn(g, turn)

            @block.vector
            def _(v):
                v.memset(one[:], 1.0).then_inc(one_ready, 1)

                def front(t, par):
                    v.wait_ge(deg_ps, t + 1)
                    wait_past(v, norm_ready, t)
                    v.tensor_scalar(deg[:], B[4][:, 0:TT], 1e-6, None, ALU.add).then_inc(deg_ready, 1)
                    v.wait_ge(gate_ps, t + 1)
                    v.tensor_tensor(gpre[par][:], tiles4(B[2][:]), w["b_t"][:, None, :].broadcast_to([P, TT, D]),
                                    ALU.add).then_inc(gpre_ready, 1)
                    v.wait_ge(norm_ready, t + 1)
                    v.wait_ge(f_ps, t + 1)
                    for k in range(TT):
                        ins = v.tensor_scalar(f[par][:, k, :], B[1][:, k * P:(k + 1) * P], norm[par][:, k:k + 1], None, ALU.mult)
                    ins.then_inc(f_ready, 1)
                normalise(v, c, 0, h).then_inc(h_ready, 1)
                front(0, 0)

                def turn(t, par, first, last):
                    if not last:
                        v.wait_ge(hT_ps, t + 1)
                        normalise(v, c, t + 1, h).then_inc(h_ready, 1)
                        front(t + 1, 1 - par)
                    v.wait_ge(agg_ps, t + 1)
                    v.wait_ge(het_ready, t + 1)
                    for k in range(TT):
                        ins = v.scalar_tensor_tensor(diff[:, k, :], B[5][:, k * P:(k + 1) * P], norm[par][:, k:k + 1],
                                                     het[par][:, k, :], ALU.mult, ALU.subtract)
                    then(v, ins, diff_ready, t + 1)
                    v.wait_ge(gate_ready, t + 1)
                    g6 = tiles4(B[6][:])
                    then(v, v.scalar_tensor_tensor(g6, g6, 1.0, diff[:], ALU.add, ALU.mult), scaled, t + 1)
                    then(v, v.scalar_tensor_tensor(g6, g6, 0.5, het[par][:], ALU.mult, ALU.add), mixed, t + 1)
                    v.tensor_scalar(pos[:], B[6][:], 0.0, None, ALU.max)
                    v.tensor_scalar(neg[:], B[6][:], 0.0, None, ALU.min).then_inc(neg_ready, 1)
                    v.wait_ge(exp_ready, t + 1)
                    then(v, v.scalar_tensor_tensor(B[7][:], B[7][:], -1.0, pos[:], ALU.add, ALU.add), elu_ready, t + 1)
                    then(v, v.tensor_tensor(c.xs[:], tiles4(B[7][:]), c.X[:, ds(t * TT, TT), :], ALU.add), x_sum, t + 1)
                    finish_rows(v, c, stats, t)
                every_turn(v, turn)

            @block.scalar
            def _(a):
                def front(t, par):
                    a.wait_ge(hT_ps, t + 1)
                    a.activation(hT[par][:], B[0][:], ACT.Copy).then_inc(hT_ready, 1)
                    a.wait_ge(het_ps, t + 1)
                    a.activation(het[par][:], tiles4(B[3][:]), ACT.Copy).then_inc(het_ready, 1)
                front(0, 0)

                def turn(t, par, first, last):
                    a.wait_ge(gpre_ready, t + 1)
                    wait_past(a, neg_ready, t)
                    a.activation(B[6][:], gpre[par][:].rearrange("p k d -> p (k d)"), ACT.Tanh, scale=0.5).then_inc(gate_ready, 1)
                    if not last:
                        front(t + 1, 1 - par)
                    a.wait_ge(neg_ready, t + 1)
                    a.activation(B[7][:], neg[:], ACT.Exp).then_inc(exp_ready, 1)
                every_turn(a, turn)

            @block.tensor
            def _(pe):
                mm = pe.matmul

                def to_features(t):
                    pe.wait_ge(h_ready, t + 1)
                    wait_past(pe, hT_ready, t)
                    for k in range(TT):
                        ins = pe.transpose(B[0][:, k * P:(k + 1) * P], h[:, k, :], c.ident[:])
                    ins.then_inc(hT_ps, 1)

                def front(t, par):
                    to_features(t)
                    pe.wait_ge(adj_ready[par], 8 * (t - par) + 16)
                    wait_past(pe, deg_ready, t)
                    for k in range(TT):
                        g, n = k // 2, k % 2
                        for m in range(2):
                            ins = mm(B[4][:, k:k + 1], adj[par][:, 2 * g + m, n * P:(n + 1) * P], one[:],
                                     start=(m == 0), stop=(m == 1))
                    ins.then_inc(deg_ps, 1)
                    pe.wait_ge(hT_ready, t + 1)
                    for bank, weight, done, used in ((B[1], "theta", f_ps, f_ready), (B[2], "w_t", gate_ps, gpre_ready),
                                                     (B[3], "w_h", het_ps, het_ready)):
                        wait_past(pe, used, t)
                        for k in range(TT):
                            ins = mm(bank[:, k * P:(k + 1) * P], hT[par][:, k * P:(k + 1) * P], w[weight], start=True, stop=True)
                        ins.then_inc(done, 1)
                pe.wait_ge(one_ready, 1)
                front(0, 0)

                def turn(t, par, first, last):
                    if not last:
                        front(t + 1, 1 - par)
                    pe.wait_ge(f_ready, t + 1)
                    wait_past(pe, diff_ready, t)
                    for k in range(TT):
                        g, n = k // 2, k % 2
                        for m in range(2):
                            ins = mm(B[5][:, k * P:(k + 1) * P], adj[par][:, 2 * g + m, n * P:(n + 1) * P],
                                     f[par][:, 2 * g + m, :], start=(m == 0), stop=(m == 1))
                    ins.then_inc(agg_ps, 1)
                every_turn(pe, turn)


LAYOUT["gnn2"] = Layout(w_rel=(P, D), w_root=(P, D), b_rel=(P, D), gamma=(P, D), beta=(P, D))


def phase_gnn2(nc, c):
    L = LAYOUT["gnn2"]
    W = c.block["gnn2"]
    w = {n: L.view(W, n) for n in L.at}
    B = c.bank

    def wide(ap):
        return ap[:, None, :].broadcast_to([P, TT, D])
    with ExitStack() as ctx:
        def sb(n, shape, dt=F32):
            return ctx.enter_context(nc.sbuf_tensor(f"g2_{n}", shape, dt))

        def sem(n):
            return c.sem(f"g2_{n}")
        u = [sb(f"u{i}", [P, TT, D]) for i in range(2)]
        hn, hg = sb("hn", [P, TT, D]), sb("hg", [P, TT, D])
        h = [sb(f"h{i}", [P, TT, D]) for i in range(2)]
        hT = [sb(f"hT{i}", [P, TURN]) for i in range(2)]
        adj = [sb(f"adj{i}", [P, 4, NODES]) for i in range(2)]
        aggT = sb("aggT", [P, TURN])
        bn2, mv2 = sb("bn2", [P, TT, 6]), sb("mv2", [P, TT, 2])
        ve2, rstd2, shift2 = sb("ve2", [P, TT]), sb("rstd2", [P, TT]), sb("shift2", [P, TT])

        adj_ready = [sem(f"adj_ready{i}") for i in range(2)]
        norm2, ve2_ready, rstd2_ready = sem("norm2"), sem("ve2_ready"), sem("rstd2_ready")
        hn_ready, hg_ready, h_ready = sem("hn_ready"), sem("hg_ready"), sem("h_ready")
        hT_ps, hT_ready, agg_ps, agg_ready = sem("hT_ps"), sem("hT_ready"), sem("agg_ps"), sem("agg_ready")
        conv_ps, tail, x_sum, stats = sem("conv_ps"), sem("tail"), sem("x_sum"), sem("stats")

        with nc.Block() as block:
            @block.sync
            def _(sp):
                def load(t, par, first, last):
                    wait_past(sp, agg_ps, t - 1)
                    sp.dma_start(adj[par][:], c.adjT[t]).then_inc(adj_ready[par], 16)
                every_turn(sp, load)

            @block.gpsimd
            def _(g):
                def front(t, par):
                    g.wait_ge(ve2_ready, t + 1)
                    g.tensor_tensor(rstd2[:], ve2[:], c.minus_half[:, 0:TT], ALU.pow).then_inc(rstd2_ready, 1)
                    g.wait_ge(hn_ready, t + 1)
                    then(g, g.tensor_tensor(hg[:], hn[:], wide(w["gamma"]), ALU.mult), hg_ready, t + 1)
                    wait_past(g, conv_ps, t - 1)
                    g.tensor_tensor(h[par][:], hg[:], wide(w["beta"]), ALU.add).then_inc(h_ready, 1)
                front(0, 0)

                def turn(t, par, first, last):
                    if not last:
                        front(t + 1, 1 - par)
                every_turn(g, turn)

            @block.vector
            def _(v):
                def front(t, par):
                    n = t * 4
                    then(v, normalise(v, c, t, u[par]), norm2, n + 1)
                    for k in range(TT):
                        ins = v.bn_stats(bn2[:, k, :], u[par][:, k, :])
                    then(v, ins, norm2, n + 2)
                    hold(v, c)
                    for k in range(TT):
                        ins = v.bn_aggr(mv2[:, k, :], bn2[:, k, :])
                    then(v, ins, norm2, n + 3)
                    v.tensor_scalar(ve2[:], mv2[:, :, 1], EPS, None, ALU.add).then_inc(ve2_ready, 1)
                    v.wait_ge(rstd2_ready, t + 1)
                    then(v, v.scalar_tensor_tensor(shift2[:], mv2[:, :, 0], -1.0, rstd2[:], ALU.mult, ALU.mult), norm2, n + 4)
                    wait_past(v, hg_ready, t)
                    for k in range(TT):
                        ins = v.tensor_scalar(hn[:, k, :], u[par][:, k, :], rstd2[:, k:k + 1], shift2[:, k:k + 1], ALU.mult, ALU.add)
                    ins.then_inc(hn_ready, 1)
                front(0, 0)

                def turn(t, par, first, last):
                    if not last:
                        front(t + 1, 1 - par)
                    v.wait_ge(conv_ps, t + 1)
                    conv = tiles4(B[2 + par][:])
                    then(v, v.tensor_tensor(conv, conv, wide(w["b_rel"]), ALU.add), tail, 2 * t + 1)
                    then(v, v.scalar_tensor_tensor(conv, conv, 0.0, u[par][:], ALU.max, ALU.add), tail, 2 * t + 2)
                    then(v, v.tensor_tensor(c.xs[:], conv, c.X[:, ds(t * TT, TT), :], ALU.add), x_sum, t + 1)
                    finish_rows(v, c, stats, t)
                every_turn(v, turn)

            @block.scalar
            def _(a):
                def turn(t, par, first, last):
                    a.wait_ge(hT_ps, t + 1)
                    a.activation(hT[par][:], B[0][:], ACT.Copy).then_inc(hT_ready, 1)
                    a.wait_ge(agg_ps, t + 1)
                    a.activation(aggT[:], B[1][:], ACT.Copy).then_inc(agg_ready, 1)
                every_turn(a, turn)

            @block.tensor
            def _(pe):
                mm = pe.matmul

                def turn(t, par, first, last):
                    pe.wait_ge(h_ready, t + 1)
                    wait_past(pe, hT_ready, t)
                    for k in range(TT):
                        ins = pe.transpose(B[0][:, k * P:(k + 1) * P], h[par][:, k, :], c.ident[:])
                    ins.then_inc(hT_ps, 1)
                    pe.wait_ge(adj_ready[par], 8 * (t - par) + 16)
                    wait_past(pe, agg_ready, t)
                    for g in range(2):
                        for m in range(2):
                            ins = mm(B[1][:, g * NODES:(g + 1) * NODES], h[par][:, 2 * g + m, :], adj[par][:, 2 * g + m, :],
                                     start=(m == 0), stop=(m == 1))
                    ins.then_inc(agg_ps, 1)
                    wait_past(pe, x_sum, t - 1)
                    pe.wait_ge(hT_ready, t + 1)
                    pe.wait_ge(agg_ready, t + 1)
                    for k in range(TT):
                        mm(B[2 + par][:, k * P:(k + 1) * P], aggT[:, k * P:(k + 1) * P], w["w_rel"], start=True, stop=False)
                        ins = mm(B[2 + par][:, k * P:(k + 1) * P], hT[par][:, k * P:(k + 1) * P], w["w_root"], start=False, stop=True)
                    ins.then_inc(conv_ps, 1)
                every_turn(pe, turn)


HEADS2, HD2, SL = 8, 64, 64
IN2 = HEADS2 * HD2
KC = IN2 // P
NS2, TAPS2 = 64, 3
PROJ2 = 2 * IN2 + 2 * NS2 + 2 * HEADS2
LAYOUT["ffn2"] = Layout(
    w_fx=(P, IN2), b_fx=(P, IN2), w_x=(P, IN2), b_x=(P, KC), w_slice=(P, P), b_slice=(P, IN2), temp=(P, HEADS2),
    in_w=(P, KC * PROJ2), conv_x=(P, KC * TAPS2), convb_x=(P, KC), conv_bc=(NS2, 2 * TAPS2), convb_bc=(NS2, 2),
    dt_bias=(P, 2 * HEADS2), a_log=(P, 2 * HEADS2), skip=(P, HEADS2), fcd=(P, KC * HEADS2), norm_w=(P, IN2),
    hy_out=(P, KC * IN2), out_w=(P, KC * D), out_b=(P, D), masks=(P, 2 * P))


def phase_ffn2(nc, c):
    L = LAYOUT["ffn2"]
    W = c.block["ffn2"]
    w = {n: L.view(W, n) for n in L.at}
    in_w = w["in_w"].rearrange("p (k n) -> p k n", k=KC)
    conv_x = w["conv_x"].rearrange("p (k n) -> p k n", k=KC)
    conv_bc = w["conv_bc"].rearrange("p (k n) -> p k n", k=2)
    hy_out = w["hy_out"].rearrange("p (k n) -> p k n", k=KC)
    out_w = w["out_w"].rearrange("p (k n) -> p k n", k=KC)
    fcd = w["fcd"].rearrange("p (k n) -> p k n", k=KC)
    masks = w["masks"].rearrange("p (a t) -> p a t", a=2)
    B = c.bank

    def heads(ap):
        return ap.rearrange("p (h c) -> p h c", h=HEADS2)

    def per_head(ap, n):
        return ap[:, :, None].broadcast_to([P, ap.shape[1], n])
    with ExitStack() as ctx:
        def sb(n, shape, dt=F32):
            return ctx.enter_context(nc.sbuf_tensor(f"f2_{n}", shape, dt))

        def sem(n):
            return c.sem(f"f2_{n}")
        h, hT, xmT = sb("h", [P, TT, D]), sb("hT", [P, TURN]), sb("xmT", [P, KC, TURN])
        fx = [sb(f"fx{i}", [P, TT, IN2]) for i in range(2)]
        sw = [sb(f"sw{i}", [P, TT, IN2]) for i in range(2)]
        swT = sb("swT", [P, TT, KC, P])
        mx, sm, rsm = sb("mx", [P, HEADS2]), sb("sm", [P, HEADS2]), sb("rsm", [P, HEADS2])
        itemp, slice_w, slice_b = sb("itemp", [P, HEADS2]), sb("slice_w", [P, KC, P]), sb("slice_b", [P, IN2])
        ones, neg_a = sb("ones", [P, P]), sb("neg_a", [P, 2 * HEADS2])
        sn = sb("sn", [P, 2, KC, SL])
        stT = sb("stT", [P, KC, 2, SL])
        tz, sz = sb("tz", [P, IN2]), sb("sz", [P, IN2])
        xpad, xc, tx = sb("xpad", [P, KC, 2, TAPS2 - 1 + SL]), sb("xc", [P, KC, 2, SL]), sb("tx", [P, IN2])
        xT = sb("xT", [P, KC, P])
        bcpad, bc, tbc = sb("bcpad", [NS2, 2, 2, TAPS2 - 1 + SL]), sb("bc", [NS2, 2, 2, SL]), sb("tbc", [NS2, 2 * P])
        Bt, Cpad = sb("Bt", [NS2, P]), sb("Cpad", [NS2, P + 2])
        dtr, u, m, e, e2, r, s, s2, poly, dt, am = (sb(n, [P, 2 * HEADS2]) for n in (
            "dtr", "u", "m", "e", "e2", "r", "s", "s2", "poly", "dt", "am"))
        gm = sb("gm", [P, 2, P])
        xtok = sb("xtok", [P, IN2])
        xdt = [sb(f"xdt{i}", [P, IN2]) for i in range(2)]
        a_run = [sb(f"a_run{i}", [P, HEADS2, P]) for i in range(2)]
        decay = [c.spare["ffn2"][:, q * 4 * P:(q + 1) * 4 * P].rearrange("p (h t) -> p h t", h=4) for q in range(4)]
        g8, term, yg, yn = sb("g8", [P, HEADS2]), sb("term", [P, IN2]), sb("yg", [P, IN2]), sb("yn", [P, IN2])
        ms, ve, rstd = sb("ms", [P, 1]), sb("ve", [P, 1]), sb("rstdy", [P, 1])
        ygT, otT = sb("ygT", [P, KC, P]), sb("otT", [P, KC, 2, P])
        pm = c.spare["ffn2"][:, 16 * P:].rearrange("p (g k d) -> p g k d", g=2, k=KC)

        (setup, a_exp, h_ready, hT_ps, hT_ready, fx_ps, fx_ready, xm_ps, xm_ready, lg_ps, soft, lg_ready, lg_exp,
         sw_ready, st_ps, stn, stT_ready, z_ps, tz_ready, sz_ready, x_ps, xpad_ready, bcd_ps, bcd_ready, conv,
         xc_ready, bc_ready, tx_ready, tbc_ready, xT_ready, bct_ready, sp, spm_ready, spe_ready, dt_ready, G_ps,
         gm_ready, xt_ps, xtok_ready, fcd_ps, g8_ready, term_ready, a_run_ready, xdt_ready, D_ps, D_exp,
         decay_ready, y_ps, y_sum, yg_ready, ms_ready, ve_ready, rstd_ready, yn_ready, yT_ps, ygT_ready, ot_ps,
         otT_ready, pm_ps, pm_ready, swT_ps, swT_ready, fin_ps, x_sum, x_done, stats) = (sem(n) for n in (
             "setup a_exp h_ready hT_ps hT_ready fx_ps fx_ready xm_ps xm_ready lg_ps soft lg_ready lg_exp "
             "sw_ready st_ps stn stT_ready z_ps tz_ready sz_ready x_ps xpad_ready bcd_ps bcd_ready conv "
             "xc_ready bc_ready tx_ready tbc_ready xT_ready bct_ready sp spm_ready spe_ready dt_ready G_ps "
             "gm_ready xt_ps xtok_ready fcd_ps g8_ready term_ready a_run_ready xdt_ready D_ps D_exp "
             "decay_ready y_ps y_sum yg_ready ms_ready ve_ready rstd_ready yn_ready yT_ps ygT_ready ot_ps "
             "otT_ready pm_ps pm_ready swT_ps swT_ready fin_ps x_sum x_done stats").split())

        with nc.Block() as block:
            @block.gpsimd
            def _(g):
                def turn(t, par, first, last):
                    for d in range(2):
                        g.wait_ge(dt_ready, t + 1)
                        g.tensor_tensor(a_run[d][:], per_head(am[:, d * HEADS2:(d + 1) * HEADS2], P),
                                        masks[:, d, None, :].broadcast_to([P, HEADS2, P]), ALU.mult).then_inc(a_run_ready, 1)
                        g.wait_ge(xtok_ready, t + 1)
                        g.tensor_tensor(heads(xdt[d][:]), heads(xtok[:]), per_head(dt[:, d * HEADS2:(d + 1) * HEADS2], HD2),
                                        ALU.mult).then_inc(xdt_ready, 1)
                    g.wait_ge(g8_ready, t + 1)
                    g.tensor_tensor(heads(term[:]), heads(xtok[:]), per_head(g8[:], HD2), ALU.mult).then_inc(term_ready, 1)
                    g.wait_ge(ve_ready, t + 1)
                    g.tensor_tensor(rstd[:], ve[:], c.minus_half[:, 0:1], ALU.pow).then_inc(rstd_ready, 1)
                every_turn(g, turn)

            @block.vector
            def _(v):
                for z in (xpad, bcpad, Cpad, otT):
                    v.memset(z[:], 0.0)
                v.memset(ones[:], 1.0)
                then(v, v.tensor_scalar(itemp[:], w["temp"], 1e-6, None, ALU.max), setup, 1)
                then(v, v.reciprocal(itemp[:], itemp[:]), setup, 2)
                for j in range(KC):
                    v.tensor_tensor(slice_w[:, j, :].rearrange("p (a g) -> p a g", a=2),
                                    w["w_slice"].rearrange("p (a g) -> p a g", a=2), per_head(itemp[:, 2 * j:2 * j + 2], SL), ALU.mult)
                v.tensor_tensor(heads(slice_b[:]), heads(w["b_slice"]), per_head(itemp[:], SL), ALU.mult)
                for n in ("conv_x", "convb_x", "conv_bc", "convb_bc"):
                    v.tensor_scalar(w[n], w[n], 0.5, None, ALU.mult)
                v.wait_ge(a_exp, 1)
                v.tensor_scalar(neg_a[:], neg_a[:], -1.0, None, ALU.mult).then_inc(setup, 1)
                v.wait_ge(setup, 3)

                def fx_piece(t, par, k):
                    v.wait_ge(fx_ps, t * TT + k + 1)
                    v.tensor_tensor(fx[par][:, k, :], B[1][:], w["b_fx"], ALU.add).then_inc(fx_ready, 1)

                def soft_a(t, k):
                    n = (t * TT + k) * 4
                    v.wait_ge(lg_ps, t * TT + k + 1)
                    b3 = heads(B[3][:])
                    then(v, v.tensor_tensor(B[3][:], B[3][:], slice_b[:], ALU.add), soft, n + 1)
                    then(v, v.tensor_reduce(mx[:], b3, AX.X, ALU.max), soft, n + 2)
                    v.tensor_tensor(b3, b3, per_head(mx[:], SL), ALU.subtract).then_inc(lg_ready, 1)

                def soft_b(t, par, k):
                    n = (t * TT + k) * 4 + 2
                    v.wait_ge(lg_exp, t * TT + k + 1)
                    b3 = heads(B[3][:])
                    then(v, v.tensor_reduce(sm[:], b3, AX.X, ALU.add), soft, n + 1)
                    then(v, v.reciprocal(rsm[:], sm[:]), soft, n + 2)
                    v.tensor_tensor(heads(sw[par][:, k, :]), b3, per_head(rsm[:], SL), ALU.mult).then_inc(sw_ready, 1)

                def pooled(t, g):
                    n = (t * 2 + g) * 2
                    v.wait_ge(st_ps, t * 2 + g + 1)
                    num, den = (B[4 + 2 * g + i][:].rearrange("p (k a s) -> p k a s", k=KC, a=2) for i in range(2))
                    for a in range(2):
                        rows_ = slice(a * HD2, (a + 1) * HD2)
                        ins = v.tensor_scalar(sn[rows_, g], den[rows_, :, a, :], 1e-5, None, ALU.add)
                    then(v, ins, stn, n + 1)
                    then(v, v.reciprocal(sn[:, g], sn[:, g]), stn, n + 2)
                    for a in range(2):
                        rows_ = slice(a * HD2, (a + 1) * HD2)
                        ins = v.tensor_tensor(stT[rows_, :, g, :], num[rows_, :, a, :], sn[rows_, g], ALU.mult)
                    ins.then_inc(stT_ready, 1)

                def convolve(t, first_time, pad, weights, bias, out, k_range, done, n):
                    for tap in range(TAPS2 - 1, -1, -1):
                        for k in k_range:
                            src = pad[:, k, :, tap:tap + SL]
                            if tap == TAPS2 - 1:
                                ins = v.tensor_scalar(out[:, k], src, weights[:, k, tap:tap + 1], bias[:, k:k + 1], ALU.mult, ALU.add)
                            else:
                                ins = v.scalar_tensor_tensor(out[:, k], src, weights[:, k, tap:tap + 1], out[:, k], ALU.mult, ALU.add)
                        if tap:
                            n += 1
                            then(v, ins, conv, n)
                        else:
                            ins.then_inc(done, 1)

                normalise(v, c, 0, h).then_inc(h_ready, 1)
                for k in range(TT):
                    fx_piece(0, 0, k)
                for k in range(TT):
                    soft_a(0, k)
                    soft_b(0, 0, k)

                def turn(t, par, first, last):
                    more = not last
                    if more:
                        v.wait_ge(hT_ps, t + 1)
                        normalise(v, c, t + 1, h).then_inc(h_ready, 1)
                    pooled(t, 0)
                    pooled(t, 1)
                    v.wait_ge(tz_ready, t + 1)
                    v.scalar_tensor_tensor(sz[:], tz[:], 1.0, B[4][:], ALU.add, ALU.mult).then_inc(sz_ready, 1)
                    if more:
                        fx_piece(t + 1, 1 - par, 0)
                        fx_piece(t + 1, 1 - par, 1)
                    v.wait_ge(xpad_ready, t + 1)
                    convolve(t, first, xpad, conv_x, w["convb_x"], xc, range(KC), xc_ready, t * 4)
                    v.wait_ge(bcd_ready, t + 1)
                    convolve(t, first, bcpad, conv_bc, w["convb_bc"], bc, range(2), bc_ready, t * 4 + 2)
                    n = t * 14
                    then(v, v.tensor_tensor(u[:], dtr[:], w["dt_bias"], ALU.add), sp, n + 1)
                    v.scalar_tensor_tensor(m[:], u[:], -1.0, u[:], ALU.mult, ALU.min).then_inc(spm_ready, 1)
                    v.wait_ge(tx_ready, t + 1)
                    v.wait_ge(xc_ready, t + 1)
                    v.scalar_tensor_tensor(xT[:].rearrange("p k n -> p (k n)"), tx[:], 1.0, xc[:].rearrange("p k a s -> p (k a s)"),
                                           ALU.add, ALU.mult).then_inc(xT_ready, 1)
                    v.wait_ge(tbc_ready, t + 1)
                    v.wait_ge(bc_ready, t + 1)
                    bcf = bc[:].rearrange("p b a s -> p b (a s)")
                    v.scalar_tensor_tensor(Bt[:], tbc[:, 0:P], 1.0, bcf[:, 0, :], ALU.add, ALU.mult)
                    v.scalar_tensor_tensor(Cpad[:, 1:P + 1], tbc[:, P:2 * P], 1.0, bcf[:, 1, :], ALU.add, ALU.mult).then_inc(bct_ready, 1)
                    v.wait_ge(spe_ready, t + 1)
                    then(v, v.tensor_scalar(e2[:], e[:], 2.0, None, ALU.add), sp, n + 2)
                    then(v, v.reciprocal(r[:], e2[:]), sp, n + 3)
                    then(v, v.tensor_tensor(s[:], e[:], r[:], ALU.mult), sp, n + 4)
                    then(v, v.tensor_tensor(s2[:], s[:], s[:], ALU.mult), sp, n + 5)
                    then(v, v.tensor_scalar(poly[:], s2[:], 2.0 / 15, None, ALU.mult), sp, n + 6)
                    for i, odd in enumerate((13, 11, 9, 7, 5, 3)):
                        then(v, v.scalar_tensor_tensor(poly[:], poly[:], 2.0 / odd, s2[:], ALU.add, ALU.mult), sp, n + 7 + i)
                    then(v, v.scalar_tensor_tensor(s[:], poly[:], 2.0, s[:], ALU.add, ALU.mult), sp, n + 13)
                    then(v, v.scalar_tensor_tensor(dt[:], u[:], 0.0, s[:], ALU.max, ALU.add), sp, n + 14)
                    v.tensor_tensor(am[:], dt[:], neg_a[:], ALU.mult).then_inc(dt_ready, 1)
                    v.wait_ge(G_ps, t + 1)
                    v.tensor_tensor(gm[:], B[7][:, 0:2 * P].rearrange("p (a n) -> p a n", a=2), masks, ALU.mult).then_inc(gm_ready, 1)
                    v.wait_ge(fcd_ps, t + 1)
                    v.tensor_tensor(g8[:], B[4][:, 0:HEADS2], w["skip"], ALU.add).then_inc(g8_ready, 1)
                    v.wait_ge(gm_ready, t + 1)
                    if more:
                        fx_piece(t + 1, 1 - par, 2)
                        fx_piece(t + 1, 1 - par, 3)

                    def weigh(q):
                        v.wait_ge(D_exp, t * 4 + q + 1)
                        v.tensor_tensor(decay[q][:], B[6 + q % 2][:].rearrange("p (a n) -> p a n", a=4),
                                        gm[:, q // 2, None, :].broadcast_to([P, 4, P]), ALU.mult).then_inc(decay_ready, 1)
                    if more:
                        soft_a(t + 1, 0)
                    weigh(0)
                    weigh(1)
                    if more:
                        soft_b(t + 1, 1 - par, 0)
                        soft_a(t + 1, 1)
                    weigh(2)
                    weigh(3)
                    if more:
                        soft_b(t + 1, 1 - par, 1)
                    v.wait_ge(y_ps, t + 1)
                    v.wait_ge(term_ready, t + 1)
                    then(v, v.tensor_tensor(B[5][:], B[5][:], term[:], ALU.add), y_sum, t + 1)
                    v.scalar_tensor_tensor(yg[:], B[5][:], 0.5, sz[:], ALU.mult, ALU.mult).then_inc(yg_ready, 1)
                    if more:
                        soft_a(t + 1, 2)
                    v.wait_ge(ms_ready, t + 1)
                    v.tensor_scalar(ve[:], ms[:], 1.0 / IN2, 1e-5, ALU.mult, ALU.add).then_inc(ve_ready, 1)
                    if more:
                        soft_b(t + 1, 1 - par, 2)
                    v.wait_ge(rstd_ready, t + 1)
                    v.scalar_tensor_tensor(yn[:], yg[:], rstd[:], w["norm_w"], ALU.mult, ALU.mult).then_inc(yn_ready, 1)
                    if more:
                        soft_a(t + 1, 3)
                        soft_b(t + 1, 1 - par, 3)
                    v.wait_ge(fin_ps, t + 1)
                    then(v, v.tensor_tensor(c.xs[:], tiles4(B[4][:]), c.X[:, ds(t * TT, TT), :], ALU.add), x_sum, t + 1)
                    then(v, v.tensor_tensor(c.xs[:], c.xs[:], w["out_b"][:, None, :].broadcast_to([P, TT, D]), ALU.add), x_done, t + 1)
                    finish_rows(v, c, stats, t)
                every_turn(v, turn)

            @block.scalar
            def _(a):
                a.activation(neg_a[:], w["a_log"], ACT.Exp).then_inc(a_exp, 1)

                def evac_hT(t):
                    a.wait_ge(hT_ps, t + 1)
                    a.activation(hT[:], B[0][:], ACT.Copy).then_inc(hT_ready, 1)

                def xm_piece(t, j):
                    a.wait_ge(xm_ps, t * KC + j + 1)
                    a.activation(xmT[:, j, :], B[2][:], ACT.Identity, bias=w["b_x"][:, j:j + 1]).then_inc(xm_ready, 1)

                def exp_piece(t, k):
                    a.wait_ge(lg_ready, t * TT + k + 1)
                    a.activation(B[3][:], B[3][:], ACT.Exp).then_inc(lg_exp, 1)

                def swT_piece(t, k):
                    a.wait_ge(swT_ps, t * TT + k + 1)
                    a.activation(swT[:, k], B[0][:].rearrange("p (j n) -> p j n", j=KC), ACT.Copy).then_inc(swT_ready, 1)

                evac_hT(0)
                for j in range(KC):
                    xm_piece(0, j)
                for k in range(TT):
                    exp_piece(0, k)

                def turn(t, par, first, last):
                    more = not last
                    if more:
                        evac_hT(t + 1)
                    swT_piece(t, 0)
                    a.wait_ge(z_ps, t + 1)
                    a.activation(tz[:], B[4][:], ACT.Tanh, scale=0.5).then_inc(tz_ready, 1)
                    a.wait_ge(x_ps, t + 1)
                    a.activation(xpad[:, :, :, TAPS2 - 1:], B[5][:].rearrange("p (k a s) -> p k a s", k=KC, a=2), ACT.Copy).then_inc(xpad_ready, 1)
                    a.wait_ge(bcd_ps, t + 1)
                    a.activation(bcpad[:, :, :, TAPS2 - 1:], B[6][0:NS2, 0:2 * P].rearrange("p (k a s) -> p k a s", k=2, a=2), ACT.Copy)
                    a.activation(dtr[:], B[6][:, 2 * P:2 * P + 2 * HEADS2], ACT.Copy).then_inc(bcd_ready, 1)
                    if more:
                        xm_piece(t + 1, 0)
                        xm_piece(t + 1, 1)
                    a.wait_ge(xc_ready, t + 1)
                    a.activation(tx[:], xc[:].rearrange("p k a s -> p (k a s)"), ACT.Tanh).then_inc(tx_ready, 1)
                    a.wait_ge(bc_ready, t + 1)
                    a.activation(tbc[:], bc[:].rearrange("p b a s -> p (b a s)"), ACT.Tanh).then_inc(tbc_ready, 1)
                    a.wait_ge(spm_ready, t + 1)
                    a.activation(e[:], m[:], ACT.Exp).then_inc(spe_ready, 1)
                    a.wait_ge(xt_ps, t + 1)
                    a.activation(xtok[:], B[5][:], ACT.Copy).then_inc(xtok_ready, 1)
                    if more:
                        xm_piece(t + 1, 2)
                        xm_piece(t + 1, 3)
                        exp_piece(t + 1, 0)
                    swT_piece(t, 1)

                    def decay_exp(q):
                        a.wait_ge(D_ps, t * 4 + q + 1)
                        a.activation(B[6 + q % 2][:], B[6 + q % 2][:], ACT.Exp).then_inc(D_exp, 1)
                    decay_exp(0)
                    decay_exp(1)
                    if more:
                        exp_piece(t + 1, 1)
                    decay_exp(2)
                    decay_exp(3)
                    swT_piece(t, 2)
                    a.wait_ge(yg_ready, t + 1)
                    a.activation(tx[:], yg[:], ACT.Square, accum_out=ms[:]).then_inc(ms_ready, 1)
                    if more:
                        exp_piece(t + 1, 2)
                    swT_piece(t, 3)
                    a.wait_ge(yT_ps, t + 1)
                    a.activation(ygT[:].rearrange("p k n -> p (k n)"), B[4][:], ACT.Copy).then_inc(ygT_ready, 1)
                    if more:
                        exp_piece(t + 1, 3)
                    a.wait_ge(ot_ps, t + 1)
                    for hh in range(2):
                        rows_ = slice(hh * HD2, (hh + 1) * HD2)
                        ins = a.activation(otT[rows_, :, :, hh * SL:(hh + 1) * SL],
                                           B[5][rows_, :].rearrange("p (k a s) -> p k a s", k=KC, a=2), ACT.Copy)
                    ins.then_inc(otT_ready, 1)
                    for g in range(2):
                        a.wait_ge(pm_ps, t * 2 + g + 1)
                        a.activation(pm[:, g].rearrange("p k d -> p (k d)"), B[6 + g][:], ACT.Copy).then_inc(pm_ready, 1)
                every_turn(a, turn)

            @block.tensor
            def _(pe):
                mm = pe.matmul

                def to_features(t):
                    pe.wait_ge(h_ready, t + 1)
                    wait_past(pe, swT_ready, t * TT - TT)
                    for k in range(TT):
                        ins = pe.transpose(B[0][:, k * P:(k + 1) * P], h[:, k, :], c.ident[:])
                    ins.then_inc(hT_ps, 1)

                def fx_piece(t, k):
                    pe.wait_ge(hT_ready, t + 1)
                    wait_past(pe, fx_ready, t * TT + k)
                    mm(B[1][:], hT[:, k * P:(k + 1) * P], w["w_fx"], start=True, stop=True).then_inc(fx_ps, 1)

                def xm_piece(t, j):
                    wait_past(pe, xm_ready, t * KC + j)
                    mm(B[2][:], w["w_x"][:, j * P:(j + 1) * P], hT[:], start=True, stop=True).then_inc(xm_ps, 1)

                def lg_piece(t, k):
                    pe.wait_ge(xm_ready, t * KC + KC)
                    wait_past(pe, sw_ready, t * TT + k)
                    for j in range(KC):
                        ins = mm(B[3][:, j * P:(j + 1) * P], xmT[:, j, k * P:(k + 1) * P], slice_w[:, j, :], start=True, stop=True)
                    ins.then_inc(lg_ps, 1)

                def swT_piece(t, par, k, hT_turn):
                    if k == 0:
                        pe.wait_ge(hT_ready, hT_turn)
                    wait_past(pe, swT_ready, t * TT + k)
                    for j in range(KC):
                        ins = pe.transpose(B[0][:, j * P:(j + 1) * P], sw[par][:, k, j * P:(j + 1) * P], c.ident[:])
                    ins.then_inc(swT_ps, 1)

                pe.wait_ge(setup, 3)
                to_features(0)
                for k in range(TT):
                    fx_piece(0, k)
                    xm_piece(0, k)
                for k in range(TT):
                    lg_piece(0, k)

                def turn(t, par, first, last):
                    more = not last
                    pe.wait_ge(sw_ready, t * TT + TT)
                    pe.wait_ge(fx_ready, t * TT + TT)
                    wait_past(pe, x_sum, t)
                    for g in range(2):
                        for j in range(KC):
                            for k in range(2):
                                mm(B[4 + 2 * g][:, j * P:(j + 1) * P], fx[par][:, 2 * g + k, j * P:(j + 1) * P],
                                   sw[par][:, 2 * g + k, j * P:(j + 1) * P], start=(k == 0), stop=(k == 1))
                        for k in range(2):
                            ins = mm(B[5 + 2 * g][:], ones[:], sw[par][:, 2 * g + k, :], start=(k == 0), stop=(k == 1))
                        ins.then_inc(st_ps, 1)
                    if more:
                        to_features(t + 1)
                    swT_piece(t, par, 0, t + 2 if more else t + 1)
                    pe.wait_ge(stT_ready, t * 2 + 2)

                    def tokens(ap):
                        return ap.rearrange("p a s -> p (a s)")
                    for k in range(KC):
                        ins = mm(B[4][:], tokens(stT[:, k]), in_w[:, k, 0:IN2], start=(k == 0), stop=(k == KC - 1))
                    ins.then_inc(z_ps, 1)
                    for j in range(KC):
                        for k in range(KC):
                            ins = mm(B[5][:, j * P:(j + 1) * P], in_w[:, k, IN2 + j * P:IN2 + (j + 1) * P], tokens(stT[:, k]),
                                     start=(k == 0), stop=(k == KC - 1))
                    ins.then_inc(x_ps, 1)
                    for j in range(2):
                        for k in range(KC):
                            mm(B[6][0:NS2, j * P:(j + 1) * P], in_w[:, k, 2 * IN2 + j * NS2:2 * IN2 + (j + 1) * NS2], tokens(stT[:, k]),
                               start=(k == 0), stop=(k == KC - 1))
                    for k in range(KC):
                        ins = mm(B[6][:, 2 * P:2 * P + 2 * HEADS2], tokens(stT[:, k]), in_w[:, k, 2 * IN2 + 2 * NS2:PROJ2],
                                 start=(k == 0), stop=(k == KC - 1))
                    ins.then_inc(bcd_ps, 1)
                    if more:
                        for k in range(2):
                            fx_piece(t + 1, k)
                            xm_piece(t + 1, k)
                    pe.wait_ge(bct_ready, t + 1)
                    for d in range(2):
                        ins = mm(B[7][:, d * P:(d + 1) * P], Bt[:], Cpad[:, 2 * d:2 * d + P], start=True, stop=True)
                    ins.then_inc(G_ps, 1)
                    pe.wait_ge(xT_ready, t + 1)
                    for k in range(KC):
                        ins = pe.transpose(B[5][:, k * P:(k + 1) * P], xT[:, k, :], c.ident[:])
                    ins.then_inc(xt_ps, 1)
                    pe.wait_ge(sz_ready, t + 1)
                    for k in range(KC):
                        ins = mm(B[4][:, 0:HEADS2], xT[:, k, :], fcd[:, k, :], start=(k == 0), stop=(k == KC - 1))
                    ins.then_inc(fcd_ps, 1)
                    if more:
                        for k in range(2, 4):
                            fx_piece(t + 1, k)
                            xm_piece(t + 1, k)
                        lg_piece(t + 1, 0)
                    swT_piece(t, par, 1, None)

                    def decays(q):
                        d = q // 2
                        pe.wait_ge(a_run_ready, t * 2 + d + 1)
                        if q == 0:
                            pe.wait_ge(gm_ready, t + 1)
                        if q >= 2:
                            pe.wait_ge(decay_ready, t * 4 + q - 1)
                        mm(B[6 + q % 2][:], masks[:, 1 - d, :], a_run[d][:, (q % 2) * 4:(q % 2) * 4 + 4, :].rearrange("p a n -> p (a n)"),
                           start=True, stop=True).then_inc(D_ps, 1)
                    decays(0)
                    decays(1)
                    if more:
                        lg_piece(t + 1, 1)
                    decays(2)
                    decays(3)
                    swT_piece(t, par, 2, None)
                    pe.wait_ge(decay_ready, t * 4 + 4)
                    pe.wait_ge(xdt_ready, t * 2 + 2)
                    for hd in range(HEADS2):
                        for d in range(2):
                            ins = mm(B[5][:, hd * HD2:(hd + 1) * HD2], decay[2 * d + hd // 4][:, hd % 4, :],
                                     xdt[d][:, hd * HD2:(hd + 1) * HD2], start=(d == 0), stop=(d == 1))
                    ins.then_inc(y_ps, 1)
                    if more:
                        lg_piece(t + 1, 2)
                    swT_piece(t, par, 3, None)
                    pe.wait_ge(yn_ready, t + 1)
                    pe.wait_ge(g8_ready, t + 1)
                    for k in range(KC):
                        ins = pe.transpose(B[4][:, k * P:(k + 1) * P], yn[:, k * P:(k + 1) * P], c.ident[:])
                    ins.then_inc(yT_ps, 1)
                    if more:
                        lg_piece(t + 1, 3)
                    pe.wait_ge(ygT_ready, t + 1)
                    for j in range(KC):
                        for k in range(KC):
                            ins = mm(B[5][:, j * P:(j + 1) * P], hy_out[:, k, j * P:(j + 1) * P], ygT[:, k, :],
                                     start=(k == 0), stop=(k == KC - 1))
                    ins.then_inc(ot_ps, 1)
                    pe.wait_ge(otT_ready, t + 1)
                    for g in range(2):
                        for j in range(KC):
                            ins = mm(B[6 + g][:, j * P:(j + 1) * P], otT[:, j, g, :], out_w[:, j, :], start=True, stop=True)
                        ins.then_inc(pm_ps, 1)
                    pe.wait_ge(swT_ready, t * TT + TT)
                    for k in range(TT):
                        pe.wait_ge(pm_ready, t * 2 + k // 2 + 1)
                        for j in range(KC):
                            ins = mm(B[4][:, k * P:(k + 1) * P], swT[:, k, j, :], pm[:, k // 2, j, :], start=(j == 0), stop=(j == KC - 1))
                    ins.then_inc(fin_ps, 1)
                every_turn(pe, turn)


HD_G, HD_A = 16, 32
LAYOUT["gnn3"] = Layout(wq=(P, D), wk=(P, D), wv=(P, D), qmask=(P, 8), sel=(P, P), wo=(P, 2 * D), bo=(P, D))
LAYOUT["att3"] = Layout(ln1=(P, 1), wq=(P, D), wq_rot=(P, D), wk=(P, D), wk_rot=(P, D), wv=(P, D), cos=(P, NODES),
                        sin=(P, NODES), qmask=(P, 4), far=(P, 384), wo=(P, D))


def phase_attention(nc, c, name):
    L = LAYOUT[name]
    W = c.block[name]
    w = {n: L.view(W, n) for n in L.at}
    B = c.bank
    causal = name == "att3"
    NH = 4 if causal else 8
    U = 2 * NH
    SPAN = [(0, 128), (128, 256)] if causal else [(0, 256), (256, 256)]
    BLOCKS = [(0, 0, 0), (1, 0, 128), (1, 1, 256)] if causal else [(0, 0, 0), (1, 0, 128), (0, 1, 256), (1, 1, 384)]
    WIDTH = 384 if causal else 512
    SCORE_BANKS = [B[2], B[3], B[5]]
    bank_of = [u % 3 for u in range(U)]
    if U == 16:
        bank_of[15] = 1
    back = []
    for u in range(U):
        k = 1
        while bank_of[(u - k) % U] != bank_of[u]:
            k += 1
        back.append(k)
    LAG_T, LAG_PV = 2, 3
    if causal:
        AT = dict(evac=2, norm_o=3, final=4, rows=4, front_n=4, front_h=5, t=5, hT=5, q=6, rope_q=6, k=7, rope_k=7, v=7, vevac=7)
    else:
        AT = dict(evac=2, sel=4, norm_o=5, final=6, rows=7, front_n=8, t=9, hT=9, q=10, k=11, v=15)
    with ExitStack() as ctx:
        def sb(n, shape, dt=F32):
            return ctx.enter_context(nc.sbuf_tensor(f"{name}_{n}", shape, dt))

        def sem(n):
            return c.sem(f"{name}_{n}")
        u_ = [sb(f"u{i}", [P, TT, D]) for i in range(2 if causal else 1)]
        h = sb("h", [P, TT, D]) if causal else u_[0]
        hT = sb("hT", [P, TURN])
        qm = [sb(f"qm{i}", [P, NH, TURN]) for i in range(2)]
        kT = [sb(f"kT{i}", [P, TURN]) for i in range(2)]
        VW = 32
        vv = [sb(f"v{i}", [P, TT, NH, VW]) for i in range(2)]
        low = [sb(f"low{u}", [P, 2]) for u in range(4)]
        prob = [sb(f"prob{u}", [P, 512]) for u in range(4)]
        probT = [sb(f"probT{u}", [P, 512]) for u in range(2)]
        if causal:
            ones, t1, qk = sb("ones", [P, VW]), sb("t1", [P, TURN]), sb("qk", [P, TURN])
            bn2, mv2, ve2, rs2 = sb("bn2", [P, TT, 6]), sb("mv2", [P, TT, 2]), sb("ve2", [P, TT]), sb("rs2", [P, TT])
            rsum, on = sb("rsum", [P, TURN]), [sb("on", [P, TURN])]
        else:
            nla = [sb(f"nla{i}", [P, 4, NODES]) for i in range(2)]
            tiny, minus1 = sb("tiny", [P, 1]), sb("minus1", [P, 1])
            oe, on = ([sb(f"{n}{i}", [P, TURN]) for i in range(2)] for n in ("oe", "on"))

        (fill, h_ready, hT_ps, hT_ready, q_ps, q_ready, k_ps, k_ready, v_ps, v_ready, sc_ps, low_ready, exp_ready, pt_ps,
         pt_ready, pv_ps, on_ready, fin_ps, x_sum, x_done, stats) = (sem(n) for n in (
             "fill h_ready hT_ps hT_ready q_ps q_ready k_ps k_ready v_ps v_ready sc_ps low_ready exp_ready pt_ps "
             "pt_ready pv_ps on_ready fin_ps x_sum x_done stats").split())
        if causal:
            (rms, ve2_ready, rs2_ready, rope, recip_done, o_free) = (sem(n) for n in "rms ve2_ready rs2_ready rope recip_done o_free".split())
        else:
            adj_ready = [sem(f"adj_ready{i}") for i in range(2)]
            (minus1_ready, log_ready, nla_ready, oe0_ready, oe1_ready, sum_ps, recip_done) = (sem(n) for n in
                "minus1_ready log_ready nla_ready oe0_ready oe1_ready sum_ps recip_done".split())

        def lagged(t, u, lag, first, do):
            if u >= lag:
                do(t, u - lag)
            elif not first:
                do(t - 1, u - lag + U)

        with nc.Block() as block:
            @block.sync
            def _(sp):
                if not causal:
                    def load(t, par, first, last):
                        if not first:
                            wait_past(sp, low_ready, (t - 1) * U)
                        sp.dma_start(nla[par][:], c.adj[t]).then_inc(adj_ready[par], 16)
                    every_turn(sp, load)

            @block.gpsimd
            def _(g):
                def front(t, par):
                    if causal:
                        g.wait_ge(ve2_ready, t + 1)
                        g.tensor_tensor(rs2[:], ve2[:], c.minus_half[:, 0:TT], ALU.pow).then_inc(rs2_ready, 1)
                    else:
                        g.wait_ge(log_ready, t + 1)
                        g.tensor_tensor(nla[par][:], nla[par][:], minus1[:, 0:1, None].broadcast_to([P, 4, NODES]),
                                        ALU.mult).then_inc(nla_ready, 1)
                if not causal:
                    g.memset(minus1[:], -1.0).then_inc(minus1_ready, 1)
                    g.wait_ge(minus1_ready, 1)
                front(0, 0)

                def turn(t, par, first, last):
                    if not last:
                        front(t + 1, 1 - par)
                every_turn(g, turn)

            @block.vector
            def _(v):
                if causal:
                    v.memset(ones[:], 1.0).then_inc(fill, 1)
                else:
                    v.memset(tiny[:], 1e-6)
                    v.memset(vv[0][:, :, :, HD_G:], 1.0)
                    v.memset(vv[1][:, :, :, HD_G:], 1.0).then_inc(fill, 1)

                def front_n(t, par):
                    if not causal:
                        wait_past(v, hT_ps, t)
                        normalise(v, c, t, h).then_inc(h_ready, 1)
                        return
                    then(v, normalise(v, c, t, u_[par]), rms, t * 3 + 1)
                    for k in range(TT):
                        ins = v.bn_stats(bn2[:, k, :], u_[par][:, k, :])
                    then(v, ins, rms, t * 3 + 2)
                    hold(v, c)
                    for k in range(TT):
                        ins = v.bn_aggr(mv2[:, k, :], bn2[:, k, :])
                    then(v, ins, rms, t * 3 + 3)
                    mean_square(v, ve2, mv2, rms2, t, ve2_ready)

                def front_h(t, par):
                    v.wait_ge(rs2_ready, t + 1)
                    wait_past(v, hT_ps, t)
                    for k in range(TT):
                        ins = v.tensor_scalar(h[:, k, :], u_[par][:, k, :], rs2[:, k:k + 1], None, ALU.mult)
                    ins.then_inc(h_ready, 1)

                def rope_into(t, n, ps, done, out):
                    v.wait_ge(ps, t + 1)

                    def two(ap):
                        return ap.rearrange("p (g n) -> p g n", g=2)
                    wide = [w[x][:, None, :].broadcast_to([P, 2, NODES]) for x in ("cos", "sin")]
                    v.tensor_tensor(two(t1[:]), two(B[1][:]), wide[0], ALU.mult)
                    then(v, v.tensor_tensor(two(B[0][:]), two(B[0][:]), wide[1], ALU.mult), rope, n + 1)
                    return v.tensor_tensor(out[:], B[0][:], t1[:], ALU.add)

                def rope_q(t, par):
                    then(v, rope_into(t, t * 3, q_ps, None, qk), rope, t * 3 + 2)
                    for i in range(NH):
                        ins = v.tensor_scalar(qm[par][:, i, :], qk[:], w["qmask"][:, i:i + 1], None, ALU.mult)
                    ins.then_inc(q_ready, 1)

                def rope_k(t, par):
                    rope_into(t, t * 3 + 2, k_ps, None, kT[par]).then_inc(k_ready, 1)

                def scores_low(t, par, u):
                    n, g = t * U + u, u // NH
                    v.wait_ge(sc_ps, n + 1)
                    hold(v, c, 2 + u % 4)
                    bank = SCORE_BANKS[bank_of[u]]
                    for qt, (c0, keys) in enumerate(SPAN):
                        blk = bank[:, c0:c0 + keys]
                        other = w["far"][:, c0:c0 + keys] if causal else nla[par][:, 2 * g + qt, :]
                        ins = v.tensor_tensor_reduce(blk, blk, other, 1.0, FLT_MAX, ALU.add, ALU.min, low[u % 4][:, qt:qt + 1])
                    ins.then_inc(low_ready, 1)

                def evac_T(t, u):
                    n = t * U + u
                    v.wait_ge(pt_ps, n + 1)
                    wait_past(v, pv_ps, n - 1)
                    v.tensor_copy(probT[u % 2][:, 0:WIDTH], B[4][:, 0:WIDTH]).then_inc(pt_ready, 1)

                def norm_o(t, par):
                    if causal:
                        v.wait_ge(pv_ps, (t + 1) * U)
                        then(v, v.reciprocal(rsum[:], B[7][:]), recip_done, t + 1)
                        v.tensor_tensor(on[0][:], B[6][:], rsum[:], ALU.mult).then_inc(on_ready, 1)
                    else:
                        v.wait_ge(sum_ps, t + 1)
                        v.reciprocal(B[0][:], B[0][:])
                        then(v, v.reciprocal(B[1][:], B[1][:]), recip_done, t + 1)
                        v.tensor_tensor(on[0][:], B[0][:], oe[0][:], ALU.mult)
                        v.tensor_tensor(on[1][:], B[1][:], oe[1][:], ALU.mult).then_inc(on_ready, 1)

                def new_rows(t, par):
                    v.wait_ge(fin_ps, t + 1)
                    rows_ = ds(t * TT, TT)
                    if causal:
                        then(v, v.tensor_tensor(c.xs[:], tiles4(B[0][:]), u_[par][:], ALU.add), x_sum, t + 1)
                        v.tensor_tensor(c.X[:, rows_, :], c.X[:, rows_, :], c.xs[:], ALU.add)
                        v.tensor_scalar(c.X1[:, rows_, :], c.xs[:], 1.0, None, ALU.mult)
                        finish_rows(v, c, stats, t, store=False)
                    else:
                        then(v, v.tensor_tensor(c.xs[:], tiles4(B[0][:]), c.X[:, rows_, :], ALU.add), x_sum, t + 1)
                        then(v, v.tensor_tensor(c.xs[:], c.xs[:], w["bo"][:, None, :].broadcast_to([P, TT, D]), ALU.add), x_done, t + 1)
                        finish_rows(v, c, stats, t)

                rms2 = sem("rms2") if causal else None
                front_n(0, 0)
                if causal:
                    front_h(0, 0)
                    rope_q(0, 0)
                    rope_k(0, 0)

                def tail(t, par, u):
                    if u == AT["evac"] and not causal:
                        v.wait_ge(pv_ps, (t + 1) * U)
                        v.tensor_copy(oe[1][:], B[7][:]).then_inc(oe1_ready, 1)
                    if u == AT["norm_o"]:
                        norm_o(t, par)
                    if u == AT["rows"]:
                        new_rows(t, par)

                def turn(t, par, first, last):
                    for u in range(U):
                        if not causal and u == 0:
                            v.wait_ge(nla_ready, t + 1)
                        scores_low(t, par, u)
                        lagged(t, u, LAG_T, first, evac_T)
                        if not first:
                            tail(t - 1, 1 - par, u)
                        if not last:
                            if u == AT["front_n"]:
                                front_n(t + 1, 1 - par)
                            if causal and u == AT["front_h"]:
                                front_h(t + 1, 1 - par)
                            if causal and u == AT["rope_q"]:
                                rope_q(t + 1, 1 - par)
                            if causal and u == AT["rope_k"]:
                                rope_k(t + 1, 1 - par)
                every_turn(v, turn)
                for u in range(U - LAG_T, U):
                    evac_T(TURNS - 1, u)
                for u in range(U):
                    tail(TURNS - 1, 1, u)

            @block.scalar
            def _(a):
                def log_adj(t, par):
                    a.wait_ge(adj_ready[par], 8 * (t - par) + 16)
                    a.activation(nla[par][:], nla[par][:], ACT.Ln, bias=tiny[:]).then_inc(log_ready, 1)

                def evac_hT(t, par):
                    a.wait_ge(hT_ps, t + 1)
                    if causal:
                        a.activation(hT[:], B[0][:], ACT.Copy, scale=w["ln1"]).then_inc(hT_ready, 1)
                    else:
                        a.activation(hT[:], B[0][:], ACT.Copy).then_inc(hT_ready, 1)

                def evac_q(t, par, i):
                    a.wait_ge(q_ps, t + 1)
                    a.activation(qm[par][:, i, :], B[1][:], ACT.Copy, scale=w["qmask"][:, i:i + 1]).then_inc(q_ready, 1)

                def evac_k(t, par):
                    a.wait_ge(k_ps, t + 1)
                    a.activation(kT[par][:], B[0][:], ACT.Copy).then_inc(k_ready, 1)

                def evac_v(t, par):
                    a.wait_ge(v_ps, t + 1)
                    width = VW if causal else HD_G
                    a.activation(vv[par][:, :, :, 0:width], B[1][:].rearrange("p (k i d) -> p k i d", k=TT, i=NH), ACT.Copy).then_inc(v_ready, 1)

                def exp(t, u):
                    n = t * U + u
                    a.wait_ge(low_ready, n + 1)
                    wait_past(a, pt_ps, n - 3)
                    bank = SCORE_BANKS[bank_of[u]]
                    for qt, (c0, keys) in enumerate(SPAN):
                        ins = a.activation(prob[u % 4][:, c0:c0 + keys], bank[:, c0:c0 + keys], ACT.Exp,
                                           bias=low[u % 4][:, qt:qt + 1], scale=-1.0)
                    ins.then_inc(exp_ready, 1)

                a.wait_ge(fill, 1)
                if not causal:
                    log_adj(0, 0)
                evac_hT(0, 0)
                if not causal:
                    for i in range(NH):
                        evac_q(0, 0, i)
                    evac_k(0, 0)
                evac_v(0, 0)

                def turn(t, par, first, last):
                    for u in range(U):
                        exp(t, u)
                        if not causal and not first and u == AT["evac"]:
                            a.wait_ge(pv_ps, t * U)
                            a.activation(oe[0][:], B[6][:], ACT.Copy).then_inc(oe0_ready, 1)
                        if not last:
                            if not causal:
                                if u == AT["front_n"]:
                                    log_adj(t + 1, 1 - par)
                                if AT["k"] <= u < AT["k"] + NH // 2:
                                    evac_q(t + 1, 1 - par, 2 * (u - AT["k"]))
                                    evac_q(t + 1, 1 - par, 2 * (u - AT["k"]) + 1)
                                if u == AT["k"] + NH // 2 - 1:
                                    evac_k(t + 1, 1 - par)
                            if u == AT["hT"]:
                                evac_hT(t + 1, 1 - par)
                            if u == AT["v"]:
                                evac_v(t + 1, 1 - par)
                every_turn(a, turn)
                if not causal:
                    a.wait_ge(pv_ps, TURNS * U)
                    a.activation(oe[0][:], B[6][:], ACT.Copy).then_inc(oe0_ready, 1)

            @block.tensor
            def _(pe):
                mm = pe.matmul
                QN = 1 if causal else NH

                def to_features(t):
                    pe.wait_ge(h_ready, t + 1)
                    wait_past(pe, x_sum, t - 1)
                    for k in range(TT):
                        ins = pe.transpose(B[0][:, k * P:(k + 1) * P], h[:, k, :], c.ident[:])
                    ins.then_inc(hT_ps, 1)

                def q_proj(t):
                    pe.wait_ge(hT_ready, t + 1)
                    wait_past(pe, v_ready, t)
                    if not causal:
                        wait_past(pe, on_ready, t - 1)
                    ins = mm(B[1][:], w["wq"], hT[:], start=True, stop=True)
                    if causal:
                        ins = mm(B[0][:], w["wq_rot"], hT[:], start=True, stop=True)
                    ins.then_inc(q_ps, 1)

                def k_proj(t):
                    if causal:
                        pe.wait_ge(q_ready, t + 1)
                        mm(B[1][:], w["wk"], hT[:], start=True, stop=True)
                        ins = mm(B[0][:], w["wk_rot"], hT[:], start=True, stop=True)
                    else:
                        ins = mm(B[0][:], w["wk"], hT[:], start=True, stop=True)
                    ins.then_inc(k_ps, 1)

                def v_proj(t):
                    if causal:
                        pe.wait_ge(k_ready, t + 1)
                    else:
                        pe.wait_ge(q_ready, t * NH + NH)
                    for k in range(TT):
                        ins = mm(B[1][:, k * P:(k + 1) * P], hT[:, k * P:(k + 1) * P], w["wv"], start=True, stop=True)
                    ins.then_inc(v_ps, 1)

                def scores(t, par, u):
                    n, g, i = t * U + u, u // NH, u % NH
                    if u == 0:
                        pe.wait_ge(q_ready, (t + 1) * QN)
                        pe.wait_ge(k_ready, t + 1)
                    wait_past(pe, exp_ready, n - back[u] + 1)
                    for qt, (c0, keys) in enumerate(SPAN):
                        q0 = g * NODES + qt * P
                        ins = mm(SCORE_BANKS[bank_of[u]][:, c0:c0 + keys], qm[par][:, i, q0:q0 + P],
                                 kT[par][:, g * NODES:g * NODES + keys], start=True, stop=True)
                    ins.then_inc(sc_ps, 1)

                def turn_T(t, u):
                    n = t * U + u
                    pe.wait_ge(exp_ready, n + 1)
                    wait_past(pe, pt_ready, n)
                    for qt, kt, col in BLOCKS:
                        src = SPAN[qt][0] + kt * P
                        ins = pe.transpose(B[4][:, col:col + P], prob[u % 4][:, src:src + P], c.ident[:])
                    ins.then_inc(pt_ps, 1)

                def product_v(par_of):
                    def do(t, u):
                        n, g, i = t * U + u, u // NH, u % NH
                        par = par_of(t, u)
                        pe.wait_ge(pt_ready, n + 1)
                        if u == 0:
                            pe.wait_ge(v_ready, t + 1)
                            if causal:
                                wait_past(pe, on_ready, t)
                            else:
                                wait_past(pe, oe0_ready, t)
                                wait_past(pe, oe1_ready, t)
                        q = 32 * (i % 4)
                        pT = probT[u % 2]
                        outs = [(B[6], None), (B[7], ones)] if causal else [(B[6 + i // 4], None)]
                        for bank, stat in outs:
                            for kt in range(2):
                                lhs = vv[par][:, 2 * g + kt, i, :] if stat is None else stat[:]
                                if causal and kt == 1:
                                    dst, src = bank[q:q + 32, g * NODES + P:(g + 1) * NODES], pT[:, 256:384]
                                else:
                                    dst, src = bank[q:q + 32, g * NODES:(g + 1) * NODES], pT[:, kt * 256:kt * 256 + 256]
                                ins = mm(dst, lhs, src, start=(kt == 0), stop=(kt == 1), skip_group_check=True)
                        ins.then_inc(pv_ps, 1)
                    return do

                def sums(t):
                    pe.wait_ge(oe0_ready, t + 1)
                    pe.wait_ge(oe1_ready, t + 1)
                    mm(B[0][:], w["sel"], oe[0][:], start=True, stop=True)
                    mm(B[1][:], w["sel"], oe[1][:], start=True, stop=True).then_inc(sum_ps, 1)

                def final(t):
                    pe.wait_ge(on_ready, t + 1)
                    wo = w["wo"].rearrange("p (j o) -> p j o", o=D)
                    for k in range(TT):
                        for j in range(len(on)):
                            ins = mm(B[0][:, k * P:(k + 1) * P], on[j][:, k * P:(k + 1) * P], wo[:, j, :],
                                     start=(j == 0), stop=(j == len(on) - 1))
                    ins.then_inc(fin_ps, 1)

                def tail(t, u):
                    if not causal and u == AT["sel"]:
                        sums(t)
                    if u == AT["final"]:
                        final(t)

                pe.wait_ge(fill, 1)
                to_features(0)
                q_proj(0)
                k_proj(0)
                v_proj(0)

                def turn(t, par, first, last):
                    pv = product_v(lambda tt, uu: par if tt is t else 1 - par)
                    for u in range(U):
                        scores(t, par, u)
                        lagged(t, u, LAG_T, first, turn_T)
                        lagged(t, u, LAG_PV, first, pv)
                        if not first:
                            tail(t - 1, u)
                        if not last:
                            if u == AT["t"]:
                                to_features(t + 1)
                            if u == AT["q"]:
                                q_proj(t + 1)
                            if u == AT["k"]:
                                k_proj(t + 1)
                            if u == AT["v"]:
                                v_proj(t + 1)
                every_turn(pe, turn)
                last_pv = product_v(lambda tt, uu: 1)
                for u in range(U, U + LAG_PV):
                    if u - LAG_T < U:
                        turn_T(TURNS - 1, u - LAG_T)
                    last_pv(TURNS - 1, u - LAG_PV)
                for u in range(U):
                    tail(TURNS - 1, u)


PHASES = {"gnn0": phase_gnn0, "gnn1": phase_gnn1, "gnn2": phase_gnn2,
          "ffn2": phase_ffn2,
          "gnn3": lambda nc, c: phase_attention(nc, c, "gnn3"), "att3": lambda nc, c: phase_attention(nc, c, "att3")}
PHASES.update({n: (lambda nc, c, n=n: phase_moe(nc, c, n)) for n in MOE})


def program(nc, dram, order):
    with ExitStack() as ctx:
        c = Core()
        c.order, c.dram = order, dram
        c.adjT, c.adj = (dram[n].rearrange("(t k p) n -> t p k n", p=P, k=4) for n in ("adjT", "adj"))

        def sb(name, shape, dt=F32):
            return ctx.enter_context(nc.sbuf_tensor(name, shape, dt))
        c.sem = lambda name: ctx.enter_context(nc.semaphore(name))
        c.X = sb("X", [P, TILES, D])
        c.MV, c.bn, c.mv = sb("MV", [P, TILES, 2]), sb("bn", [P, TT, 6]), sb("mv", [P, TT, 2])
        c.xs = sb("xs", [P, TT, D])
        c.tick = sb("tick", [P, 6])
        c.var_eps, c.rstd, c.shift, c.minus_half = (sb(n, [P, TILES]) for n in ("var_eps", "rstd", "shift", "minus_half"))
        c.ident = sb("ident", [P, P])
        cols = [LAYOUT[n].cols for n in order] + [0]
        size = max(cols[k] + cols[k + 1] + SPARE.get(order[k], 0) for k in range(len(order)))
        arena = sb("constants", [P, size])
        c.block = {n: arena[:, 0:cols[k]] if k % 2 == 0 else arena[:, size - cols[k]:size] for k, n in enumerate(order)}
        c.spare = {}
        for k, n in enumerate(order):
            if n in SPARE:
                low = cols[k] if k % 2 == 0 else cols[k + 1]
                c.spare[n] = arena[:, low:low + SPARE[n]]
        c.bank = [ctx.enter_context(nc.psum_tensor(f"bank{i}", [P, 512], F32)) for i in range(8)]
        c.dma_sem = {(name, n, i): c.sem(f"{name}_{n}{i}") for name in MOE for n in ("gathered", "scattered") for i in range(2)}
        c.w_ready = {n: c.sem("w_ready_" + n) for n in order}
        x_in, zeroed, ident_ready, xs_ready, stats, x_out = (
            c.sem(n) for n in ("x_in", "zeroed", "ident_ready", "xs_ready", "stats", "x_out"))
        x_tiles = dram["x"].rearrange("(t p) d -> p t d", p=P)
        out_tiles = dram["out"].rearrange("(t p) d -> p t d", p=P)

        c.h_rows = nc.dram_tensor("h_rows", (TOKENS, D), F32, kind="Internal").ap()
        slots = max(m.tiles for m in MOE.values()) * P
        c.y_rows = nc.dram_tensor("y_rows", (2 * TOKENS + slots, D), F32, kind="Internal").ap()
        c.h_turns = c.h_rows.rearrange("(t k p) d -> t p k d", p=P, k=TT)
        c.y_turns = c.y_rows[0:2 * TOKENS].rearrange("(t k p) d -> t p k d", p=P, k=TT)

        with nc.Block() as block:
            @block.sync
            def _(sp):
                for k in range(4):
                    sp.dma_start(c.X[:, 16 * k:16 * k + 16, :], x_tiles[:, 16 * k:16 * k + 16, :]).then_inc(x_in, 16)
                    sp.wait_ge(x_in, 16 * k + 16)

            @block.gpsimd
            def _(g):
                g.memset(c.minus_half[:], -0.5)
                g.memset(c.tick[:], 0.0)
                g.memset(c.ident[:], 0.0).then_inc(zeroed, 1)
                g.wait_ge(zeroed, 1)
                g.affine_select(out=c.ident[:], in_=c.ident[:], compare_op=ALU.not_equal, fill=1.0, base=0,
                                pattern=[[-1, P]], channel_multiplier=1).then_inc(ident_ready, 1)

            @block.vector
            def _(v):
                for k in range(4):
                    v.wait_ge(x_in, 16 * k + 16)
                    with v.Fori(4 * k, 4 * k + 4) as t:
                        then(v, v.tensor_scalar(c.xs[:], c.X[:, ds(t * TT, TT), :], 1.0, None, ALU.mult),
                             xs_ready, t + 1)
                        finish_rows(v, c, stats, t)

        for k, name in enumerate(order):
            if name == "att3":
                c.X1 = sb("X1", [P, TILES, D])
            c.src = c.X1 if name == "ffn3" else c.X
            with ExitStack() as phase:
                used = []

                def sem(n):
                    used.append(phase.enter_context(nc.semaphore(n)))
                    return used[-1]
                c.sem = sem
                begin_phase(nc, c, name, order[k + 1] if k + 1 < len(order) else None)
                PHASES[name](nc, c)
                with nc.Block() as block:
                    @block.gpsimd
                    def _(g):
                        for one in used:
                            g.sem_clear(one)

        with nc.Block() as block:
            @block.sync
            def _(sp):
                for k in range(4):
                    sp.dma_start(out_tiles[:, 16 * k:16 * k + 16, :], c.X[:, 16 * k:16 * k + 16, :]).then_inc(x_out, 16)
                sp.wait_ge(x_out, 64)


def rows(a):
    return np.broadcast_to(np.reshape(a, (1, -1)), (P, np.size(a)))


def moe_numbers(m):
    lane = np.arange(P)[:, None]
    return dict(order=rows(m.count - np.arange(m.count)), tile_no=rows(np.arange(m.tiles)), lane_no=rows(np.arange(P)),
                token1=lane + P * np.arange(TILES) + 1, spare1=2 * TOKENS + lane + P * np.arange(m.tiles) + 1)


def layout_arrays(inp):
    g = {k: np.asarray(v) for k, v in inp.items()}
    out = {}

    def of(prefix):
        return {k[len(prefix):]: v for k, v in g.items() if k.startswith(prefix)}
    a = of("L0_gnn_")
    out["gnn0"] = dict(
        conv1=a["conv1_w"][:, :, 0].T, conv2=a["conv2_w"].transpose(1, 2, 0), w_se=a["w_se"].T, b_se=a["b_se"],
        bn=np.stack([a[f"bn{l}_{k}"] for l in (1, 2) for k in "gbmv"], 1), w_msg=a["w_msg"].T, b_msg=rows(a["b_msg"]),
        w_ih=a["w_ih"].reshape(3, D, 2, D).transpose(3, 2, 0, 1), w_hh=a["w_hh"].reshape(3, D, D).transpose(2, 0, 1),
        b_ih=a["b_ih"].reshape(3, D).T, b_hh=a["b_hh"].reshape(3, D).T)
    for name, prefix in (("ffn0", "L0_ffn_"), ("ffn1", "L1_ffn_")):
        a, m = of(prefix), MOE[name]
        first = np.concatenate([a["w1"], a["w2"]], 2) if m.gated else a["w1"]
        second = a["w3"] if m.gated else a["w2"]
        out[name] = dict(gate_w=a["gate_w"], gate_b=rows(a["gate_b"]), w1=first.transpose(1, 0, 2),
                         w3=second.reshape(m.count, m.chunks, P, D).transpose(2, 0, 1, 3), **moe_numbers(m))
    out["ffn1"].update(b1=rows(a["b1"]), b2=rows(a["b2"]))
    a = of("L1_gnn_")
    out["gnn1"] = dict(theta=a["theta"], w_t=a["W_t"], w_h=a["W_h"], b_t=rows(a["b_t"]))
    a = of("L2_gnn_")
    out["gnn2"] = dict(w_rel=a["W_rel"], w_root=a["W_root"], b_rel=rows(a["b_rel"]), gamma=rows(a["ln_gamma"]), beta=rows(a["ln_beta"]))
    a = of("L2_ffn_")
    diagonal = np.zeros((P, P), np.float32)
    for k in range(2):
        diagonal[k * SL:(k + 1) * SL, k * SL:(k + 1) * SL] = a["W_slice"].T

    def chunks(m):
        return m.reshape(KC, P, -1).transpose(1, 0, 2)
    i = np.arange(P)
    same = i[:, None] // SL == i[None, :] // SL
    conv, cb = a["hy_conv_w"], a["hy_conv_b"]
    out["ffn2"] = dict(
        w_fx=a["W_fx"].T, b_fx=rows(a["b_fx"]), w_x=a["W_x"].T, b_x=a["b_x"].reshape(KC, P).T, w_slice=diagonal,
        b_slice=rows(np.tile(a["b_slice"], HEADS2)), temp=rows(a["temperature"]), in_w=chunks(a["hy_in_w"].T),
        conv_x=chunks(conv[:IN2]), convb_x=cb[:IN2].reshape(KC, P).T,
        conv_bc=conv[IN2:].reshape(2, NS2, TAPS2).transpose(1, 0, 2), convb_bc=cb[IN2:].reshape(2, NS2).T,
        dt_bias=rows(np.tile(a["hy_dt_bias"], 2)), a_log=rows(np.tile(a["hy_A_log"], 2)), skip=rows(a["hy_D"]),
        fcd=chunks(a["hy_fcD_w"].T), norm_w=rows(a["hy_norm_w"]), hy_out=chunks(a["hy_out_w"].T),
        out_w=chunks(a["out_w"].T), out_b=rows(a["out_b"]),
        masks=np.stack([same & (i[:, None] < i[None, :]), same & (i[:, None] > i[None, :])], 1).astype(np.float32))
    a = of("L3_gnn_")
    i = np.arange(P)
    head = (i[:, None] // HD_G == np.arange(8)[None, :])
    sel = (i[:, None] == i[None, :] // 32 * 32 + HD_G)
    wo = np.zeros((2, 4, 32, D), np.float32)
    wo[:, :, 0:HD_G] = a["Wo"].T.reshape(2, 4, HD_G, D)
    out["gnn3"] = dict(wq=a["Wq"].T, wk=a["Wk"].T, wv=a["Wv"].T, qmask=head * np.float32(-HD_G ** -0.5),
                       sel=sel.astype(np.float32), wo=wo.reshape(2, P, D).transpose(1, 0, 2), bo=rows(a["bo"]))
    a = of("L3_ffn_")
    d = np.arange(P) % HD_A
    turned = np.arange(P) // HD_A * HD_A + (d + HD_A // 2) % HD_A
    kv = np.arange(P) // HD_A // 2 * HD_A + d
    angle = np.outer(1.0 / 10000.0 ** (np.arange(0, HD_A, 2, dtype=np.float32) / HD_A),
                     np.arange(NODES, dtype=np.float32))[d % (HD_A // 2)]
    q, k_ = np.arange(P)[:, None], np.arange(NODES)[None, :]
    far = np.concatenate([k_[:, :P] > q, k_ > q + P], 1) * np.float32(1e30)
    out["att3"] = dict(
        ln1=a["ln1_w"], wq=a["wq"].T, wq_rot=a["wq"].T[:, turned], wk=a["wk"].T[:, kv], wk_rot=a["wk"].T[:, kv[turned]],
        wv=a["wv"].T[:, kv], cos=np.cos(angle), sin=np.sin(angle) * np.where(d < HD_A // 2, -1, 1)[:, None],
        qmask=(np.arange(P)[:, None] // HD_A == np.arange(4)[None, :]) * np.float32(-HD_A ** -0.5), far=far, wo=a["wo"].T)
    m = MOE["ffn3"]
    second = np.zeros((m.count, 3 * P, D), np.float32)
    second[:, 0:m.hidden] = a["w2"].transpose(0, 2, 1)
    first = np.concatenate([a["w1"], a["w3"]], 1)
    out["ffn3"] = dict(ln2=a["ln2_w"], gate_w=a["router_w"].T, w1=first.transpose(2, 0, 1),
                       w3=second.reshape(m.count, m.chunks, P, D).transpose(2, 0, 1, 3), **moe_numbers(m))
    return {n: LAYOUT[n].pack(out[n]) for n in out}


ORDER = ["gnn0", "ffn0", "gnn1", "ffn1", "gnn2", "ffn2", "gnn3", "att3", "ffn3"]


def kernel(**inputs):
    import concourse.bacc as _bacc
    from concourse.bass_utils import run_bass_kernel_spmd as _run

    adj = np.asarray(inputs["adj"])
    arrays = {"x": np.ascontiguousarray(np.asarray(inputs["x"]).reshape(-1, D)),
              "adj": np.ascontiguousarray(adj.reshape(-1, NODES)),
              "adjT": np.ascontiguousarray(adj.transpose(0, 2, 1).reshape(-1, NODES))}
    arrays.update(layout_arrays(inputs))
    nc = _bacc.Bacc("TRN2", target_bir_lowering=False, num_devices=1)
    dram = {n: nc.dram_tensor("in_" + n, a.shape, F32, kind="ExternalInput").ap() for n, a in arrays.items()}
    dram["out"] = nc.dram_tensor("out", (GRAPHS * NODES, D), F32, kind="ExternalOutput").ap()
    program(nc, dram, ORDER)
    r = _run(nc, [{"in_" + n: a for n, a in arrays.items()}], core_ids=[0])
    return np.reshape(r.results[0]["out"], (GRAPHS, NODES, D))
```
